# Optimizing a Trainium2 kernel written in Bass

```python
import numpy as np
import jax
import jax.numpy as jnp

def _softmax(x, axis=-1):
    return jax.nn.softmax(x, axis=axis)

def _gelu(x):
    return jax.nn.gelu(x, approximate=True)

def _silu(x):
    return jax.nn.silu(x)

def _sigmoid(x):
    return jax.nn.sigmoid(x)

def _layernorm(x, axis=-1, eps=1e-05):
    m = jnp.mean(x, axis=axis, keepdims=True)
    v = jnp.var(x, axis=axis, keepdims=True)
    return (x - m) / jnp.sqrt(v + eps)

def _scatter_add(tgt, idx, src, axis=0):
    return tgt.at[idx].add(src)

def _segment_sum(src, seg, n):
    return jax.ops.segment_sum(src, seg, n)
kernel_name = 'mk_macaron_d1_jaxref_r4_d84acc'

def setup_inputs(seed: int=0):
    np.random.seed(seed)
    _w = jnp.asarray

    def _L0_attn_setup():
        import jax, jax.numpy as jnp
        import numpy as np
        D_MODEL = 512
        D_STATE = 64
        D_CONV = 4
        HEADDIM = 64
        NHEADS = D_MODEL // HEADDIM
        D_IN_PROJ = 2 * D_MODEL + 2 * D_STATE + NHEADS
        CONV_DIM = D_MODEL + 2 * D_STATE
        B = 2
        L = 256

        def _mamba_fwd(u, W_in, conv_w, conv_b, W_out, A_log, D_param, dt_bias):
            Bb, Ll, _ = u.shape
            proj = u @ W_in.T
            z, x, B_toks, C_toks, dt_toks = jnp.split(proj, [D_MODEL, 2 * D_MODEL, 2 * D_MODEL + D_STATE, 2 * D_MODEL + 2 * D_STATE], axis=-1)
            xBC = jnp.concatenate([x, B_toks, C_toks], axis=-1).transpose(0, 2, 1)
            xBC = jax.lax.conv_general_dilated(xBC, conv_w, window_strides=(1,), padding=[(D_CONV - 1, 0)], feature_group_count=CONV_DIM) + conv_b[None, :, None]
            xBC = jax.nn.silu(xBC.transpose(0, 2, 1))
            x, B_toks, C_toks = jnp.split(xBC, [D_MODEL, D_MODEL + D_STATE], axis=-1)
            A = -jnp.exp(A_log)
            dt = jax.nn.softplus(dt_toks + dt_bias)
            dA = jnp.exp(dt * A)
            xh = x.reshape(Bb, Ll, NHEADS, HEADDIM)

            def step(S, inp):
                dA_t, dt_t, B_t, C_t, x_t = inp
                S = S * dA_t[:, :, None, None] + jnp.einsum('bh,bn,bhp->bhpn', dt_t, B_t, x_t)
                y_t = jnp.einsum('bhpn,bn->bhp', S, C_t)
                return (S, y_t)
            S0 = jnp.zeros((Bb, NHEADS, HEADDIM, D_STATE), u.dtype)
            xs = (dA.transpose(1, 0, 2), dt.transpose(1, 0, 2), B_toks.transpose(1, 0, 2), C_toks.transpose(1, 0, 2), xh.transpose(1, 0, 2, 3))
            _, ys = jax.lax.scan(step, S0, xs)
            y = ys.transpose(1, 0, 2, 3) + D_param[None, None, :, None] * xh
            y = y * jax.nn.silu(z.reshape(Bb, Ll, NHEADS, HEADDIM))
            return y.reshape(Bb, Ll, D_MODEL) @ W_out.T
        key = jax.random.key(seed)
        ks = jax.random.split(key, 8)
        u = jax.random.normal(ks[0], (B, L, D_MODEL), jnp.float32)
        W_in = jax.random.normal(ks[1], (D_IN_PROJ, D_MODEL), jnp.float32) * 0.02
        conv_w = jax.random.normal(ks[2], (CONV_DIM, 1, D_CONV), jnp.float32) * 0.2
        conv_b = jnp.zeros((CONV_DIM,), jnp.float32)
        W_out = jax.random.normal(ks[3], (D_MODEL, D_MODEL), jnp.float32) * 0.02
        A_log = jnp.log(jax.random.uniform(ks[4], (NHEADS,), jnp.float32, 1.0, 16.0))
        D_param = jnp.ones((NHEADS,), jnp.float32)
        dt = jnp.exp(jax.random.uniform(ks[5], (NHEADS,), jnp.float32) * (np.float32(np.log(0.1)) - np.float32(np.log(0.001))) + np.float32(np.log(0.001)))
        dt = jnp.clip(dt, 0.0001)
        dt_bias = dt + jnp.log(-jnp.expm1(-dt))
        return dict(u=u, W_in=W_in, conv_w=conv_w, conv_b=conv_b, W_out=W_out, A_log=A_log, D_param=D_param, dt_bias=dt_bias)
    _L0_attn_in = _L0_attn_setup()

    def _L0_ffn_setup():
        import jax, jax.numpy as jnp
        import numpy as np
        D_MODEL = 512
        D_EXPERT = 2048
        EPS = 1e-08

        def ternary_quant(w):
            scale = jnp.mean(jnp.abs(w)) + EPS
            q = jnp.clip(jnp.round(w / scale), -1.0, 1.0) * scale
            return w + jax.lax.stop_gradient(q - w)
        key = jax.random.key(seed)
        k_x, k_up, k_gate, k_down = jax.random.split(key, 4)
        std_in = 1.0 / np.sqrt(D_MODEL)
        std_exp = 1.0 / np.sqrt(D_EXPERT)
        return {'x': jax.random.normal(k_x, (4, 512, D_MODEL), dtype=jnp.float32), 'W_up': jax.random.normal(k_up, (D_EXPERT, D_MODEL), dtype=jnp.float32) * std_in, 'W_gate': jax.random.normal(k_gate, (D_EXPERT, D_MODEL), dtype=jnp.float32) * std_in, 'W_down': jax.random.normal(k_down, (D_MODEL, D_EXPERT), dtype=jnp.float32) * std_exp}
    _L0_ffn_in = _L0_ffn_setup()
    _d = {'L0_attn_u': _L0_attn_in['u'], 'L0_attn_W_in': _L0_attn_in['W_in'], 'L0_attn_conv_w': _L0_attn_in['conv_w'], 'L0_attn_conv_b': _L0_attn_in['conv_b'], 'L0_attn_W_out': _L0_attn_in['W_out'], 'L0_attn_A_log': _L0_attn_in['A_log'], 'L0_attn_D_param': _L0_attn_in['D_param'], 'L0_attn_dt_bias': _L0_attn_in['dt_bias'], 'L0_ffn_W_up': _L0_ffn_in['W_up'], 'L0_ffn_W_gate': _L0_ffn_in['W_gate'], 'L0_ffn_W_down': _L0_ffn_in['W_down']}
    _x0 = _d['L0_attn_u']
    _d['L0_attn_u'] = jax.random.normal(jax.random.fold_in(jax.random.key(seed), 1), (2, 2048, 512), dtype=_x0.dtype)
    del _x0
    return _d

def reference(L0_attn_u, L0_attn_W_in, L0_attn_conv_w, L0_attn_conv_b, L0_attn_W_out, L0_attn_A_log, L0_attn_D_param, L0_attn_dt_bias, L0_ffn_W_up, L0_ffn_W_gate, L0_ffn_W_down):

    def _L0_attn_ref(u, W_in, conv_w, conv_b, W_out, A_log, D_param, dt_bias):
        import jax, jax.numpy as jnp
        import numpy as np
        D_MODEL = 512
        D_STATE = 64
        D_CONV = 4
        HEADDIM = 64
        NHEADS = D_MODEL // HEADDIM
        D_IN_PROJ = 2 * D_MODEL + 2 * D_STATE + NHEADS
        CONV_DIM = D_MODEL + 2 * D_STATE
        B = 2
        L = 256

        def _mamba_fwd(u, W_in, conv_w, conv_b, W_out, A_log, D_param, dt_bias):
            Bb, Ll, _ = u.shape
            proj = u @ W_in.T
            z, x, B_toks, C_toks, dt_toks = jnp.split(proj, [D_MODEL, 2 * D_MODEL, 2 * D_MODEL + D_STATE, 2 * D_MODEL + 2 * D_STATE], axis=-1)
            xBC = jnp.concatenate([x, B_toks, C_toks], axis=-1).transpose(0, 2, 1)
            xBC = jax.lax.conv_general_dilated(xBC, conv_w, window_strides=(1,), padding=[(D_CONV - 1, 0)], feature_group_count=CONV_DIM) + conv_b[None, :, None]
            xBC = jax.nn.silu(xBC.transpose(0, 2, 1))
            x, B_toks, C_toks = jnp.split(xBC, [D_MODEL, D_MODEL + D_STATE], axis=-1)
            A = -jnp.exp(A_log)
            dt = jax.nn.softplus(dt_toks + dt_bias)
            dA = jnp.exp(dt * A)
            xh = x.reshape(Bb, Ll, NHEADS, HEADDIM)

            def step(S, inp):
                dA_t, dt_t, B_t, C_t, x_t = inp
                S = S * dA_t[:, :, None, None] + jnp.einsum('bh,bn,bhp->bhpn', dt_t, B_t, x_t)
                y_t = jnp.einsum('bhpn,bn->bhp', S, C_t)
                return (S, y_t)
            S0 = jnp.zeros((Bb, NHEADS, HEADDIM, D_STATE), u.dtype)
            xs = (dA.transpose(1, 0, 2), dt.transpose(1, 0, 2), B_toks.transpose(1, 0, 2), C_toks.transpose(1, 0, 2), xh.transpose(1, 0, 2, 3))
            _, ys = jax.lax.scan(step, S0, xs)
            y = ys.transpose(1, 0, 2, 3) + D_param[None, None, :, None] * xh
            y = y * jax.nn.silu(z.reshape(Bb, Ll, NHEADS, HEADDIM))
            return y.reshape(Bb, Ll, D_MODEL) @ W_out.T
        return _mamba_fwd(u, W_in, conv_w, conv_b, W_out, A_log, D_param, dt_bias)

    def _L0_ffn_ref(x, W_up, W_gate, W_down):
        import jax, jax.numpy as jnp
        import numpy as np
        D_MODEL = 512
        D_EXPERT = 2048
        EPS = 1e-08

        def ternary_quant(w):
            scale = jnp.mean(jnp.abs(w)) + EPS
            q = jnp.clip(jnp.round(w / scale), -1.0, 1.0) * scale
            return w + jax.lax.stop_gradient(q - w)
        wu = ternary_quant(W_up)
        wg = ternary_quant(W_gate)
        wd = ternary_quant(W_down)
        up = jnp.einsum('bsd,ed->bse', x, wu)
        gate = jnp.einsum('bsd,ed->bse', x, wg)
        hidden = jax.nn.silu(up) * gate
        return jnp.einsum('bse,de->bsd', hidden, wd)
    x = L0_attn_u
    x = x + 0.5 * _L0_ffn_ref(_layernorm(x, axis=-1), L0_ffn_W_up, L0_ffn_W_gate, L0_ffn_W_down)
    x = x + _L0_attn_ref(_layernorm(x, axis=-1), L0_attn_W_in, L0_attn_conv_w, L0_attn_conv_b, L0_attn_W_out, L0_attn_A_log, L0_attn_D_param, L0_attn_dt_bias)
    x = x + 0.5 * _L0_ffn_ref(_layernorm(x, axis=-1), L0_ffn_W_up, L0_ffn_W_gate, L0_ffn_W_down)
    return x

_drawn_inputs = setup_inputs


def setup_inputs(seed=0):
    import zlib

    import numpy as np

    out = dict(_drawn_inputs(seed))
    spreads = {'L0_attn_conv_b': (0.0, 0.8), 'L0_attn_D_param': (1.0, 0.6)}
    factors = {'L0_attn_W_in': 3.683,
     'L0_attn_conv_w': 3.815,
     'L0_attn_W_out': 3.333,
     'L0_attn_A_log': 8.0,
     'L0_attn_dt_bias': 8.0}
    for name, (base, spread) in spreads.items():
        noise = np.random.default_rng([zlib.crc32(name.encode()), seed]).standard_normal(out[name].shape)
        drawn = base * np.exp(spread * noise) if base else spread * noise
        out[name] = jnp.asarray(drawn.astype(out[name].dtype))
    for name, factor in factors.items():
        out[name] = (out[name] * factor).astype(out[name].dtype)
    return out
```

```python
from contextlib import ExitStack

import concourse.bass as bass
from concourse import mybir

F32 = mybir.dt.float32
F16 = mybir.dt.float16
F8 = mybir.dt.float8e4
ALU = mybir.AluOpType
ACT = mybir.ActivationFunctionType
AX = mybir.AxisListType

P = 128
B, L, D, E = 2, 2048, 512, 2048
H, N, HD = 8, 64, 64
KD, KE = D // P, E // P
TG = 512
CH = TG // P
NG = B * L // TG
GB = NG // B
NCONV = (D + 2 * N) // P
TAPS = 4
W_IN = 2 * D + 2 * N + H
LN_EPS, Q_EPS = 1e-5, 1e-8
XS = 2.0 ** 11
HS = 2.0 ** -3
AS = 2.0 ** 7
A_MIN = -200.0


def macaron_kernel(nc, u, w_up, w_gate, w_down, w_in, w_out, conv_w, conv_b, head_par, out):
    top = ExitStack()

    def sb(ctx, name, shape, dt=F32):
        return ctx.enter_context(nc.sbuf_tensor(name, shape, dt))

    def ps(ctx, name, shape, dt=F32):
        return ctx.enter_context(nc.psum_tensor(name, shape, dt))

    def sem(ctx, name):
        return ctx.enter_context(nc.semaphore(name))

    def sems(ctx, name, n):
        return [sem(ctx, f"{name}{i}") for i in range(n)]

    with top:
        x = sb(top, "x", [P, NG * CH * D])
        wu = sb(top, "wu", [P, KD, E], F16)
        wg = sb(top, "wg", [P, KD, E], F8)
        wd = sb(top, "wd", [P, KE, D], F16)
        xn = sb(top, "xn", [P, CH, D])
        ident = sb(top, "ident", [P, P])
        neg_half = sb(top, "neg_half", [P, CH])
        silu_scale = sb(top, "silu_scale", [P, 1])
        hid_scale = sb(top, "hid_scale", [P, 1])
        tern_done = sem(top, "tern_done")
        out_scale = sb(top, "out_scale", [P, 1])

        late = sb(top, "late", [P, KD * E])
        late_in = sem(top, "late_in")
        bounds = [0]
        for n in (KD * W_IN, KD * D, NCONV * TAPS, NCONV, 3 * H, D, D, N, P, P, P // 2):
            bounds.append(bounds[-1] + n)
        parts = [late[:, a:b] for a, b in zip(bounds, bounds[1:])]
        win = parts[0].rearrange("p (k n) -> p k n", k=KD)
        wout = parts[1].rearrange("p (k n) -> p k n", k=KD)
        cvw = parts[2].rearrange("p (k n) -> p k n", k=NCONV)
        cvb = parts[3]
        head_alog, head_d, head_bias = (parts[4][:, i * H:(i + 1) * H] for i in range(3))
        state = [parts[5][0:N, :], parts[6][0:N, :]]
        late_loads = [(parts[0], w_in), (parts[1], w_out), (parts[2], conv_w), (parts[3], conv_b), (parts[4], head_par)]
        N_LATE = len(late_loads)

        def after(n):
            return n + 1

        def start_counts(eng, counting, head_start=()):
            for s in counting:
                eng.sem_inc(s, 1)
            for s, n in head_start:
                eng.sem_inc(s, n)

        def xt(t):
            return x[:, bass.ds(t * D, D)]

        def ffn_part(tag, first):
            ctx = ExitStack()
            with ctx:
                xhi = sb(ctx, tag + "xhi", [P, KD, TG], F16)
                xlo = sb(ctx, tag + "xlo", [P, KD, TG], F16)
                sil = sb(ctx, tag + "sil", [P, 2, TG])
                hid = sb(ctx, tag + "hid", [P, 2, TG])
                hhi = sb(ctx, tag + "hhi", [P, KE, TG], F16)
                hlo = sb(ctx, tag + "hlo", [P, KE, TG], F16)
                stat = sb(ctx, tag + "stat", [P, CH, 6])
                mv = sb(ctx, tag + "mv", [P, CH, 2])
                var = sb(ctx, tag + "var", [P, CH])
                rstd = sb(ctx, tag + "rstd", [P, CH])
                up_ps = [ps(ctx, f"{tag}up_ps{i}", [P, TG]) for i in range(2)]
                gate_ps = [ps(ctx, f"{tag}gate_ps{i}", [P, TG]) for i in range(2)]
                down_ps = [ps(ctx, f"{tag}down_ps{i}", [P, D]) for i in range(2)]
                tr_ps = [ps(ctx, f"{tag}tr_ps{i}", [P, TG]) for i in range(2)]

                stat_done = sem(ctx, tag + "stat_done")
                mv_done = sem(ctx, tag + "mv_done")
                var_done = sem(ctx, tag + "var_done")
                rstd_done = sem(ctx, tag + "rstd_done")
                xn_done = sem(ctx, tag + "xn_done")
                tr_done = sem(ctx, tag + "tr_done")
                xhi_done = sem(ctx, tag + "xhi_done")
                xlo_done = sems(ctx, tag + "xlo_done", 2)
                ug_done = sem(ctx, tag + "ug_done")
                sil_done = sem(ctx, tag + "sil_done")
                hid_done = sems(ctx, tag + "hid_done", 2)
                hhi_done = sem(ctx, tag + "hhi_done")
                hlo_done = sems(ctx, tag + "hlo_done", 2)
                down_done = sem(ctx, tag + "down_done")
                res_done = sems(ctx, tag + "res_done", 2)
                if first:
                    ones = sb(ctx, "ones", [P, P])
                    raw_u = x[:, 16 * D:32 * D]
                    raw_d = [hlo[:, KE // 2:, :].rearrange("p e t -> p (e t)").bitcast(F32),
                             x[:, 8 * D:12 * D], x[:, 12 * D:16 * D],
                             xn[:, :, :].rearrange("p c d -> p (c d)")]
                    raw_g = late[:, :]
                    mask = sb(ctx, "mask", [P, 2, 2048], F16)
                    wsum = sb(ctx, "wsum", [P, 3, 4])
                    total = sb(ctx, "total", [P, 3])
                    scale = sb(ctx, "scale", [P, 3])
                    half = sb(ctx, "half", [P, 3])
                    nhalf = sb(ctx, "nhalf", [P, 3])
                    rscale = sb(ctx, "rscale", [P, 1])
                    prod = sb(ctx, "prod", [P, 2])
                    const_done = sem(ctx, "const_done")
                    raw_in = sems(ctx, "raw_in", 12)
                    x_in = sem(ctx, "x_in")
                    abs_done = sem(ctx, "abs_done")
                    sum_done = sem(ctx, "sum_done")
                    sc_done = sem(ctx, "sc_done")
                    mask_done = sem(ctx, "mask_done")
                else:
                    x_out = sem(ctx, "x_out")

                u_v = u.rearrange("(t p) d -> p t d", p=P)
                out_v = out.rearrange("(t p) d -> p t d", p=P)
                x_v = x[:, :].rearrange("p (t d) -> p t d", d=D)
                raws = [(w_up, 0), (w_gate, 1), (w_down, 2)]

                TERNARY = ([(0, 0, 0, 512), (0, 1, 0, 512), (1, 0, 0, P), (1, 0, P, 512), (1, 1, 0, 512)]
                           + [(0, 2, 0, 512), (1, 2, 0, 512), (0, 3, 0, 512), (1, 3, 0, 512)]
                           + [(2, q, 0, 512) for q in range(4)])
                N_TERN, T_EARLY = len(TERNARY), 5
                T_BETWEEN = (0, 1, 2, 3, 5, 7, 8, 10)

                def raw_q(w, q):
                    if w == 2:
                        return raw_d[q]
                    return (raw_u, raw_g)[w][:, q * 2048:(q + 1) * 2048]

                with nc.Block() as block:

                    @block.sync
                    def _(sp):
                        start_counts(sp, [stat_done, mv_done, var_done, rstd_done, xn_done, tr_done, xhi_done, *xlo_done,
                                          ug_done, sil_done, *hid_done, hhi_done, *hlo_done, down_done, *res_done],
                                     () if first else ((stat_done, CH), (mv_done, 1), (var_done, 1), (rstd_done, 1), (xn_done, 1)))
                        if first:
                            def load_x(g):
                                sp.dma_start(x_v[:, CH * g:CH * g + CH, :],
                                             u_v[:, CH * g:CH * g + CH, :]).then_inc(x_in, 16)

                            load_x(0)
                            for w in (0, 1, 2):
                                for q in range(4):
                                    if (w, q) == (2, 3):
                                        sp.wait_ge(tr_done, after(KD))
                                    sp.dma_start(raw_q(w, q), raws[w][0][:, q * 2048:(q + 1) * 2048])\
                                      .then_inc(raw_in[4 * w + q], 16)
                            for g in range(1, NG):
                                sp.wait_ge(x_in, 16 * g)
                                if g == 2:
                                    sp.wait_ge(tern_done, N_TERN)
                                    for dst, src in late_loads:
                                        sp.dma_start(dst, src[:, :]).then_inc(late_in, 16)
                                load_x(g)
                            sp.wait_ge(x_in, 16 * NG)
                        else:
                            with sp.Fori(0, NG) as g:
                                for c in (2, 3):
                                    sp.wait_ge(res_done[c % 2], after(2 * g + 2))
                                sp.dma_start(out_v[:, bass.ds(CH * g, CH), :],
                                             x_v[:, bass.ds(CH * g, CH), :]).then_inc(x_out, 16)
                            sp.wait_ge(x_out, 16 * NG)

                    @block.gpsimd
                    def _(pool):
                        if first:
                            nc.gpsimd.memset(ones[:, :], 1.0).then_inc(const_done, 1)
                            nc.gpsimd.memset(neg_half[:, :], -0.5).then_inc(const_done, 1)
                            pool.wait_ge(const_done, 1)
                            nc.gpsimd.affine_select(out=ident[:, :], in_=ones[:, :], compare_op=ALU.is_equal, fill=0.0,
                                                    base=0, pattern=[[-1, P]], channel_multiplier=1)\
                              .then_inc(const_done, 1)
                            pool.wait_ge(const_done, 3)

                        def inv_std(g):
                            pool.wait_ge(var_done, after(g + 1))
                            nc.gpsimd.tensor_tensor(rstd[:, :], var[:, :], neg_half[:, :], ALU.pow)\
                              .then_inc(rstd_done, 1)

                        def low_parts(g, e):
                            pool.wait_ge(hhi_done, after(KE * g + e + 1))
                            nc.gpsimd.tensor_tensor(hlo[:, e, :], hid[:, e % 2, :], hhi[:, e, :], ALU.subtract)\
                              .then_inc(hlo_done[e % 2], 1)

                        def group(g, more_ln):
                            for e in range(KE):
                                if first and e == KE // 2:
                                    pool.wait_ge(tern_done, 1 + TERNARY.index((2, 0, 0, D)))
                                low_parts(g, e)
                                if e == 9 and more_ln:
                                    inv_std(g + 1)

                        if first:
                            inv_std(0)
                        with pool.Fori(0, NG - 1) as g:
                            group(g, True)
                        group(NG - 1, first)

                    @block.scalar
                    def _(act):
                        def abs_sum(w, q):
                            blocks = 4 * q if w < 2 else KE - 4
                            act.wait_ge(raw_in[4 * w + q], 16)
                            if w:
                                act.wait_ge(abs_done, 4 * (w - 1) + q + 1 if w < 2 else 4 * w + q)
                            nc.scalar.activation(hhi[:, blocks:blocks + 4, :], raw_q(w, q), ACT.Abs,
                                                 accum_out=wsum[:, w, q:q + 1]).then_inc(abs_done, 1)

                        def high_parts(act, g, k):
                            act.wait_ge(tr_done, after(KD * g + k + 1))
                            nc.scalar.activation(xhi[:, k, :], tr_ps[k % 2][:, :], ACT.Copy, scale=XS)\
                              .then_inc(xhi_done, 1)

                        if first:
                            for w in range(2):
                                for q in range(4):
                                    if w == 0 and q == 2:
                                        for k in range(KD):
                                            high_parts(act, 0, k)
                                    abs_sum(w, q)
                        else:
                            for k in range(KD):
                                high_parts(act, 0, k)

                        def silu(g, e):
                            n = KE * g + e
                            act.wait_ge(ug_done, after(n + 1))
                            act.wait_ge(hid_done[e % 2], after(KE // 2 * g + e // 2))
                            nc.scalar.activation(sil[:, e % 2, :], up_ps[e % 2][:, :], ACT.Silu,
                                                 scale=silu_scale[:, 0:1]).then_inc(sil_done, 1)

                        def hid_high(g, e):
                            act.wait_ge(hid_done[e % 2], after(KE // 2 * g + e // 2 + 1))
                            nc.scalar.activation(hhi[:, e, :], hid[:, e % 2, :], ACT.Copy).then_inc(hhi_done, 1)

                        def group(g, more, between=None):
                            for e in range(KE):
                                silu(g, e)
                                if between is not None:
                                    between(e)
                                if first and e == KE - 3:
                                    act.wait_ge(abs_done, 12)
                                if e:
                                    hid_high(g, e - 1)
                            hid_high(g, KE - 1)
                            if more:
                                for k in range(KD):
                                    high_parts(act, g + 1, k)

                        if first:
                            def w_down_sums(e):
                                if e in (0, 1):
                                    abs_sum(2, 2 * e)
                                    abs_sum(2, 2 * e + 1)

                            group(0, True, w_down_sums)
                        with act.Fori(1 if first else 0, NG - 1) as g:
                            group(g, True)
                        group(NG - 1, False)

                    @block.vector
                    def _(dve):
                        def tile(g, c):
                            return CH * (0 if isinstance(g, int) and g == NG else g) + c

                        def stats(g, c):
                            nc.vector.bn_stats(stat[:, c, :], xt(tile(g, c))).then_inc(stat_done, 1)

                        def variance(g):
                            for c in range(CH):
                                last = nc.vector.bn_aggr(mv[:, c, :], stat[:, c, :])
                            last.then_inc(mv_done, 1)
                            dve.wait_ge(mv_done, after(g + 1))
                            nc.vector.tensor_scalar(var[:, :], mv[:, :, 1], LN_EPS, None, ALU.add)\
                              .then_inc(var_done, 1)

                        def normalize(g, c0, c1):
                            dve.wait_ge(rstd_done, after(g + 1))
                            if c0 == 0:
                                dve.wait_ge(tr_done, after(KD * g))
                                if first and not (isinstance(g, int) and g == 0):
                                    dve.wait_ge(tern_done, N_TERN)
                            for c in range(c0, c1):
                                last = nc.vector.tensor_scalar(xn[:, c, :], xt(tile(g, c)), mv[:, c, 0:1],
                                                               rstd[:, c:c + 1], ALU.subtract, ALU.mult)
                            if c1 == CH:
                                last.then_inc(xn_done, 1)

                        def low_part(g, k):
                            dve.wait_ge(xhi_done, after(KD * g + k + 1))
                            nc.vector.scalar_tensor_tensor(xlo[:, k, :], tr_ps[k % 2][:, :], XS, xhi[:, k, :],
                                                           ALU.mult, ALU.subtract).then_inc(xlo_done[k % 2], 1)

                        def hidden(g, e, stats_of=None):
                            if stats_of is not None:
                                dve.wait_ge(stat_done, after(CH * stats_of + CH))
                            dve.wait_ge(sil_done, after(KE * g + e + 1))
                            dve.wait_ge(hlo_done[e % 2], after(KE // 2 * g + e // 2))
                            nc.vector.scalar_tensor_tensor(hid[:, e % 2, :], sil[:, e % 2, :], hid_scale[:, 0:1],
                                                           gate_ps[e % 2][:, :], ALU.mult, ALU.mult)\
                              .then_inc(hid_done[e % 2], 1)

                        def residual(g, c):
                            dve.wait_ge(down_done, after(CH * g + c + 1))
                            nc.vector.scalar_tensor_tensor(xt(CH * g + c), down_ps[c % 2][:, :], out_scale[:, 0:1],
                                                           xt(CH * g + c), ALU.mult, ALU.add)\
                              .then_inc(res_done[c % 2], 1)

                        def group(g, more, between=None):
                            more_ln = more or first
                            for e in range(KE):
                                hidden(g, e, g + 1 if more_ln and e == 8 else None)
                                if between is not None:
                                    between(e)
                                if more_ln:
                                    if e == 4 and first and more:
                                        dve.wait_ge(x_in, 16 * g + 32)
                                    if e in (4, 6):
                                        stats(g + 1, e - 4)
                                        stats(g + 1, e - 3)
                                    if e == 8:
                                        variance(g + 1)
                                    if e == 11:
                                        normalize(g + 1, 0, 2)
                                    if e == 13:
                                        normalize(g + 1, 2, 4)
                            residual(g, 0)
                            if more:
                                low_part(g + 1, 0)
                                low_part(g + 1, 1)
                            residual(g, 1)
                            if more:
                                low_part(g + 1, 2)
                                low_part(g + 1, 3)
                            residual(g, 2)
                            residual(g, 3)

                        if first:
                            dve.wait_ge(x_in, 16)
                            for c in range(CH):
                                stats(0, c)
                            dve.wait_ge(stat_done, after(CH))
                            variance(0)
                            normalize(0, 0, 4)

                        steps = [0]

                        def step(ins):
                            steps[0] += 1
                            ins.then_inc(sc_done, 1)
                            dve.wait_ge(sc_done, steps[0])

                        def weight_scale(w):
                            dve.wait_ge(sum_done, w + 1)
                            step(nc.vector.tensor_reduce(total[:, w:w + 1], down_ps[w % 2][:, 0:4], AX.X, ALU.add))
                            step(nc.vector.tensor_scalar(scale[:, w:w + 1], total[:, w:w + 1], 1.0 / (D * E), Q_EPS,
                                                         ALU.mult, ALU.add))
                            step(nc.vector.tensor_scalar(half[:, w:w + 1], scale[:, w:w + 1], 0.5, None, ALU.mult))
                            step(nc.vector.tensor_scalar(nhalf[:, w:w + 1], scale[:, w:w + 1], -0.5, None, ALU.mult))

                        def ternary(n):
                            w, q, e0, e1 = TERNARY[n]
                            dst = (wu, wg)[w][:, :, q * 512 + e0:q * 512 + e1] if w < 2 else wd[:, 4 * q:4 * q + 4, :]
                            src = raw_q(w, q).rearrange("p (k e) -> p k e", k=4)[:, :, e0:e1]
                            m = mask[:, n % 2, :].rearrange("p (k e) -> p k e", k=4)[:, :, e0:e1]
                            nc.vector.tensor_scalar(m, src, nhalf[:, w:w + 1], None, ALU.is_lt).then_inc(mask_done, 1)
                            dve.wait_ge(mask_done, n + 1)
                            nc.vector.scalar_tensor_tensor(dst, src, half[:, w:w + 1], m, ALU.is_gt, ALU.subtract,
                                                           saturate=False)\
                              .then_inc(tern_done, 1)

                        def last_weights(e):
                            if e == 4:
                                weight_scale(2)
                                step(nc.vector.tensor_tensor(prod[:, 0:1], scale[:, 0:1], scale[:, 1:2], ALU.mult))
                                step(nc.vector.tensor_tensor(prod[:, 1:2], prod[:, 0:1], scale[:, 2:3], ALU.mult))
                                step(nc.vector.tensor_scalar(out_scale[:, :], prod[:, 1:2], 0.5 / HS, None, ALU.mult))
                            if e in T_BETWEEN:
                                ternary(T_EARLY + T_BETWEEN.index(e))

                        for k in range(KD):
                            low_part(0, k)
                        if first:
                            weight_scale(0)
                            step(nc.vector.tensor_scalar(silu_scale[:, :], scale[:, 0:1], 1.0 / XS, None, ALU.mult))
                            step(nc.vector.reciprocal(rscale[:, :], scale[:, 0:1]))
                            step(nc.vector.tensor_scalar(hid_scale[:, :], rscale[:, :], HS / XS, None, ALU.mult))
                            for n in range(T_EARLY):
                                if n == 2:
                                    weight_scale(1)
                                ternary(n)
                            group(0, True, last_weights)
                        with dve.Fori(1 if first else 0, NG - 1) as g:
                            group(g, True)
                        group(NG - 1, False)

                    @block.tensor
                    def _(pe):
                        def transposes(g, k):
                            if k == 0:
                                pe.wait_ge(xn_done, after(g + 1))
                            pe.wait_ge(xlo_done[k % 2], after(2 * g + k // 2))
                            for c in range(CH):
                                last = nc.tensor.transpose(tr_ps[k % 2][:, c * P:(c + 1) * P],
                                                           xn[:, c, k * P:(k + 1) * P], ident[:, :])
                            last.then_inc(tr_done, 1)

                        def up_gate(g, e):
                            if e == 0:
                                pe.wait_ge(xlo_done[0], after(2 * g + 2))
                                pe.wait_ge(xlo_done[1], after(2 * g + 2))
                            if first:
                                pe.wait_ge(tern_done, 1 + max(n for n, (w, q, e0, e1) in enumerate(TERNARY)
                                                              if w < 2 and q == e // 4 and e0 <= e % 4 * P < e1))
                            pe.wait_ge(hid_done[e % 2], after(KE // 2 * g + e // 2))
                            for w, acc in ((wu, up_ps[e % 2]), (wg, gate_ps[e % 2])):
                                for k in range(KD):
                                    for part in (xhi, xlo):
                                        last = nc.tensor.matmul(acc[:, :], w[:, k, e * P:(e + 1) * P], part[:, k, :],
                                                                start=(k == 0 and part is xhi),
                                                                stop=(k == KD - 1 and part is xlo))
                            last.then_inc(ug_done, 1)

                        def down(g, c):
                            for e in range(KE):
                                if first and c == 0 and e % 4 == 0:
                                    pe.wait_ge(tern_done, 1 + TERNARY.index((2, e // 4, 0, D)))
                                if e == 0:
                                    pe.wait_ge(res_done[c % 2], after(2 * g + c // 2))
                                if c == 0:
                                    pe.wait_ge(hlo_done[e % 2], after(KE // 2 * g + e // 2 + 1))
                                for part in (hhi, hlo):
                                    last = nc.tensor.matmul(down_ps[c % 2][:, :], part[:, e, c * P:(c + 1) * P],
                                                            wd[:, e, :], start=(e == 0 and part is hhi),
                                                            stop=(e == KE - 1 and part is hlo))
                            last.then_inc(down_done, 1)

                        def group(g, more, between=None):
                            for e in range(KE):
                                up_gate(g, e)
                                if between is not None:
                                    between(e)
                            down(g, 0)
                            if more:
                                transposes(g + 1, 0)
                                transposes(g + 1, 1)
                            down(g, 1)
                            if more:
                                transposes(g + 1, 2)
                                transposes(g + 1, 3)
                            down(g, 2)
                            down(g, 3)

                        if first:
                            pe.wait_ge(const_done, 3)
                        for k in range(KD):
                            transposes(0, k)
                        if first:
                            def weight_sum(w):
                                pe.wait_ge(abs_done, 4 * w + 4)
                                if w == 2:
                                    pe.wait_ge(sc_done, 1)
                                nc.tensor.matmul(down_ps[w % 2][:, 0:4], ones[:, :], wsum[:, w, :],
                                                 start=True, stop=True).then_inc(sum_done, 1)

                            def last_sum(e):
                                if e == 3:
                                    weight_sum(2)

                            weight_sum(0)
                            weight_sum(1)
                            group(0, True, last_sum)
                        with pe.Fori(1 if first else 0, NG - 1) as g:
                            group(g, True)
                        group(NG - 1, False)

        def ssm_part():
            ctx = ExitStack()
            with ctx:
                xnt = sb(ctx, "s_xnt", [P, KD, TG])
                xpad = sb(ctx, "s_xpad", [P, TAPS - 1 + TG])
                hist = sb(ctx, "s_hist", [P, B, NCONV, TAPS - 1])
                xc = sb(ctx, "s_xc", [P, B, NCONV, TG])
                cc = sb(ctx, "s_cc", [N, B, TG])
                zs = sb(ctx, "s_zs", [P, CH, D])
                dtv = sb(ctx, "s_dtv", [P, CH * H])
                sp_t = sb(ctx, "s_sp", [P, 7, CH * H])
                dt = sb(ctx, "s_dt", [P, B, CH, H])
                a32 = sp_t[:, 6, :]
                al = sb(ctx, "s_al", [P, B, 2, CH, H], F16)
                dec = sb(ctx, "s_dec", [P, B, 3, CH, H])
                am = sb(ctx, "s_am", [P, 2, H, P], F16)
                lx = sb(ctx, "s_lx", [P, H, P])
                btok = parts[7]
                gm = parts[8]
                xtok = sb(ctx, "s_xtok", [P, D])
                dtx = sb(ctx, "s_dtx", [P, D])
                dx = sb(ctx, "s_dx", [P, D])
                yv = sb(ctx, "s_yv", [P, D])
                yt = sb(ctx, "s_yt", [P, KD, P])
                stat = sb(ctx, "s_stat", [P, CH, 6])
                mv = sb(ctx, "s_mv", [P, CH, 2])
                var = sb(ctx, "s_var", [P, CH])
                rstd = sb(ctx, "s_rstd", [P, CH])
                a_neg = sb(ctx, "s_a_neg", [P, H])
                a_exp = sb(ctx, "s_a_exp", [P, H])
                tri = parts[9]
                tri16 = sb(ctx, "s_tri16", [P, P], F16)
                after16 = sb(ctx, "s_after16", [P, P], F16)
                ones16 = parts[10].bitcast(F16)

                wide = [ps(ctx, f"s_wide{i}", [P, 512]) for i in range(2)]
                seg = ps(ctx, "s_seg", [P, H * P])
                turn = ps(ctx, "s_turn", [P, D])
                bc = ps(ctx, "s_bc", [P, P + N])
                near = ps(ctx, "s_near", [P, D])
                far = ps(ctx, "s_far", [P, D])

                stat_done = sem(ctx, "s_stat_done")
                mv_done = sem(ctx, "s_mv_done")
                var_done = sem(ctx, "s_var_done")
                rstd_done = sem(ctx, "s_rstd_done")
                xn_done = sem(ctx, "s_xn_done")
                wide_free = sems(ctx, "s_wide_free", 2)
                tr_done = sem(ctx, "s_tr_done")
                conv_in = sem(ctx, "s_conv_in")
                dt_in = sem(ctx, "s_dt_in")
                z_in = sem(ctx, "s_z_in")
                dec_in = sem(ctx, "s_dec_in")
                pad_done = sem(ctx, "s_pad_done")
                tap_done = sem(ctx, "s_tap_done")
                xc_done = sem(ctx, "s_xc_done")
                cc_in = sem(ctx, "s_cc_in")
                abs_done = sem(ctx, "s_abs_done")
                exp_done = sem(ctx, "s_exp_done")
                sp_step = sem(ctx, "s_sp_step")
                a_done = sem(ctx, "s_a_done")
                am_done = sem(ctx, "s_am_done")
                seg_done = sem(ctx, "s_seg_done")
                bc_done = sem(ctx, "s_bc_done")
                xt_done = sem(ctx, "s_xt_done")
                y_done = sem(ctx, "s_y_done")
                st_done = sem(ctx, "s_st_done")
                yt_done = sem(ctx, "s_yt_done")
                out_done = sem(ctx, "s_out_done")
                lx_done = sem(ctx, "s_lx_done")
                xtok_done = sem(ctx, "s_xtok_done")
                ytc_done = sem(ctx, "s_ytc_done")
                gm_done = sem(ctx, "s_gm_done")
                btok_done = sem(ctx, "s_btok_done")
                dtx_done = sem(ctx, "s_dtx_done")
                m_done = sem(ctx, "s_m_done")
                y1_done = sem(ctx, "s_y1_done")
                y2_done = sem(ctx, "s_y2_done")
                y3_done = sem(ctx, "s_y3_done")
                y4_done = sem(ctx, "s_y4_done")
                s1_done = sem(ctx, "s_s1_done")
                s2_done = sem(ctx, "s_s2_done")
                res_done = sem(ctx, "s_res_done")
                dx_done = sem(ctx, "s_dx_done")
                dtxe_done = sem(ctx, "s_dtxe_done")
                set_done = sem(ctx, "s_set_done")
                a_exp_done = sem(ctx, "s_a_exp_done")
                a_neg_done = sem(ctx, "s_a_neg_done")

                N_SET = 8
                W_TR, W_BC, W_DT, W_X, W_Z, W_DEC, W_ALL = (0, 1, 2, 3), 4, 5, (6, 8, 10, 13), (7, 9, 11, 14), 12, 15
                CONV = (4, 0, 1, 2, 3)
                W_CONV = (W_BC,) + W_X
                BEHIND = (GB, 0)
                SP_STEPS = 17

                def order(g):
                    return 2 * g[0] + g[1]

                def follower(g):
                    return (g[0], 1) if g[1] == 0 else (g[0] + 1, 0)

                def tile(g, c):
                    return c if g is BEHIND else GB * CH * g[1] + CH * g[0] + c

                def wide_use(g, k):
                    j, b = g
                    return (W_ALL * b + k) % 2, W_ALL * j + (W_ALL * b + k) // 2

                def taken(eng, g, k):
                    bank, before = wide_use(g, k)
                    eng.wait_ge(wide_free[bank], after(before + 1))

                def cols(c):
                    return slice(c * P, (c + 1) * P)

                def heads(ap):
                    return ap.rearrange("p (h n) -> p h n", h=H)

                def over(ap, n):
                    return ap.unsqueeze(2).to_broadcast([ap.shape[0], H, n])

                def all_groups(eng, group):
                    with eng.Fori(0, GB - 1) as j:
                        for b in range(B):
                            group((j, b), follower((j, b)), (j + 1, b))
                    group((GB - 1, 0), (GB - 1, 1), None)
                    group((GB - 1, 1), None, BEHIND)

                with nc.Block() as block:

                    @block.sync
                    def _(sp):
                        start_counts(sp, [stat_done, mv_done, var_done, rstd_done, xn_done, *wide_free, tr_done, conv_in,
                                          dt_in, z_in, dec_in, pad_done, tap_done, xc_done, abs_done, exp_done, sp_step,
                                          a_done, am_done, seg_done, bc_done, xt_done, y_done, st_done, yt_done, out_done,
                                          lx_done, xtok_done, ytc_done, gm_done, btok_done, dtx_done, m_done, y1_done,
                                          y2_done, y3_done, y4_done, s1_done, s2_done, res_done, dx_done, dtxe_done],
                                     ((stat_done, CH), (mv_done, 1), (var_done, 1), (rstd_done, 1), (xn_done, 1)))

                        def move_c(f):
                            n = order(f)
                            sp.wait_ge(xc_done, after(NCONV * n + 1))
                            sp.dma_start(cc[:, f[1], :], xc[N:2 * N, f[1], 4, :]).then_inc(cc_in, 16)

                        move_c((0, 0))

                        def group(g, front, ahead):
                            if front is not None:
                                move_c(front)

                        all_groups(sp, group)
                        sp.wait_ge(cc_in, 16 * NG)

                    @block.gpsimd
                    def _(pool):
                        def mask(out, src, base, step, mult):
                            return nc.gpsimd.affine_select(out=out, in_=src, compare_op=ALU.is_ge, fill=0.0, base=base,
                                                           pattern=[[step, P]], channel_multiplier=mult)

                        nc.gpsimd.memset(ones16[:, :], 1.0).then_inc(set_done, 1)
                        nc.gpsimd.memset(state[0], 0.0).then_inc(set_done, 1)
                        nc.gpsimd.memset(state[1], 0.0).then_inc(set_done, 1)
                        nc.gpsimd.memset(hist[:, :, :, :], 0.0).then_inc(set_done, 1)
                        nc.gpsimd.memset(tri[:, :], 1.0).then_inc(set_done, 1)
                        pool.wait_ge(set_done, 5)
                        mask(tri[:, :], tri[:, :], 0, 1, -1).then_inc(set_done, 1)
                        mask(tri16[:, :], ones16[:, :], 0, 1, -1).then_inc(set_done, 1)
                        mask(after16[:, :], ones16[:, :], -1, -1, 1).then_inc(set_done, 1)
                        pool.wait_ge(set_done, N_SET)

                        def inv_std(f):
                            pool.wait_ge(var_done, after(order(f) + 1))
                            nc.gpsimd.tensor_tensor(rstd[:, :], var[:, :], neg_half[:, :], ALU.pow).then_inc(rstd_done, 1)

                        def masked(g, c):
                            q = CH * order(g) + c
                            if c == 0:
                                pool.wait_ge(a_done, after(order(g) + 1))
                            pool.wait_ge(seg_done, after(q))
                            nc.gpsimd.tensor_tensor(
                                am[:, :, :, :],
                                tri16[:, :].unsqueeze(1).unsqueeze(1).to_broadcast([P, 2, H, P]),
                                al[:, g[1], :, c, :].unsqueeze(3).to_broadcast([P, 2, H, P]),
                                ALU.mult).then_inc(am_done, 1)

                        def group(g, front, ahead):
                            for c in range(CH):
                                q = CH * order(g) + c
                                if c == 0:
                                    taken(pool, g, W_DEC)
                                pool.wait_ge(xtok_done, after(q + 1))
                                pool.wait_ge(y3_done, after(q))
                                nc.gpsimd.tensor_tensor(heads(dx[:, :]), heads(xtok[:, :]), over(head_d, HD), ALU.mult)\
                                  .then_inc(dx_done, 1)
                                pool.wait_ge(dtx_done, after(q + 1))
                                pool.wait_ge(dx_done, after(q + 1))
                                nc.gpsimd.tensor_tensor(heads(xtok[:, :]), heads(dtx[:, :]),
                                                        over(dec[:, g[1], 1, c, :], HD), ALU.mult).then_inc(dtxe_done, 1)
                                if c < CH - 1:
                                    masked(g, c + 1)
                                elif front is not None:
                                    masked(front, 0)
                                if c == 1 and ahead is not None:
                                    inv_std(ahead)

                        inv_std((0, 1))
                        masked((0, 0), 0)
                        all_groups(pool, group)

                    @block.scalar
                    def _(act):
                        def copy_transposed(f, k):
                            bank, _ = wide_use(f, W_TR[k])
                            act.wait_ge(tr_done, after(KD * order(f) + k + 1))
                            nc.scalar.activation(xnt[:, k, :], wide[bank][:, :], ACT.Copy).then_inc(wide_free[bank], 1)

                        def conv_start(f, i):
                            b, blk, n = f[1], CONV[i], NCONV * order(f) + i
                            bank, _ = wide_use(f, W_CONV[i])
                            act.wait_ge(conv_in, after(n + 1))
                            act.wait_ge(tap_done, after((TAPS - 1) * n))
                            nc.scalar.activation(xpad[:, 0:TAPS - 1], hist[:, b, blk, :], ACT.Copy)
                            nc.scalar.activation(xpad[:, TAPS - 1:], wide[bank][:, :], ACT.Copy).then_inc(pad_done, 1)
                            act.wait_ge(pad_done, after(n + 1))
                            nc.scalar.activation(hist[:, b, blk, :], wide[bank][:, TG - TAPS + 1:], ACT.Copy)
                            nc.scalar.activation(xc[:, b, blk, :], wide[bank][:, :], ACT.Identity,
                                                 bias=cvb[:, blk:blk + 1], scale=cvw[:, blk, TAPS - 1:TAPS])\
                              .then_inc(wide_free[bank], 1)

                        def conv_end(f, i):
                            b, blk, n = f[1], CONV[i], NCONV * order(f) + i
                            act.wait_ge(tap_done, after((TAPS - 1) * (n + 1)))
                            nc.scalar.activation(xc[:, b, blk, :], xc[:, b, blk, :], ACT.Silu).then_inc(xc_done, 1)

                        def gate(f, c, g):
                            bank, _ = wide_use(f, W_Z[c])
                            act.wait_ge(z_in, after(CH * order(f) + c + 1))
                            if g is not None:
                                act.wait_ge(y4_done, after(CH * order(g) + c + 1))
                            nc.scalar.activation(zs[:, c, :], wide[bank][:, :], ACT.Silu).then_inc(wide_free[bank], 1)

                        def softplus_exp(f):
                            act.wait_ge(abs_done, after(order(f) + 1))
                            nc.scalar.activation(sp_t[:, 1, :], sp_t[:, 0, :], ACT.Exp).then_inc(exp_done, 1)

                        def decays(f):
                            bank, _ = wide_use(f, W_DEC)
                            act.wait_ge(dec_in, after(order(f) + 1))
                            nc.scalar.activation(dec[:, f[1], :, :, :].rearrange("p a c h -> p (a c h)"),
                                                 wide[bank][:, 0:3 * CH * H], ACT.Exp, scale=1.0 / AS)\
                              .then_inc(wide_free[bank], 1)

                        def group(g, front, ahead):
                            for c in range(CH):
                                q = CH * order(g) + c
                                if front is not None and c == 0:
                                    for k in range(KD):
                                        copy_transposed(front, k)
                                act.wait_ge(seg_done, after(q + 1))
                                act.wait_ge(y_done, after(q))
                                nc.scalar.activation(lx[:, :, :].rearrange("p h i -> p (h i)"), seg[:, :], ACT.Exp,
                                                     scale=1.0 / AS).then_inc(lx_done, 1)
                                if front is not None and c == 1:
                                    softplus_exp(front)
                                act.wait_ge(xt_done, after(q + 1))
                                act.wait_ge(st_done, after(q))
                                nc.scalar.activation(xtok[:, :], turn[:, :], ACT.Copy).then_inc(xtok_done, 1)
                                if front is not None:
                                    if c == 0:
                                        conv_start(front, 0)
                                    if c == 3:
                                        decays(front)
                                    conv_end(front, c)
                                    conv_start(front, c + 1)
                                    if c < CH - 1:
                                        gate(front, c, g)
                                act.wait_ge(yt_done, after(q + 1))
                                act.wait_ge(out_done, after(q))
                                nc.scalar.activation(yt[:, :, :].rearrange("p k i -> p (k i)"), turn[:, :], ACT.Copy)\
                                  .then_inc(ytc_done, 1)
                                if front is not None and c == CH - 1:
                                    gate(front, c, g)
                                    conv_end(front, CH)

                        act.wait_ge(late_in, 16 * N_LATE)
                        nc.scalar.activation(a_exp[:, :], head_alog, ACT.Exp).then_inc(a_exp_done, 1)
                        act.wait_ge(set_done, N_SET)
                        f0 = (0, 0)
                        for k in range(KD):
                            copy_transposed(f0, k)
                        conv_start(f0, 0)
                        softplus_exp(f0)
                        conv_end(f0, 0)
                        for c in range(CH):
                            conv_start(f0, c + 1)
                            gate(f0, c, None)
                            if c == 2:
                                decays(f0)
                            conv_end(f0, c + 1)
                        all_groups(act, group)

                    @block.vector
                    def _(dve):
                        def stats(f):
                            for c in range(CH):
                                nc.vector.bn_stats(stat[:, c, :], xt(tile(f, c))).then_inc(stat_done, 1)

                        def variance(f):
                            for c in range(CH):
                                last = nc.vector.bn_aggr(mv[:, c, :], stat[:, c, :])
                            last.then_inc(mv_done, 1)
                            dve.wait_ge(mv_done, after(order(f) + 1))
                            nc.vector.tensor_scalar(var[:, :], mv[:, :, 1], LN_EPS, None, ALU.add).then_inc(var_done, 1)

                        def normalize(f):
                            dve.wait_ge(rstd_done, after(order(f) + 1))
                            dve.wait_ge(tr_done, after(KD * order(f)))
                            for c in range(CH):
                                last = nc.vector.tensor_scalar(xn[:, c, :], xt(tile(f, c)), mv[:, c, 0:1],
                                                               rstd[:, c:c + 1], ALU.subtract, ALU.mult)
                            last.then_inc(xn_done, 1)

                        def taps(f, i):
                            b, blk, n = f[1], CONV[i], NCONV * order(f) + i
                            dve.wait_ge(pad_done, after(n + 1))
                            taken(dve, f, W_CONV[i])
                            for t in range(TAPS - 1):
                                if t:
                                    dve.wait_ge(tap_done, after((TAPS - 1) * n + t))
                                nc.vector.scalar_tensor_tensor(xc[:, b, blk, :], xpad[:, t:t + TG], cvw[:, blk, t:t + 1],
                                                               xc[:, b, blk, :], ALU.mult, ALU.add).then_inc(tap_done, 1)

                        def softplus_start(f):
                            bank, _ = wide_use(f, W_DT)
                            dve.wait_ge(dt_in, after(order(f) + 1))
                            nc.vector.tensor_tensor(dtv[:, :].rearrange("p (c h) -> p c h", h=H),
                                                    wide[bank][:, 0:CH * H].rearrange("p (c h) -> p c h", h=H),
                                                    head_bias.unsqueeze(1).to_broadcast([P, CH, H]), ALU.add)\
                              .then_inc(wide_free[bank], 1)
                            taken(dve, f, W_DT)
                            nc.vector.scalar_tensor_tensor(sp_t[:, 0, :], dtv[:, :], -1.0, dtv[:, :], ALU.mult, ALU.min)\
                              .then_inc(abs_done, 1)

                        def softplus_end(f):
                            n = order(f)
                            count = [0]

                            def step(ins):
                                count[0] += 1
                                ins.then_inc(sp_step, 1)
                                dve.wait_ge(sp_step, after(SP_STEPS * n + count[0]))

                            v, u, r, s, s2, p = (sp_t[:, i, :] for i in (0, 1, 2, 3, 4, 5))
                            dve.wait_ge(exp_done, after(n + 1))
                            step(nc.vector.tensor_scalar(r, dtv[:, :], 0.0, None, ALU.max))
                            step(nc.vector.tensor_scalar(v, u, 2.0, None, ALU.add))
                            step(nc.vector.reciprocal(s2, v))
                            step(nc.vector.tensor_tensor(s, u, s2, ALU.mult))
                            step(nc.vector.tensor_tensor(s2, s, s, ALU.mult))
                            step(nc.vector.tensor_scalar(p, s2, 1.0 / 15, None, ALU.mult))
                            for odd in (13, 11, 9, 7, 5, 3):
                                step(nc.vector.scalar_tensor_tensor(p, p, 1.0 / odd, s2, ALU.add, ALU.mult))
                            step(nc.vector.scalar_tensor_tensor(p, p, 1.0, s, ALU.add, ALU.mult))
                            d = dt[:, f[1], :, :].rearrange("p c h -> p (c h)")
                            step(nc.vector.scalar_tensor_tensor(d, p, 2.0, r, ALU.mult, ALU.add))
                            step(nc.vector.tensor_tensor(a32.rearrange("p (c h) -> p c h", h=H), dt[:, f[1], :, :],
                                                         a_neg[:, :].unsqueeze(1).to_broadcast([P, CH, H]), ALU.mult))
                            step(nc.vector.tensor_scalar(a32, a32, A_MIN, AS, ALU.max, ALU.mult))
                            hi, lo = (al[:, f[1], i, :, :].rearrange("p c h -> p (c h)") for i in (0, 1))
                            step(nc.vector.tensor_copy(hi, a32))
                            assert count[0] == SP_STEPS
                            nc.vector.tensor_tensor(lo, a32, hi, ALU.subtract).then_inc(a_done, 1)

                        def residual(g, c):
                            q = CH * order(g) + c
                            dve.wait_ge(out_done, after(q + 1))
                            nc.vector.tensor_tensor(xt(tile(g, c)), xt(tile(g, c)), near[:, :], ALU.add)\
                              .then_inc(res_done, 1)

                        def group(g, front, ahead):
                            b = g[1]
                            for c in range(CH):
                                q = CH * order(g) + c
                                dve.wait_ge(bc_done, after(q + 1))
                                dve.wait_ge(m_done, after(q))
                                nc.vector.tensor_tensor(gm[:, :], bc[:, 0:P], tri[:, :], ALU.mult).then_inc(gm_done, 1)
                                dve.wait_ge(st_done, after(q))
                                nc.vector.tensor_copy(btok[:, :], bc[:, P:P + N]).then_inc(btok_done, 1)
                                dve.wait_ge(xtok_done, after(q + 1))
                                dve.wait_ge(dtxe_done, after(q))
                                if c == 0:
                                    dve.wait_ge(a_done, after(order(g) + 1))
                                nc.vector.tensor_tensor(heads(dtx[:, :]), heads(xtok[:, :]), over(dt[:, b, c, :], HD),
                                                        ALU.mult).then_inc(dtx_done, 1)
                                dve.wait_ge(lx_done, after(q + 1))
                                dve.wait_ge(gm_done, after(q + 1))
                                nc.vector.tensor_tensor(lx[:, :, :], lx[:, :, :],
                                                        gm[:, :].unsqueeze(1).to_broadcast([P, H, P]), ALU.mult)\
                                  .then_inc(m_done, 1)
                                if c:
                                    residual(g, c - 1)
                                if c == 0 and ahead is not None:
                                    stats(ahead)
                                if c == 0 and front is not None:
                                    softplus_start(front)
                                    taps(front, 0)
                                if c == 2 and front is not None:
                                    softplus_end(front)
                                if c == 3 and ahead is not None:
                                    normalize(ahead)
                                dve.wait_ge(y_done, after(q + 1))
                                dve.wait_ge(yt_done, after(q))
                                if c == 0:
                                    taken(dve, g, W_DEC)
                                nc.vector.tensor_tensor(heads(yv[:, :]), heads(far[:, :]), over(dec[:, b, 0, c, :], HD),
                                                        ALU.mult).then_inc(y1_done, 1)
                                dve.wait_ge(y1_done, after(q + 1))
                                nc.vector.tensor_tensor(yv[:, :], yv[:, :], near[:, :], ALU.add).then_inc(y2_done, 1)
                                dve.wait_ge(y2_done, after(q + 1))
                                dve.wait_ge(dx_done, after(q + 1))
                                nc.vector.tensor_tensor(yv[:, :], yv[:, :], dx[:, :], ALU.add).then_inc(y3_done, 1)
                                dve.wait_ge(y3_done, after(q + 1))
                                taken(dve, g, W_Z[c])
                                nc.vector.tensor_tensor(yv[:, :], yv[:, :], zs[:, c, :], ALU.mult).then_inc(y4_done, 1)
                                if c == 1 and ahead is not None:
                                    dve.wait_ge(stat_done, after(CH * order(ahead) + CH))
                                dve.wait_ge(s2_done, after(q))
                                nc.vector.tensor_tensor(heads(state[b]), heads(state[b]), over(dec[0:N, b, 2, c, :], HD),
                                                        ALU.mult).then_inc(s1_done, 1)
                                if c == 1 and ahead is not None:
                                    variance(ahead)
                                dve.wait_ge(st_done, after(q + 1))
                                dve.wait_ge(s1_done, after(q + 1))
                                nc.vector.tensor_tensor(state[b], state[b], far[0:N, :], ALU.add).then_inc(s2_done, 1)
                                if front is not None:
                                    taps(front, c + 1)
                            residual(g, CH - 1)

                        f0, f1 = (0, 0), (0, 1)
                        stats(f1)
                        dve.wait_ge(late_in, 16 * N_LATE)
                        dve.wait_ge(a_exp_done, 1)
                        nc.vector.tensor_scalar(a_neg[:, :], a_exp[:, :], -1.0, None, ALU.mult).then_inc(a_neg_done, 1)
                        dve.wait_ge(stat_done, after(CH * order(f1) + CH))
                        variance(f1)
                        dve.wait_ge(a_neg_done, 1)
                        softplus_start(f0)
                        dve.wait_ge(set_done, N_SET)
                        taps(f0, 0)
                        softplus_end(f0)
                        for c in range(CH):
                            taps(f0, c + 1)
                            if c == 0:
                                normalize(f1)
                        all_groups(dve, group)

                    @block.tensor
                    def _(pe):
                        def product(f, k):
                            bank, before = wide_use(f, k)
                            pe.wait_ge(wide_free[bank], after(before))
                            return wide[bank]

                        def transposes(f, k0, k1):
                            if k0 == 0:
                                pe.wait_ge(xn_done, after(order(f) + 1))
                            for k in range(k0, k1):
                                acc = product(f, W_TR[k])
                                for c in range(CH):
                                    last = nc.tensor.transpose(acc[:, cols(c)], xn[:, c, cols(k)], ident[:, :])
                                last.then_inc(tr_done, 1)

                        def project_conv(f, i):
                            if i == 0:
                                taken(pe, f, W_TR[2])
                                taken(pe, f, W_TR[3])
                            acc = product(f, W_CONV[i])
                            row = D + CONV[i] * P
                            for k in range(KD):
                                last = nc.tensor.matmul(acc[:, :], win[:, k, row:row + P], xnt[:, k, :],
                                                        start=(k == 0), stop=(k == KD - 1))
                            last.then_inc(conv_in, 1)

                        def project_dt(f):
                            acc = product(f, W_DT)
                            for c in range(CH):
                                for k in range(KD):
                                    last = nc.tensor.matmul(acc[:, c * H:(c + 1) * H], xnt[:, k, cols(c)],
                                                            win[:, k, W_IN - H:W_IN], start=(k == 0), stop=(k == KD - 1))
                            last.then_inc(dt_in, 1)

                        def project_z(f, c, k0=0, k1=KD):
                            acc = product(f, W_Z[c]) if k0 == 0 else wide[wide_use(f, W_Z[c])[0]]
                            for k in range(k0, k1):
                                last = nc.tensor.matmul(acc[:, :], xnt[:, k, cols(c)], win[:, k, 0:D],
                                                        start=(k == 0), stop=(k == KD - 1))
                            if k1 == KD:
                                last.then_inc(z_in, 1)

                        def sum_decays(f):
                            pe.wait_ge(a_done, after(order(f) + 1))
                            acc = product(f, W_DEC)
                            for i, m in enumerate((tri16, after16, ones16)):
                                for part in range(2):
                                    last = nc.tensor.matmul(acc[:, i * CH * H:(i + 1) * CH * H], m[:, :],
                                                            al[:, f[1], part, :, :].rearrange("p c h -> p (c h)"),
                                                            start=(part == 0), stop=(part == 1))
                            last.then_inc(dec_in, 1)

                        def chunk_decays(g, c):
                            q, b = CH * order(g) + c, g[1]
                            pe.wait_ge(am_done, after(q + 1))
                            pe.wait_ge(lx_done, after(q))
                            for half in range(2):
                                for part in range(2):
                                    last = nc.tensor.matmul(seg[:, half * 512:(half + 1) * 512], after16[:, :],
                                                            am[:, part, 4 * half:4 * half + 4, :].rearrange("p h i -> p (h i)"),
                                                            start=(part == 0), stop=(part == 1))
                            last.then_inc(seg_done, 1)

                        def chunk_start(g, c):
                            q, b = CH * order(g) + c, g[1]
                            if c == 0:
                                pe.wait_ge(xc_done, after(NCONV * (order(g) + 1)))
                                pe.wait_ge(cc_in, 16 * (order(g) + 1))
                            pe.wait_ge(btok_done, after(q))
                            nc.tensor.matmul(bc[:, 0:P], xc[0:N, b, 4, cols(c)], cc[:, b, cols(c)], start=True, stop=True)
                            nc.tensor.transpose(bc[:, P:P + N], xc[0:N, b, 4, cols(c)], ident[0:N, 0:N]).then_inc(bc_done, 1)
                            pe.wait_ge(ytc_done, after(q))
                            for k in range(KD):
                                last = nc.tensor.transpose(turn[:, cols(k)], xc[:, b, k, cols(c)], ident[:, :])
                            last.then_inc(xt_done, 1)

                        def chunk_y(g, c):
                            q, b = CH * order(g) + c, g[1]
                            pe.wait_ge(s2_done, after(q))
                            nc.tensor.matmul(far[:, :], cc[:, b, cols(c)], state[b], start=True, stop=True)
                            pe.wait_ge(dtx_done, after(q + 1))
                            pe.wait_ge(m_done, after(q + 1))
                            pe.wait_ge(res_done, after(q))
                            for h in range(H):
                                last = nc.tensor.matmul(near[:, h * HD:(h + 1) * HD], lx[:, h, :],
                                                        dtx[:, h * HD:(h + 1) * HD], start=True, stop=True)
                            last.then_inc(y_done, 1)

                        def chunk_state(g, c):
                            q = CH * order(g) + c
                            pe.wait_ge(y1_done, after(q + 1))
                            pe.wait_ge(dtxe_done, after(q + 1))
                            pe.wait_ge(btok_done, after(q + 1))
                            nc.tensor.matmul(far[0:N, :], btok[:, :], xtok[:, :], start=True, stop=True).then_inc(st_done, 1)

                        def turn_y(g, c):
                            q = CH * order(g) + c
                            pe.wait_ge(y4_done, after(q + 1))
                            pe.wait_ge(xtok_done, after(q + 1))
                            for k in range(KD):
                                last = nc.tensor.transpose(turn[:, cols(k)], yv[:, cols(k)], ident[:, :])
                            last.then_inc(yt_done, 1)

                        def project_out(g, c):
                            q = CH * order(g) + c
                            pe.wait_ge(ytc_done, after(q + 1))
                            pe.wait_ge(y2_done, after(q + 1))
                            for k in range(KD):
                                last = nc.tensor.matmul(near[:, :], yt[:, k, :], wout[:, k, :],
                                                        start=(k == 0), stop=(k == KD - 1))
                            last.then_inc(out_done, 1)

                        def group(g, front, ahead):
                            for c in range(CH):
                                if front is not None and c == 0:
                                    transposes(front, 0, 2)
                                    chunk_decays(g, c)
                                    transposes(front, 2, 4)
                                else:
                                    chunk_decays(g, c)
                                chunk_start(g, c)
                                if c:
                                    project_out(g, c - 1)
                                if front is not None:
                                    if c == 0:
                                        project_conv(front, 0)
                                        project_dt(front)
                                    if c == 3:
                                        sum_decays(front)
                                    if c:
                                        project_conv(front, c + 1)
                                chunk_y(g, c)
                                if front is not None:
                                    if c == 0:
                                        project_conv(front, c + 1)
                                    project_z(front, c, 0, KD if c < CH - 1 else KD - 1)
                                chunk_state(g, c)
                                turn_y(g, c)
                            if front is not None:
                                project_z(front, CH - 1, KD - 1, KD)
                            project_out(g, CH - 1)

                        pe.wait_ge(late_in, 16 * N_LATE)
                        pe.wait_ge(set_done, N_SET)
                        f0 = (0, 0)
                        transposes(f0, 0, KD)
                        project_conv(f0, 0)
                        project_dt(f0)
                        for c in range(CH):
                            project_conv(f0, c + 1)
                            project_z(f0, c)
                            if c == 2:
                                sum_decays(f0)
                        all_groups(pe, group)

        ffn_part("f1_", True)
        ssm_part()
        ffn_part("f2_", False)


def kernel(L0_attn_u, L0_attn_W_in, L0_attn_conv_w, L0_attn_conv_b, L0_attn_W_out, L0_attn_A_log, L0_attn_D_param,
           L0_attn_dt_bias, L0_ffn_W_up, L0_ffn_W_gate, L0_ffn_W_down):
    import numpy as np
    import concourse.bacc as bacc
    from concourse.bass_utils import run_bass_kernel_spmd

    def rows(w_t, blocks):
        n = w_t.shape[1]
        return np.ascontiguousarray(w_t.reshape(blocks, P, n).transpose(1, 0, 2).reshape(P, blocks * n))

    def quarters(w):
        v = np.asarray(w).T.reshape(KD, P, 4, E // 4).transpose(1, 2, 0, 3)
        return np.ascontiguousarray(v.reshape(P, KD * E))

    arrays = dict(
        u=np.ascontiguousarray(np.asarray(L0_attn_u).reshape(B * L, D)),
        w_up=quarters(L0_ffn_W_up),
        w_gate=quarters(L0_ffn_W_gate),
        w_down=rows(np.asarray(L0_ffn_W_down).T, KE),
        w_in=rows(np.asarray(L0_attn_W_in).T, KD),
        w_out=rows(np.asarray(L0_attn_W_out).T, KD),
        conv_w=rows(np.asarray(L0_attn_conv_w).reshape(NCONV * P, TAPS), NCONV),
        conv_b=rows(np.asarray(L0_attn_conv_b).reshape(NCONV * P, 1), NCONV),
        head_par=np.ascontiguousarray(np.tile(np.concatenate(
            [np.asarray(L0_attn_A_log), np.asarray(L0_attn_D_param), np.asarray(L0_attn_dt_bias)])[None, :], (P, 1))),
    )
    nc = bacc.Bacc("TRN2", target_bir_lowering=False, num_devices=1)
    args = [nc.dram_tensor("in_" + n, a.shape, mybir.dt.from_np(a.dtype), kind="ExternalInput").ap()
            for n, a in arrays.items()]
    res = nc.dram_tensor("res", (B * L, D), F32, kind="ExternalOutput").ap()
    macaron_kernel(nc, *args, res)
    r = run_bass_kernel_spmd(nc, [{"in_" + n: a for n, a in arrays.items()}], core_ids=[0])
    return r.results[0]["res"].reshape(B, L, D)
```

```python
from contextlib import ExitStack

import concourse.bass as bass
from concourse import mybir

F32 = mybir.dt.float32
F16 = mybir.dt.float16
F8 = mybir.dt.float8e4
ALU = mybir.AluOpType
ACT = mybir.ActivationFunctionType
AX = mybir.AxisListType

P = 128
B, L, D, E = 2, 2048, 512, 2048
H, N, HD = 8, 64, 64
KD, KE = D // P, E // P
TG = 512
CH = TG // P
NG = B * L // TG
GB = NG // B
NCONV = (D + 2 * N) // P
TAPS = 4
W_IN = 2 * D + 2 * N + H
LN_EPS, Q_EPS = 1e-5, 1e-8
XS = 2.0 ** 11
HS = 2.0 ** -5
HT, HE, HK = TG // 2, D // 2, KE // 2
AS = 2.0 ** 7
A_MIN = -200.0


def macaron_kernel(nc, u, w_up, w_gate, w_down, w_in, w_out, conv_w, conv_b, head_par, out):
    top = ExitStack()

    def sb(ctx, name, shape, dt=F32):
        return ctx.enter_context(nc.sbuf_tensor(name, shape, dt))

    def ps(ctx, name, shape, dt=F32):
        return ctx.enter_context(nc.psum_tensor(name, shape, dt))

    def sem(ctx, name):
        return ctx.enter_context(nc.semaphore(name))

    def sems(ctx, name, n):
        return [sem(ctx, f"{name}{i}") for i in range(n)]

    with top:
        x = sb(top, "x", [P, NG * CH * D])
        wu = sb(top, "wu", [P, KD, E], F8)
        wg = sb(top, "wg", [P, KD, E], F8)
        wd = sb(top, "wd", [P, 7, HK, HE], F8)
        xn = sb(top, "xn", [P, CH, D])
        xnt = sb(top, "xnt", [P, KD, TG])
        xhi, xlo = (v.rearrange("p (k t) -> p k t", k=KD) for v in
                    (xnt[:, 0:KD // 2, :].rearrange("p k t -> p (k t)").bitcast(F16),
                     xnt[:, KD // 2:, :].rearrange("p k t -> p (k t)").bitcast(F16)))
        ident = sb(top, "ident", [P, P])
        neg_half = sb(top, "neg_half", [P, CH])
        silu_scale = sb(top, "silu_scale", [P, 1])
        hid_scale = sb(top, "hid_scale", [P, 1])
        tern_done = sem(top, "tern_done")
        out_scale = sb(top, "out_scale", [P, 1])

        late = sb(top, "late", [P, KD * E])
        late_in = sem(top, "late_in")
        bounds = [0]
        for n in (KD * W_IN, KD * D, NCONV * TAPS, NCONV, 3 * H, D, D, N, P, P, P // 2):
            bounds.append(bounds[-1] + n)
        parts = [late[:, a:b] for a, b in zip(bounds, bounds[1:])]
        win = parts[0].rearrange("p (k n) -> p k n", k=KD)
        wout = parts[1].rearrange("p (k n) -> p k n", k=KD)
        cvw = parts[2].rearrange("p (k n) -> p k n", k=NCONV)
        cvb = parts[3]
        head_alog, head_d, head_bias = (parts[4][:, i * H:(i + 1) * H] for i in range(3))
        behind = late[:, KD * E - 4 * HT:]
        state = [parts[5][0:N, :], parts[6][0:N, :]]
        late_loads = [(parts[0], w_in), (parts[1], w_out), (parts[2], conv_w), (parts[3], conv_b), (parts[4], head_par)]
        N_LATE = len(late_loads)

        def after(n):
            return n + 1

        def start_counts(eng, counting, head_start=()):
            ahead = dict(head_start)
            for s in counting:
                eng.sem_inc(s, 1 + ahead.get(s, 0))

        def xt(t):
            return x[:, bass.ds(t * D, D)]

        def ffn_part(tag, first):
            ctx = ExitStack()
            with ctx:
                h = sb(ctx, tag + "h", [P, 2, 4, HT])
                sums = behind.rearrange("p (s t) -> p s t", s=4)
                hhi = sb(ctx, tag + "hhi", [P, HK, 7, HT], F16)
                hlo = sb(ctx, tag + "hlo", [P, HK, 7, HT], F16)
                stat = sb(ctx, tag + "stat", [P, CH, 6])
                mv = sb(ctx, tag + "mv", [P, CH, 2])
                var = sb(ctx, tag + "var", [P, CH])
                rstd = sb(ctx, tag + "rstd", [P, CH])
                up_ps = [ps(ctx, f"{tag}up_ps{i}", [P, TG]) for i in range(2)]
                gate_ps = [ps(ctx, f"{tag}gate_ps{i}", [P, TG]) for i in range(2)]
                down_ps = ps(ctx, tag + "down_ps", [P, 4 * HE])
                tr_ps = [ps(ctx, f"{tag}tr_ps{i}", [P, TG]) for i in range(2)]

                stat_done = sem(ctx, tag + "stat_done")
                mv_done = sem(ctx, tag + "mv_done")
                var_done = sem(ctx, tag + "var_done")
                rstd_done = sem(ctx, tag + "rstd_done")
                xn_done = sem(ctx, tag + "xn_done")
                tr_done = sem(ctx, tag + "tr_done")
                xhi_done = sem(ctx, tag + "xhi_done")
                xlo_done = sems(ctx, tag + "xlo_done", 2)
                ug_done = sem(ctx, tag + "ug_done")
                sil_done = sem(ctx, tag + "sil_done")
                hid_done = sems(ctx, tag + "hid_done", 2)
                sum_step = sem(ctx, tag + "sum_step")
                hhi_done = sem(ctx, tag + "hhi_done")
                hla_done = sems(ctx, tag + "hla_done", 2)
                hlo_done = sems(ctx, tag + "hlo_done", 2)
                down_done = sem(ctx, tag + "down_done")
                res_done = sem(ctx, tag + "res_done")
                pe_free = sem(ctx, tag + "pe_free")
                if first:
                    ones = sb(ctx, "ones", [P, P])
                    raw_u = x[:, 16 * D:32 * D]
                    flat_hi, flat_lo = (v[:, :, :, :].rearrange("p k s t -> p (k s t)") for v in (hhi, hlo))
                    raw_d = [flat_lo[:, 5 * 7 * HT:5 * 7 * HT + 4096].bitcast(F32), xn[:, :, :].rearrange("p c d -> p (c d)"),
                             x[:, 8 * D:12 * D], x[:, 12 * D:16 * D]]
                    masks = [flat_hi[:, 49 * HT:49 * HT + 1024], flat_lo[:, 51 * HT:51 * HT + 1024]]
                    b12 = late[:, 4736:4736 + HK * HE // 4].bitcast(F8).rearrange("p (k d) -> p k d", k=HK)
                    raw_g = late[:, :]
                    wsum = sb(ctx, "wsum", [P, 3, 4])
                    total = sb(ctx, "total", [P, 3])
                    scale = sb(ctx, "scale", [P, 3])
                    half = sb(ctx, "half", [P, 3])
                    nhalf = sb(ctx, "nhalf", [P, 3])
                    rscale = sb(ctx, "rscale", [P, 1])
                    prod = sb(ctx, "prod", [P, 2])
                    const_done = sem(ctx, "const_done")
                    raw_in = sems(ctx, "raw_in", 12)
                    x_in = sem(ctx, "x_in")
                    abs_done = sem(ctx, "abs_done")
                    up_done = sem(ctx, "up_done")
                    sum_done = sem(ctx, "sum_done")
                    sc_done = sem(ctx, "sc_done")
                    mask_done = sem(ctx, "mask_done")
                    t_done = sem(ctx, "t_done")
                else:
                    x_out = sem(ctx, "x_out")

                done_before = () if first else ((stat_done, CH), (mv_done, 1), (var_done, 1), (rstd_done, 1), (xn_done, 1),
                                                (tr_done, KD), (xhi_done, KD), *((s, KD // 2) for s in xlo_done))

                u_v = u.rearrange("(t p) d -> p t d", p=P)
                out_v = out.rearrange("(t p) d -> p t d", p=P)
                x_v = x[:, :].rearrange("p (t d) -> p t d", d=D)
                raws = [(w_up, 0), (w_gate, 1), (w_down, 2)]

                def raw_q(w, q):
                    if w == 2:
                        return raw_d[q]
                    at = q if w == 0 else 3 - q
                    return (raw_u, raw_g)[w][:, at * 2048:(at + 1) * 2048]

                TERNARY = ([(0, q, n, n + 256) for q in (0, 2) for n in (0, 256)]
                           + [(1, q, 0, P) for q in (0, 2)]
                           + [(1, 0, P, 256), (1, 2, P, 256), (1, 0, 256, 512), (1, 2, 256, 512)]
                           + [(w, q, n, n + 256) for n in (0, 256) for q in (1, 3) for w in (0, 1)]
                           + [(2, q, n, n + HE) for q in range(4) for n in (0, HE)])
                N_TERN, T_EARLY, T_AFTER = len(TERNARY), 8, (1, 1, 1, 1, 1, 1, 1, 1, 2, 1, 2, 1, 2, 1, 1, 0)
                AT_DOWN = [n for n, piece in enumerate(TERNARY) if piece[0] == 2]

                def block_of(i):
                    return i // 2 + HK * (i % 2)

                def halves(i, buf):
                    return h[:, buf, 0:4:3, :] if i % 2 == 0 else h[:, buf, 1:3, :]

                def two(ap):
                    return ap.rearrange("p (a t) -> p a t", a=2)

                PRODUCT = dict(P1=(0, 0, ((0, 0), (0, 1), (1, 0), (1, 1))), P2=(1, 1, ((0, 0),)), P3=(2, 6, ((0, 1),)),
                               P4=(3, 2, ((1, 0),)), P5=(4, 3, ((0, 1), (1, 1))), P6=(5, 4, ((0, 1), (1, 0), (1, 1))),
                               P7=(6, 5, ((1, 0), (1, 1))))
                ORDER = ("P2", "P1", "P3", "P5", "P7", "P6", "P4")
                T_ORDER = ("P5", "P7", "P6", "P4")
                STEPS = [sum(len(PRODUCT[name][2]) for name in ORDER[:j + 1]) for j in range(7)]

                def down_at(g, name):
                    return after(7 * g + 1 + ORDER.index(name))

                def res_at(g, k):
                    return after(STEPS[-1] * g + k)

                def bank(name):
                    return down_ps[:, D * (ORDER.index(name) % 2):D * (ORDER.index(name) % 2 + 1)]

                def at_first(p):
                    return 3 if p < HK - 1 else 2

                def pair_sums(eng, ops, g, p):
                    n = 4 * (HK * g + p)
                    A11, A12, A22, A21 = (h[:, p % 2, k, :] for k in range(4))
                    S1, S2, S3, S4 = (sums[:, k, :] for k in range(4))
                    for half in range(2):
                        eng.wait_ge(hid_done[half], after(HK * g + p + 1))
                    if p:
                        eng.wait_ge(hlo_done[(p - 1) % 2], after(HK // 2 * g + (p - 1) // 2 + 1))
                    else:
                        eng.wait_ge(hlo_done[1], after(HK // 2 * g))
                        if first:
                            eng.wait_ge(tern_done, 1 + max(n for n, v in enumerate(TERNARY) if v[:2] == (1, 0)))
                    ops.tensor_tensor(S1, A21, A22, ALU.add).then_inc(sum_step, 1)
                    ops.tensor_tensor(S3, A11, A21, ALU.subtract).then_inc(sum_step, 1)
                    eng.wait_ge(sum_step, after(n + 1))
                    ops.tensor_tensor(S2, S1, A11, ALU.subtract).then_inc(sum_step, 1)
                    eng.wait_ge(sum_step, after(n + 3))
                    ops.tensor_tensor(S4, A12, S2, ALU.subtract).then_inc(sum_step, 1)

                with nc.Block() as block:

                    @block.sync
                    def _(sp):
                        if first:
                            def load_x(g):
                                sp.dma_start(x_v[:, CH * g:CH * g + CH, :],
                                             u_v[:, CH * g:CH * g + CH, :]).then_inc(x_in, 16)

                            load_x(0)
                            for w in (0, 1, 2):
                                for q in range(4):
                                    if (w, q) == (2, 1):
                                        sp.wait_ge(tr_done, after(KD))
                                    sp.dma_start(raw_q(w, q), raws[w][0][:, q * 2048:(q + 1) * 2048])\
                                      .then_inc(raw_in[4 * w + q], 16)
                            for g in range(1, NG):
                                sp.wait_ge(x_in, 16 * g)
                                if g == 2:
                                    sp.wait_ge(tern_done, N_TERN)
                                    sp.wait_ge(t_done, 4)
                                    for dst, src in late_loads:
                                        sp.dma_start(dst, src[:, :]).then_inc(late_in, 16)
                                load_x(g)
                            sp.wait_ge(x_in, 16 * NG)
                        else:
                            with sp.Fori(0, NG) as g:
                                sp.wait_ge(res_done, res_at(g, STEPS[-1]))
                                sp.dma_start(out_v[:, bass.ds(CH * g, CH), :],
                                             x_v[:, bass.ds(CH * g, CH), :]).then_inc(x_out, 16)
                            sp.wait_ge(x_out, 16 * NG)

                    @block.gpsimd
                    def _(pool):
                        start_counts(pool, [rstd_done, *hla_done, *hlo_done] + [sum_step] * first, done_before)
                        if first:
                            nc.gpsimd.memset(ones[:, :], 1.0).then_inc(const_done, 1)
                            nc.gpsimd.memset(neg_half[:, :], -0.5).then_inc(const_done, 1)
                            pool.wait_ge(const_done, 1)
                            nc.gpsimd.affine_select(out=ident[:, :], in_=ones[:, :], compare_op=ALU.is_equal, fill=0.0,
                                                    base=0, pattern=[[-1, P]], channel_multiplier=1)\
                              .then_inc(const_done, 1)
                            pool.wait_ge(const_done, 3)

                        def inv_std(g):
                            pool.wait_ge(var_done, after(g + 1))
                            nc.gpsimd.tensor_tensor(rstd[:, :], var[:, :], neg_half[:, :], ALU.pow)\
                              .then_inc(rstd_done, 1)

                        def low_parts(g, p, part):
                            pool.wait_ge(hhi_done, after(2 * (HK * g + p) + part + 1))
                            n = at_first(p)
                            for a, b, src in (((0, n, h[:, p % 2, 0:n, :]),), ((n, 3, h[:, p % 2, n:3, :]), (3, 7, sums)))[part]:
                                if a < b:
                                    last = nc.gpsimd.tensor_tensor(hlo[:, p, a:b, :], src, hhi[:, p, a:b, :], ALU.subtract)
                            last.then_inc((hla_done, hlo_done)[part][p % 2], 1)

                        def t_sums():
                            B11, B21, B22, T4, T1, T2, T3 = (wd[:, i, :, :] for i in range(7))
                            pool.wait_ge(tern_done, N_TERN)
                            for dst, a, b in ((T1, b12, B11), (T3, B22, b12), (T2, B22, T1), (T4, B21, T2)):
                                if dst is T4 or dst is T2:
                                    pool.wait_ge(t_done, 3 if dst is T4 else 1)
                                nc.gpsimd.tensor_tensor(dst, a, b, ALU.subtract, saturate=False).then_inc(t_done, 1)

                        def group(g, more_ln, between=None):
                            for p in range(HK):
                                if first and p == 5:
                                    pool.wait_ge(tern_done, 2 + AT_DOWN[0])
                                if first and p == HK - 1:
                                    pool.wait_ge(tern_done, N_TERN)
                                if between is not None and p < HK - 1:
                                    pair_sums(pool, nc.gpsimd, g, p)
                                low_parts(g, p, 0)
                                low_parts(g, p, 1)
                                if between is not None:
                                    between(p)
                                if p == 4 and more_ln:
                                    inv_std(g + 1)

                        if first:
                            inv_std(0)
                            group(0, True, lambda p: t_sums() if p == HK - 1 else None)
                        with pool.Fori(1 if first else 0, NG - 1) as g:
                            group(g, True)
                        group(NG - 1, first)

                    @block.scalar
                    def _(act):
                        start_counts(act, [xhi_done, sil_done, hhi_done], done_before)
                        def abs_sum(w, q):
                            at = (q if w < 2 else 3) * 2048
                            act.wait_ge(raw_in[4 * w + q], 16)
                            if w:
                                act.wait_ge(abs_done, 4 * (w - 1) + q + 1 if w < 2 else 4 * w + q)
                            nc.scalar.activation(flat_hi[:, at:at + 2048], raw_q(w, q), ACT.Abs,
                                                 accum_out=wsum[:, w, q:q + 1]).then_inc(abs_done, 1)

                        def high_parts(act, g, k):
                            act.wait_ge(tr_done, after(KD * g + k + 1))
                            if first and isinstance(g, int) and g == NG:
                                nc.scalar.activation(xnt[:, k, :], tr_ps[k % 2][:, :], ACT.Copy).then_inc(xlo_done[k % 2], 1)
                                return
                            nc.scalar.activation(xhi[:, k, :], tr_ps[k % 2][:, :], ACT.Copy, scale=XS)\
                              .then_inc(xhi_done, 1)

                        if first:
                            for w in range(2):
                                for q in range(4):
                                    if w == 0 and q == 2:
                                        for k in range(KD):
                                            high_parts(act, 0, k)
                                    abs_sum(w, q)

                        def silu(g, i):
                            if first and i < 2 and isinstance(g, int) and g == 0:
                                act.wait_ge(up_done, i + 1)
                            else:
                                act.wait_ge(ug_done, after(KE * g + i + 1))
                            act.wait_ge(hlo_done[i // 2 % 2], after(HK // 2 * g + i // 4))
                            nc.scalar.activation(halves(i, i // 2 % 2), two(up_ps[i % 2][:, :]), ACT.Silu,
                                                 scale=silu_scale[:, 0:1]).then_inc(sil_done, 1)

                        def hid_high(g, p):
                            if first and p == 3:
                                act.wait_ge(abs_done, 12)
                            if first and p == HK - 1:
                                act.wait_ge(tern_done, N_TERN)
                            for half in range(2):
                                act.wait_ge(hid_done[half], after(HK * g + p + 1))
                            n = at_first(p)
                            nc.scalar.activation(hhi[:, p, 0:n, :], h[:, p % 2, 0:n, :], ACT.Copy).then_inc(hhi_done, 1)
                            if n < 3:
                                nc.scalar.activation(hhi[:, p, n:3, :], h[:, p % 2, n:3, :], ACT.Copy)

                        def sums_high(g, p):
                            act.wait_ge(sum_step, after(4 * (HK * g + p) + 4))
                            nc.scalar.activation(hhi[:, p, 3:7, :], sums, ACT.Copy).then_inc(hhi_done, 1)

                        def group(g, more, between=None):
                            for i in range(KE):
                                silu(g, i)
                                if between is not None:
                                    between(i)
                                if i and i % 2 == 0:
                                    hid_high(g, i // 2 - 1)
                                    sums_high(g, i // 2 - 1)
                            hid_high(g, HK - 1)
                            sums_high(g, HK - 1)
                            if more or first:
                                for k in range(KD):
                                    high_parts(act, g + 1, k)

                        if first:
                            def w_down_sums(e):
                                if 1 <= e <= 4:
                                    abs_sum(2, e - 1)

                            group(0, True, w_down_sums)
                        with act.Fori(1 if first else 0, NG - 1) as g:
                            group(g, True)
                        group(NG - 1, False)

                    @block.vector
                    def _(dve):
                        start_counts(dve, [*hid_done, *xlo_done, stat_done, mv_done, var_done, xn_done, res_done]
                                     + [sum_step] * (not first), done_before)
                        def tile(g, c):
                            return CH * (0 if isinstance(g, int) and g == NG else g) + c

                        def stats(g, c):
                            nc.vector.bn_stats(stat[:, c, :], xt(tile(g, c))).then_inc(stat_done, 1)

                        def variance(g):
                            for c in range(CH):
                                last = nc.vector.bn_aggr(mv[:, c, :], stat[:, c, :])
                            last.then_inc(mv_done, 1)
                            dve.wait_ge(mv_done, after(g + 1))
                            nc.vector.tensor_scalar(var[:, :], mv[:, :, 1], LN_EPS, None, ALU.add)\
                              .then_inc(var_done, 1)

                        def normalize(g, c0, c1):
                            dve.wait_ge(rstd_done, after(g + 1))
                            if c0 == 0:
                                dve.wait_ge(tr_done, after(KD * g))
                                if first and not (isinstance(g, int) and g == 0):
                                    dve.wait_ge(tern_done, 1 + AT_DOWN[3])
                            for c in range(c0, c1):
                                last = nc.vector.tensor_scalar(xn[:, c, :], xt(tile(g, c)), mv[:, c, 0:1],
                                                               rstd[:, c:c + 1], ALU.subtract, ALU.mult)
                            if c1 == CH:
                                last.then_inc(xn_done, 1)

                        def low_part(g, k):
                            dve.wait_ge(xhi_done, after(KD * g + k + 1))
                            nc.vector.scalar_tensor_tensor(xlo[:, k, :], tr_ps[k % 2][:, :], XS, xhi[:, k, :],
                                                           ALU.mult, ALU.subtract).then_inc(xlo_done[k % 2], 1)

                        def hidden(g, i, stats_of=None):
                            if stats_of is not None:
                                dve.wait_ge(stat_done, after(CH * stats_of + CH))
                            dve.wait_ge(sil_done, after(KE * g + i + 1))
                            if first and i < 2 and isinstance(g, int) and g == 0:
                                dve.wait_ge(ug_done, after(i + 1))
                            at = halves(i, i // 2 % 2)
                            nc.vector.scalar_tensor_tensor(at, at, hid_scale[:, 0:1], two(gate_ps[i % 2][:, :]),
                                                           ALU.mult, ALU.mult).then_inc(hid_done[i % 2], 1)

                        def add_product(g, name):
                            j = ORDER.index(name)
                            dve.wait_ge(down_done, down_at(g, name))
                            for n, (row, column) in enumerate(PRODUCT[name][2]):
                                if n == 0 and j:
                                    dve.wait_ge(res_done, res_at(g, STEPS[j - 1]))
                                dst = x_v[:, bass.ds(CH * g + 2 * row, 2), HE * column:HE * (column + 1)]
                                src = bank(name).rearrange("p (m d) -> p m d", m=2)
                                nc.vector.scalar_tensor_tensor(dst, src, out_scale[:, 0:1], dst, ALU.mult, ALU.add)\
                                  .then_inc(res_done, 1)

                        def group(g, more, between=None):
                            more_ln = more or first
                            for i in range(KE):
                                hidden(g, i, g + 1 if more_ln and i == 8 else None)
                                if i % 2 and (between is None or i == KE - 1):
                                    pair_sums(dve, nc.vector, g, i // 2)
                                if between is not None:
                                    between(i)
                                if more_ln:
                                    if i == 4 and first and more:
                                        dve.wait_ge(x_in, 16 * g + 32)
                                    if i in (4, 6):
                                        stats(g + 1, i - 4)
                                        stats(g + 1, i - 3)
                                    if i == 8:
                                        variance(g + 1)
                                    if i == 12:
                                        normalize(g + 1, 0, 2)
                                    if i == 14:
                                        normalize(g + 1, 2, 4)

                            def low(k0):
                                if more:
                                    low_part(g + 1, k0)
                                    low_part(g + 1, k0 + 1)

                            low(0)
                            for name in ORDER:
                                add_product(g, name)
                                if name == "P1":
                                    low(2)

                        if first:
                            dve.wait_ge(x_in, 16)
                            for c in range(CH):
                                stats(0, c)
                            dve.wait_ge(stat_done, after(CH))
                            variance(0)
                            normalize(0, 0, 4)

                        steps = [0]

                        def step(ins):
                            steps[0] += 1
                            ins.then_inc(sc_done, 1)
                            dve.wait_ge(sc_done, steps[0])

                        def weight_scale(w):
                            dve.wait_ge(sum_done, w + 1)
                            step(nc.vector.tensor_reduce(total[:, w:w + 1], down_ps[:, 2 * HE * (w % 2):2 * HE * (w % 2) + 4], AX.X, ALU.add))
                            step(nc.vector.tensor_scalar(scale[:, w:w + 1], total[:, w:w + 1], 1.0 / (D * E), Q_EPS,
                                                         ALU.mult, ALU.add))
                            step(nc.vector.tensor_scalar(half[:, w:w + 1], scale[:, w:w + 1], 0.5, None, ALU.mult))
                            step(nc.vector.tensor_scalar(nhalf[:, w:w + 1], scale[:, w:w + 1], -0.5, None, ALU.mult))

                        def ternary(n):
                            w, q, e0, e1 = TERNARY[n]
                            src = raw_q(w, q).rearrange("p (k e) -> p k e", k=4)[:, :, e0:e1]
                            if w < 2:
                                dst = (wu, wg)[w][:, :, q * 512 + e0:q * 512 + e1]
                            elif (q // 2, e0) == (0, HE):
                                dst = b12[:, 4 * q:4 * q + 4, :]
                            else:
                                dst = wd[:, {(0, 0): 0, (1, 0): 1, (1, HE): 2}[q // 2, e0], 4 * (q % 2):4 * (q % 2) + 4, :]
                            m = masks[n % 2][:, 0:4 * (e1 - e0)].rearrange("p (k e) -> p k e", k=4)
                            if w == 2 and (q, e0) == (0, HE):
                                dve.wait_ge(tern_done, n)
                            nc.vector.tensor_scalar(m, src, nhalf[:, w:w + 1], None, ALU.is_lt).then_inc(mask_done, 1)
                            dve.wait_ge(mask_done, n + 1)
                            nc.vector.scalar_tensor_tensor(dst, src, half[:, w:w + 1], m, ALU.is_gt, ALU.subtract,
                                                           saturate=False)\
                              .then_inc(tern_done, 1)

                        def last_weights(e):
                            if e == 6:
                                weight_scale(2)
                                step(nc.vector.tensor_tensor(prod[:, 0:1], scale[:, 0:1], scale[:, 1:2], ALU.mult))
                                step(nc.vector.tensor_tensor(prod[:, 1:2], prod[:, 0:1], scale[:, 2:3], ALU.mult))
                                step(nc.vector.tensor_scalar(out_scale[:, :], prod[:, 1:2], 0.5 / HS, None, ALU.mult))
                            done = T_EARLY + sum(T_AFTER[:e])
                            for n in range(done, done + T_AFTER[e]):
                                ternary(n)

                        if first:
                            for k in range(KD):
                                low_part(0, k)
                            weight_scale(0)
                            step(nc.vector.tensor_scalar(silu_scale[:, :], scale[:, 0:1], 1.0 / XS, None, ALU.mult))
                            step(nc.vector.reciprocal(rscale[:, :], scale[:, 0:1]))
                            step(nc.vector.tensor_scalar(hid_scale[:, :], rscale[:, :], HS / XS, None, ALU.mult))
                            for n in range(T_EARLY):
                                if n == 4:
                                    weight_scale(1)
                                ternary(n)
                            group(0, True, last_weights)
                        with dve.Fori(1 if first else 0, NG - 1) as g:
                            group(g, True)
                        group(NG - 1, False)

                    @block.tensor
                    def _(pe):
                        start_counts(pe, [tr_done, ug_done, down_done], done_before)
                        def transposes(g, k):
                            if k == 0:
                                pe.wait_ge(xn_done, after(g + 1))
                            pe.wait_ge(xlo_done[k % 2], after(2 * g + k // 2))
                            for c in range(CH):
                                last = nc.tensor.transpose(tr_ps[k % 2][:, c * P:(c + 1) * P],
                                                           xn[:, c, k * P:(k + 1) * P], ident[:, :])
                            last.then_inc(tr_done, 1)

                        def up_gate(g, i):
                            if i == 0:
                                pe.wait_ge(xlo_done[0], after(2 * g + 2))
                                pe.wait_ge(xlo_done[1], after(2 * g + 2))
                            pe.wait_ge(hid_done[i % 2], after(HK * g + i // 2))
                            pe.sem_inc(pe_free, 1)
                            up_or_gate(i, 0)
                            up_or_gate(i, 1).then_inc(ug_done, 1)

                        def up_or_gate(i, which):
                            e, w, acc = block_of(i), (wu, wg)[which], (up_ps, gate_ps)[which][i % 2]
                            if first:
                                pe.wait_ge(tern_done, 1 + max(n for n, (v, q, e0, e1) in enumerate(TERNARY)
                                                              if v == which and q == e // 4 and e0 <= e % 4 * P < e1))
                            for k in range(KD):
                                for part in (xhi, xlo):
                                    last = nc.tensor.matmul(acc[:, :], w[:, k, e * P:(e + 1) * P], part[:, k, :],
                                                            start=(k == 0 and part is xhi),
                                                            stop=(k == KD - 1 and part is xlo))
                            return last

                        def product(g, name, m, p0=0, p1=HK):
                            weight, kind, _ = PRODUCT[name]
                            j = ORDER.index(name)
                            if m == 0 and p0 == 0:
                                pe.wait_ge(res_done, res_at(g, STEPS[j - 2] if j >= 2 else 0))
                            if m == 0 and name == "P2":
                                for p in range(p0, p1):
                                    pe.wait_ge(hla_done[p % 2], after(HK // 2 * g + p // 2 + 1))
                            if m == 0 and name == "P3":
                                for half in range(2):
                                    pe.wait_ge(hlo_done[half], after(HK // 2 * (g + 1)))
                            pe.sem_inc(pe_free, 1)
                            if first and m == 0 and p0 == 0:
                                pe.wait_ge(tern_done, N_TERN)
                                if name in T_ORDER:
                                    pe.wait_ge(t_done, 1 + T_ORDER.index(name))
                            at = bank(name)[:, m * HE:(m + 1) * HE]
                            for p in range(p0, p1):
                                for part in (hhi, hlo):
                                    last = nc.tensor.matmul(at, part[:, p, kind, m * P:(m + 1) * P], wd[:, weight, p, :],
                                                            start=(p == 0 and part is hhi),
                                                            stop=(p == HK - 1 and part is hlo))
                            if m == 1:
                                last.then_inc(down_done, 1)

                        def group(g, more, between=None):
                            more = more or first
                            for i in range(KE):
                                if between is None or i > 3:
                                    up_gate(g, i)
                                if between is not None:
                                    between(i)
                            product(g, "P2", 0, 0, HK - 1)
                            product(g, "P1", 0, 0, HK - 1)
                            if more:
                                transposes(g + 1, 0)
                                transposes(g + 1, 1)
                            for name in ORDER[0:2]:
                                product(g, name, 0, HK - 1, HK)
                                product(g, name, 1)
                            if more:
                                transposes(g + 1, 2)
                                transposes(g + 1, 3)
                            for name in ORDER[2:]:
                                product(g, name, 0)
                                product(g, name, 1)

                        if first:
                            pe.wait_ge(const_done, 3)
                        if first:
                            def weight_sum(w):
                                pe.wait_ge(abs_done, 4 * w + 4)
                                if w == 2:
                                    pe.wait_ge(sc_done, 1)
                                nc.tensor.matmul(down_ps[:, 2 * HE * (w % 2):2 * HE * (w % 2) + 4], ones[:, :], wsum[:, w, :],
                                                 start=True, stop=True).then_inc(sum_done, 1)

                            def last_sum(i):
                                if i == 1:
                                    for half in range(2):
                                        pe.wait_ge(xlo_done[half], after(KD // 2))
                                    for k in range(2):
                                        up_or_gate(k, 0).then_inc(up_done, 1)
                                    weight_sum(1)
                                    for k in range(2):
                                        pe.wait_ge(sil_done, after(k + 1))
                                        up_or_gate(k + 2, 0)
                                    for k in range(2):
                                        up_or_gate(k, 1).then_inc(ug_done, 1)
                                if i in (2, 3):
                                    pe.wait_ge(hid_done[i % 2], after(1))
                                    up_or_gate(i, 1).then_inc(ug_done, 1)
                                if i == 5:
                                    weight_sum(2)

                            for k in range(KD):
                                transposes(0, k)
                            weight_sum(0)
                            group(0, True, last_sum)
                        with pe.Fori(1 if first else 0, NG - 1) as g:
                            group(g, True)
                        group(NG - 1, False)

        def ssm_part():
            ctx = ExitStack()
            with ctx:
                xpad = sb(ctx, "s_xpad", [P, TAPS - 1 + TG])
                hist = sb(ctx, "s_hist", [P, B, NCONV, TAPS - 1])
                xc = sb(ctx, "s_xc", [P, B, NCONV, TG])
                cc = sb(ctx, "s_cc", [N, B, TG])
                zs = sb(ctx, "s_zs", [P, CH, D])
                dtv = sb(ctx, "s_dtv", [P, CH * H])
                sp_t = sb(ctx, "s_sp", [P, 7, CH * H])
                dt = sb(ctx, "s_dt", [P, B, CH, H])
                a32 = sp_t[:, 6, :]
                al = sb(ctx, "s_al", [P, B, 2, CH, H], F16)
                dec = sb(ctx, "s_dec", [P, B, 3, CH, H])
                am = sb(ctx, "s_am", [P, 2, H, P], F16)
                lx = sb(ctx, "s_lx", [P, H, P])
                btok = parts[7]
                gm = parts[8]
                xtok = sb(ctx, "s_xtok", [P, D])
                dtx = sb(ctx, "s_dtx", [P, D])
                dx = sb(ctx, "s_dx", [P, D])
                yv = sb(ctx, "s_yv", [P, D])
                yt = sb(ctx, "s_yt", [P, KD, P])
                stat = sb(ctx, "s_stat", [P, CH, 6])
                mv = sb(ctx, "s_mv", [P, CH, 2])
                var = sb(ctx, "s_var", [P, CH])
                rstd = sb(ctx, "s_rstd", [P, CH])
                a_neg = sb(ctx, "s_a_neg", [P, H])
                a_exp = sb(ctx, "s_a_exp", [P, H])
                tri = parts[9]
                tri16 = sb(ctx, "s_tri16", [P, P], F16)
                after16 = sb(ctx, "s_after16", [P, P], F16)
                ones16 = parts[10].bitcast(F16)

                wide = [ps(ctx, f"s_wide{i}", [P, 512]) for i in range(2)]
                seg = ps(ctx, "s_seg", [P, H * P])
                turn = ps(ctx, "s_turn", [P, D])
                bc = ps(ctx, "s_bc", [P, P + N])
                near = ps(ctx, "s_near", [P, D])
                far = ps(ctx, "s_far", [P, D])

                stat_done = sem(ctx, "s_stat_done")
                mv_done = sem(ctx, "s_mv_done")
                var_done = sem(ctx, "s_var_done")
                rstd_done = sem(ctx, "s_rstd_done")
                xn_done = sem(ctx, "s_xn_done")
                wide_free = sems(ctx, "s_wide_free", 2)
                tr_done = sem(ctx, "s_tr_done")
                conv_in = sem(ctx, "s_conv_in")
                dt_in = sem(ctx, "s_dt_in")
                z_in = sem(ctx, "s_z_in")
                dec_in = sem(ctx, "s_dec_in")
                pad_done = sem(ctx, "s_pad_done")
                tap_done = sem(ctx, "s_tap_done")
                xhi_done = sem(ctx, "s_xhi_done")
                xc_done = sem(ctx, "s_xc_done")
                cc_in = sem(ctx, "s_cc_in")
                abs_done = sem(ctx, "s_abs_done")
                exp_done = sem(ctx, "s_exp_done")
                sp_step = sem(ctx, "s_sp_step")
                a_done = sem(ctx, "s_a_done")
                am_done = sem(ctx, "s_am_done")
                seg_done = sem(ctx, "s_seg_done")
                bc_done = sem(ctx, "s_bc_done")
                xt_done = sem(ctx, "s_xt_done")
                y_done = sem(ctx, "s_y_done")
                st_done = sem(ctx, "s_st_done")
                yt_done = sem(ctx, "s_yt_done")
                out_done = sem(ctx, "s_out_done")
                lx_done = sem(ctx, "s_lx_done")
                xtok_done = sem(ctx, "s_xtok_done")
                ytc_done = sem(ctx, "s_ytc_done")
                gm_done = sem(ctx, "s_gm_done")
                btok_done = sem(ctx, "s_btok_done")
                dtx_done = sem(ctx, "s_dtx_done")
                m_done = sem(ctx, "s_m_done")
                y1_done = sem(ctx, "s_y1_done")
                y2_done = sem(ctx, "s_y2_done")
                y3_done = sem(ctx, "s_y3_done")
                y4_done = sem(ctx, "s_y4_done")
                s1_done = sem(ctx, "s_s1_done")
                s2_done = sem(ctx, "s_s2_done")
                res_done = sem(ctx, "s_res_done")
                dx_done = sem(ctx, "s_dx_done")
                dtxe_done = sem(ctx, "s_dtxe_done")
                set_done = sem(ctx, "s_set_done")
                a_exp_done = sem(ctx, "s_a_exp_done")
                a_neg_done = sem(ctx, "s_a_neg_done")

                done_before = ((stat_done, CH), (mv_done, 1), (var_done, 1), (rstd_done, 1), (xn_done, 1), (tr_done, KD),
                               *((s, KD // 2) for s in wide_free))

                N_SET = 8
                W_TR, W_BC, W_ALL = (0, 1, 2, 3), 4, 15
                CONV = (4, 0, 1, 2, 3)
                FIRST, LAST, BEHIND = (0, 0), (GB - 1, 1), (GB, 0)

                def w_dt(f):
                    return 7 if f is FIRST else 5

                def w_conv(f, i):
                    return ((W_BC, 6, 7, 8, 10) if f is LAST else (W_BC, 6, 8, 12, 13) if f is FIRST else (W_BC, 6, 8, 10, 13))[i]

                def w_z(f, c):
                    return ((11, 12, 13, 14) if f is LAST else (5, 9, 11, 14) if f is FIRST else (7, 9, 11, 14))[c]

                def w_dec(f):
                    return 9 if f is LAST else 10 if f is FIRST else 12

                SP_STEPS = 17

                def order(g):
                    return 2 * g[0] + g[1]

                def follower(g):
                    return (g[0], 1) if g[1] == 0 else (g[0] + 1, 0)

                def tile(g, c):
                    return c if g is BEHIND else GB * CH * g[1] + CH * g[0] + c

                def wide_use(g, k):
                    j, b = g
                    return (W_ALL * b + k) % 2, W_ALL * j + (W_ALL * b + k) // 2

                def taken(eng, g, k):
                    bank, before = wide_use(g, k)
                    eng.wait_ge(wide_free[bank], after(before + 1))

                def cols(c):
                    return slice(c * P, (c + 1) * P)

                def heads(ap):
                    return ap.rearrange("p (h n) -> p h n", h=H)

                def over(ap, n):
                    return ap.unsqueeze(2).to_broadcast([ap.shape[0], H, n])

                def all_groups(eng, group):
                    with eng.Fori(0, GB - 1) as j:
                        for b in range(B):
                            group((j, b), follower((j, b)), (j + 1, b))
                    group((GB - 1, 0), LAST, None)
                    group(LAST, None, BEHIND)

                with nc.Block() as block:

                    @block.sync
                    def _(sp):
                        def move_c(f):
                            n = order(f)
                            sp.wait_ge(xc_done, after(NCONV * n + 1))
                            sp.dma_start(cc[:, f[1], :], xc[N:2 * N, f[1], 4, :]).then_inc(cc_in, 16)

                        move_c((0, 0))

                        def group(g, front, ahead):
                            if front is not None:
                                move_c(front)

                        all_groups(sp, group)
                        sp.wait_ge(cc_in, 16 * NG)

                    @block.gpsimd
                    def _(pool):
                        start_counts(pool, [rstd_done, am_done, dx_done, dtxe_done], done_before)

                        def mask(out, src, base, step, mult):
                            return nc.gpsimd.affine_select(out=out, in_=src, compare_op=ALU.is_ge, fill=0.0, base=base,
                                                           pattern=[[step, P]], channel_multiplier=mult)

                        nc.gpsimd.memset(hist[:, :, :, :], 0.0).then_inc(set_done, 1)
                        nc.gpsimd.memset(ones16[:, :], 1.0).then_inc(set_done, 1)
                        nc.gpsimd.memset(state[0], 0.0).then_inc(set_done, 1)
                        nc.gpsimd.memset(state[1], 0.0).then_inc(set_done, 1)
                        nc.gpsimd.memset(tri[:, :], 1.0).then_inc(set_done, 1)
                        pool.wait_ge(set_done, 5)
                        mask(tri[:, :], tri[:, :], 0, 1, -1).then_inc(set_done, 1)
                        mask(tri16[:, :], ones16[:, :], 0, 1, -1).then_inc(set_done, 1)
                        mask(after16[:, :], ones16[:, :], -1, -1, 1).then_inc(set_done, 1)
                        pool.wait_ge(set_done, N_SET)

                        def inv_std(f):
                            pool.wait_ge(var_done, after(order(f) + 1))
                            nc.gpsimd.tensor_tensor(rstd[:, :], var[:, :], neg_half[:, :], ALU.pow).then_inc(rstd_done, 1)

                        def masked(g, c):
                            q = CH * order(g) + c
                            if c == 0:
                                pool.wait_ge(a_done, after(order(g) + 1))
                            pool.wait_ge(seg_done, after(q))
                            nc.gpsimd.tensor_tensor(
                                am[:, :, :, :],
                                tri16[:, :].unsqueeze(1).unsqueeze(1).to_broadcast([P, 2, H, P]),
                                al[:, g[1], :, c, :].unsqueeze(3).to_broadcast([P, 2, H, P]),
                                ALU.mult).then_inc(am_done, 1)

                        def group(g, front, ahead):
                            for c in range(CH):
                                q = CH * order(g) + c
                                if c == 0:
                                    taken(pool, g, w_dec(g))
                                pool.wait_ge(xtok_done, after(q + 1))
                                pool.wait_ge(y3_done, after(q))
                                nc.gpsimd.tensor_tensor(heads(dx[:, :]), heads(xtok[:, :]), over(head_d, HD), ALU.mult)\
                                  .then_inc(dx_done, 1)
                                pool.wait_ge(dtx_done, after(q + 1))
                                pool.wait_ge(dx_done, after(q + 1))
                                nc.gpsimd.tensor_tensor(heads(xtok[:, :]), heads(dtx[:, :]),
                                                        over(dec[:, g[1], 1, c, :], HD), ALU.mult).then_inc(dtxe_done, 1)
                                if c < CH - 1:
                                    masked(g, c + 1)
                                elif front is not None:
                                    masked(front, 0)
                                if c == 1 and ahead is not None:
                                    inv_std(ahead)

                        inv_std((0, 1))
                        masked((0, 0), 0)
                        all_groups(pool, group)

                    @block.scalar
                    def _(act):
                        start_counts(act, [*wide_free, pad_done, xc_done, exp_done, lx_done, xtok_done, ytc_done], done_before)

                        def copy_transposed(f, k):
                            bank, _ = wide_use(f, W_TR[k])
                            act.wait_ge(tr_done, after(KD * order(f) + k + 1))
                            nc.scalar.activation(xnt[:, k, :], wide[bank][:, :], ACT.Copy).then_inc(wide_free[bank], 1)

                        def high_parts(k0, k1):
                            act.wait_ge(z_in, after(CH * order(LAST) + CH))
                            for k in range(k0, k1):
                                act.wait_ge(tr_done, after(KD * order(BEHIND) + k + 1))
                                nc.scalar.activation(xhi[:, k, :], wide[wide_use(BEHIND, k)[0]][:, :], ACT.Copy, scale=XS)\
                                  .then_inc(xhi_done, 1)

                        def conv_start(f, i):
                            b, blk, n = f[1], CONV[i], NCONV * order(f) + i
                            bank, _ = wide_use(f, w_conv(f, i))
                            act.wait_ge(conv_in, after(n + 1))
                            act.wait_ge(tap_done, after((TAPS - 1) * n))
                            nc.scalar.activation(xpad[:, 0:TAPS - 1], hist[:, b, blk, :], ACT.Copy)
                            nc.scalar.activation(xpad[:, TAPS - 1:], wide[bank][:, :], ACT.Copy).then_inc(pad_done, 1)
                            act.wait_ge(pad_done, after(n + 1))
                            nc.scalar.activation(hist[:, b, blk, :], wide[bank][:, TG - TAPS + 1:], ACT.Copy)
                            nc.scalar.activation(xc[:, b, blk, :], wide[bank][:, :], ACT.Identity,
                                                 bias=cvb[:, blk:blk + 1], scale=cvw[:, blk, TAPS - 1:TAPS])\
                              .then_inc(wide_free[bank], 1)

                        def conv_end(f, i):
                            b, blk, n = f[1], CONV[i], NCONV * order(f) + i
                            act.wait_ge(tap_done, after((TAPS - 1) * (n + 1)))
                            nc.scalar.activation(xc[:, b, blk, :], xc[:, b, blk, :], ACT.Silu).then_inc(xc_done, 1)

                        def gate(f, c, g):
                            bank, _ = wide_use(f, w_z(f, c))
                            act.wait_ge(z_in, after(CH * order(f) + c + 1))
                            if g is not None:
                                act.wait_ge(y4_done, after(CH * order(g) + c + 1))
                            nc.scalar.activation(zs[:, c, :], wide[bank][:, :], ACT.Silu).then_inc(wide_free[bank], 1)

                        def softplus_exp(f):
                            act.wait_ge(abs_done, after(order(f) + 1))
                            nc.scalar.activation(sp_t[:, 1, :], sp_t[:, 0, :], ACT.Exp).then_inc(exp_done, 1)

                        def decays(f):
                            bank, _ = wide_use(f, w_dec(f))
                            act.wait_ge(dec_in, after(order(f) + 1))
                            nc.scalar.activation(dec[:, f[1], :, :, :].rearrange("p a c h -> p (a c h)"),
                                                 wide[bank][:, 0:3 * CH * H], ACT.Exp, scale=1.0 / AS)\
                              .then_inc(wide_free[bank], 1)

                        def group(g, front, ahead):
                            for c in range(CH):
                                q = CH * order(g) + c
                                if front is not None and c == 0:
                                    for k in range(KD):
                                        copy_transposed(front, k)
                                act.wait_ge(seg_done, after(q + 1))
                                act.wait_ge(y_done, after(q))
                                nc.scalar.activation(lx[:, :, :].rearrange("p h i -> p (h i)"), seg[:, :], ACT.Exp,
                                                     scale=1.0 / AS).then_inc(lx_done, 1)
                                if front is not None and c == 1:
                                    softplus_exp(front)
                                act.wait_ge(xt_done, after(q + 1))
                                act.wait_ge(st_done, after(q))
                                nc.scalar.activation(xtok[:, :], turn[:, :], ACT.Copy).then_inc(xtok_done, 1)
                                if front is not None:
                                    if c == 0:
                                        conv_start(front, 0)
                                    if c == 3:
                                        decays(front)
                                    conv_end(front, c)
                                    conv_start(front, c + 1)
                                    if c < CH - 1 and front is not LAST:
                                        gate(front, c, g)
                                if g is LAST:
                                    gate(g, c, (GB - 1, 0))
                                    if c == CH - 1:
                                        high_parts(0, KD // 2)
                                act.wait_ge(yt_done, after(q + 1))
                                act.wait_ge(out_done, after(q))
                                nc.scalar.activation(yt[:, :, :].rearrange("p k i -> p (k i)"), turn[:, :], ACT.Copy)\
                                  .then_inc(ytc_done, 1)
                                if g is LAST and c == CH - 1:
                                    high_parts(KD // 2, KD)
                                if front is not None and c == CH - 1:
                                    if front is not LAST:
                                        gate(front, c, g)
                                    conv_end(front, CH)

                        act.wait_ge(late_in, 16 * N_LATE)
                        nc.scalar.activation(a_exp[:, :], head_alog, ACT.Exp).then_inc(a_exp_done, 1)
                        act.wait_ge(set_done, 1)
                        for c in range(CH):
                            conv_start(FIRST, c)
                            if c == 1:
                                softplus_exp(FIRST)
                            if c == 2:
                                decays(FIRST)
                            if c < CH - 1:
                                gate(FIRST, c, None)
                            conv_end(FIRST, c)
                        conv_start(FIRST, CH)
                        gate(FIRST, CH - 1, None)
                        conv_end(FIRST, CH)
                        all_groups(act, group)

                    @block.vector
                    def _(dve):
                        start_counts(dve, [stat_done, mv_done, var_done, xn_done, tap_done, abs_done, sp_step, a_done, gm_done,
                                           btok_done, dtx_done, m_done, y1_done, y2_done, y3_done, y4_done, s1_done, s2_done,
                                           res_done], done_before)

                        def stats(f):
                            for c in range(CH):
                                nc.vector.bn_stats(stat[:, c, :], xt(tile(f, c))).then_inc(stat_done, 1)

                        def variance(f):
                            for c in range(CH):
                                last = nc.vector.bn_aggr(mv[:, c, :], stat[:, c, :])
                            last.then_inc(mv_done, 1)
                            dve.wait_ge(mv_done, after(order(f) + 1))
                            nc.vector.tensor_scalar(var[:, :], mv[:, :, 1], LN_EPS, None, ALU.add).then_inc(var_done, 1)

                        def normalize(f):
                            dve.wait_ge(rstd_done, after(order(f) + 1))
                            dve.wait_ge(tr_done, after(KD * order(f)))
                            for c in range(CH):
                                last = nc.vector.tensor_scalar(xn[:, c, :], xt(tile(f, c)), mv[:, c, 0:1],
                                                               rstd[:, c:c + 1], ALU.subtract, ALU.mult)
                            last.then_inc(xn_done, 1)

                        def low_parts(k0, k1):
                            for k in range(k0, k1):
                                bank, _ = wide_use(BEHIND, k)
                                dve.wait_ge(xhi_done, k + 1)
                                nc.vector.scalar_tensor_tensor(xlo[:, k, :], wide[bank][:, :], XS, xhi[:, k, :],
                                                               ALU.mult, ALU.subtract).then_inc(wide_free[bank], 1)

                        def taps(f, i):
                            b, blk, n = f[1], CONV[i], NCONV * order(f) + i
                            dve.wait_ge(pad_done, after(n + 1))
                            taken(dve, f, w_conv(f, i))
                            for t in range(TAPS - 1):
                                if t:
                                    dve.wait_ge(tap_done, after((TAPS - 1) * n + t))
                                nc.vector.scalar_tensor_tensor(xc[:, b, blk, :], xpad[:, t:t + TG], cvw[:, blk, t:t + 1],
                                                               xc[:, b, blk, :], ALU.mult, ALU.add).then_inc(tap_done, 1)

                        def softplus_start(f):
                            bank, _ = wide_use(f, w_dt(f))
                            dve.wait_ge(dt_in, after(order(f) + 1))
                            nc.vector.tensor_tensor(dtv[:, :].rearrange("p (c h) -> p c h", h=H),
                                                    wide[bank][:, 0:CH * H].rearrange("p (c h) -> p c h", h=H),
                                                    head_bias.unsqueeze(1).to_broadcast([P, CH, H]), ALU.add)\
                              .then_inc(wide_free[bank], 1)
                            taken(dve, f, w_dt(f))
                            nc.vector.scalar_tensor_tensor(sp_t[:, 0, :], dtv[:, :], -1.0, dtv[:, :], ALU.mult, ALU.min)\
                              .then_inc(abs_done, 1)

                        def softplus_end(f):
                            n = order(f)
                            count = [0]

                            def step(ins):
                                count[0] += 1
                                ins.then_inc(sp_step, 1)
                                dve.wait_ge(sp_step, after(SP_STEPS * n + count[0]))

                            v, u, r, s, s2, p = (sp_t[:, i, :] for i in (0, 1, 2, 3, 4, 5))
                            dve.wait_ge(exp_done, after(n + 1))
                            step(nc.vector.tensor_scalar(r, dtv[:, :], 0.0, None, ALU.max))
                            step(nc.vector.tensor_scalar(v, u, 2.0, None, ALU.add))
                            step(nc.vector.reciprocal(s2, v))
                            step(nc.vector.tensor_tensor(s, u, s2, ALU.mult))
                            step(nc.vector.tensor_tensor(s2, s, s, ALU.mult))
                            step(nc.vector.tensor_scalar(p, s2, 1.0 / 15, None, ALU.mult))
                            for odd in (13, 11, 9, 7, 5, 3):
                                step(nc.vector.scalar_tensor_tensor(p, p, 1.0 / odd, s2, ALU.add, ALU.mult))
                            step(nc.vector.scalar_tensor_tensor(p, p, 1.0, s, ALU.add, ALU.mult))
                            d = dt[:, f[1], :, :].rearrange("p c h -> p (c h)")
                            step(nc.vector.scalar_tensor_tensor(d, p, 2.0, r, ALU.mult, ALU.add))
                            step(nc.vector.tensor_tensor(a32.rearrange("p (c h) -> p c h", h=H), dt[:, f[1], :, :],
                                                         a_neg[:, :].unsqueeze(1).to_broadcast([P, CH, H]), ALU.mult))
                            step(nc.vector.tensor_scalar(a32, a32, A_MIN, AS, ALU.max, ALU.mult))
                            hi, lo = (al[:, f[1], i, :, :].rearrange("p c h -> p (c h)") for i in (0, 1))
                            step(nc.vector.tensor_copy(hi, a32))
                            assert count[0] == SP_STEPS
                            nc.vector.tensor_tensor(lo, a32, hi, ALU.subtract).then_inc(a_done, 1)

                        def residual(g, c):
                            q = CH * order(g) + c
                            dve.wait_ge(out_done, after(q + 1))
                            nc.vector.tensor_tensor(xt(tile(g, c)), xt(tile(g, c)), near[:, :], ALU.add)\
                              .then_inc(res_done, 1)

                        def group(g, front, ahead):
                            b = g[1]
                            for c in range(CH):
                                q = CH * order(g) + c
                                dve.wait_ge(bc_done, after(q + 1))
                                dve.wait_ge(m_done, after(q))
                                nc.vector.tensor_tensor(gm[:, :], bc[:, 0:P], tri[:, :], ALU.mult).then_inc(gm_done, 1)
                                dve.wait_ge(st_done, after(q))
                                nc.vector.tensor_copy(btok[:, :], bc[:, P:P + N]).then_inc(btok_done, 1)
                                dve.wait_ge(xtok_done, after(q + 1))
                                dve.wait_ge(dtxe_done, after(q))
                                if c == 0:
                                    dve.wait_ge(a_done, after(order(g) + 1))
                                nc.vector.tensor_tensor(heads(dtx[:, :]), heads(xtok[:, :]), over(dt[:, b, c, :], HD),
                                                        ALU.mult).then_inc(dtx_done, 1)
                                dve.wait_ge(lx_done, after(q + 1))
                                dve.wait_ge(gm_done, after(q + 1))
                                nc.vector.tensor_tensor(lx[:, :, :], lx[:, :, :],
                                                        gm[:, :].unsqueeze(1).to_broadcast([P, H, P]), ALU.mult)\
                                  .then_inc(m_done, 1)
                                if c:
                                    residual(g, c - 1)
                                if c == 0 and ahead is not None:
                                    stats(ahead)
                                if c == 0 and front is not None:
                                    softplus_start(front)
                                    taps(front, 0)
                                if c == 2 and front is not None:
                                    softplus_end(front)
                                if c == (2 if ahead is BEHIND else 3) and ahead is not None:
                                    normalize(ahead)
                                dve.wait_ge(y_done, after(q + 1))
                                dve.wait_ge(yt_done, after(q))
                                if c == 0:
                                    taken(dve, g, w_dec(g))
                                nc.vector.tensor_tensor(heads(yv[:, :]), heads(far[:, :]), over(dec[:, b, 0, c, :], HD),
                                                        ALU.mult).then_inc(y1_done, 1)
                                dve.wait_ge(y1_done, after(q + 1))
                                nc.vector.tensor_tensor(yv[:, :], yv[:, :], near[:, :], ALU.add).then_inc(y2_done, 1)
                                dve.wait_ge(y2_done, after(q + 1))
                                dve.wait_ge(dx_done, after(q + 1))
                                nc.vector.tensor_tensor(yv[:, :], yv[:, :], dx[:, :], ALU.add).then_inc(y3_done, 1)
                                dve.wait_ge(y3_done, after(q + 1))
                                taken(dve, g, w_z(g, c))
                                nc.vector.tensor_tensor(yv[:, :], yv[:, :], zs[:, c, :], ALU.mult).then_inc(y4_done, 1)
                                if g is LAST and c == CH - 1:
                                    low_parts(0, KD // 2)
                                if c == 1 and ahead is not None:
                                    dve.wait_ge(stat_done, after(CH * order(ahead) + CH))
                                dve.wait_ge(s2_done, after(q))
                                nc.vector.tensor_tensor(heads(state[b]), heads(state[b]), over(dec[0:N, b, 2, c, :], HD),
                                                        ALU.mult).then_inc(s1_done, 1)
                                if c == 1 and ahead is not None:
                                    variance(ahead)
                                dve.wait_ge(st_done, after(q + 1))
                                dve.wait_ge(s1_done, after(q + 1))
                                nc.vector.tensor_tensor(state[b], state[b], far[0:N, :], ALU.add).then_inc(s2_done, 1)
                                if front is not None:
                                    taps(front, c + 1)
                            if g is LAST:
                                low_parts(KD // 2, KD)
                            residual(g, CH - 1)

                        f1 = (0, 1)
                        stats(f1)
                        dve.wait_ge(late_in, 16 * N_LATE)
                        dve.wait_ge(a_exp_done, 1)
                        nc.vector.tensor_scalar(a_neg[:, :], a_exp[:, :], -1.0, None, ALU.mult).then_inc(a_neg_done, 1)
                        dve.wait_ge(stat_done, after(CH * order(f1) + CH))
                        variance(f1)
                        dve.wait_ge(a_neg_done, 1)
                        taps(FIRST, 0)
                        softplus_start(FIRST)
                        taps(FIRST, 1)
                        softplus_end(FIRST)
                        normalize(f1)
                        for c in range(1, CH):
                            taps(FIRST, c + 1)
                        dve.wait_ge(set_done, N_SET)
                        all_groups(dve, group)

                    @block.tensor
                    def _(pe):
                        def product(f, k):
                            bank, before = wide_use(f, k)
                            pe.wait_ge(wide_free[bank], after(before))
                            return wide[bank]

                        def transposes(f, k0, k1):
                            if k0 == 0:
                                pe.wait_ge(xn_done, after(order(f) + 1))
                            for k in range(k0, k1):
                                acc = product(f, W_TR[k])
                                for c in range(CH):
                                    last = nc.tensor.transpose(acc[:, cols(c)], xn[:, c, cols(k)], ident[:, :])
                                last.then_inc(tr_done, 1)

                        def project_conv(f, i, dt_behind=None):
                            if i == 0:
                                taken(pe, f, W_TR[2])
                                taken(pe, f, W_TR[3])
                            acc = product(f, w_conv(f, i))
                            row = D + CONV[i] * P
                            small = [(c, k) for c in range(CH) for k in range(KD)] if dt_behind else []
                            for k in range(KD):
                                last = nc.tensor.matmul(acc[:, :], win[:, k, row:row + P], xnt[:, k, :],
                                                        start=(k == 0), stop=(k == KD - 1))
                                if k == KD - 1:
                                    last.then_inc(conv_in, 1)
                                if dt_behind:
                                    if k == 0:
                                        acc_dt = product(f, w_dt(f))
                                    done = sum(dt_behind[:k])
                                    for c, n in small[done:done + dt_behind[k]]:
                                        last_dt = nc.tensor.matmul(acc_dt[:, c * H:(c + 1) * H], xnt[:, n, cols(c)],
                                                                   win[:, n, W_IN - H:W_IN], start=(n == 0), stop=(n == KD - 1))
                                    if done < len(small) == done + dt_behind[k]:
                                        last_dt.then_inc(dt_in, 1)

                        def project_z(f, c, k0=0, k1=KD):
                            acc = product(f, w_z(f, c)) if k0 == 0 else wide[wide_use(f, w_z(f, c))[0]]
                            for k in range(k0, k1):
                                last = nc.tensor.matmul(acc[:, :], xnt[:, k, cols(c)], win[:, k, 0:D],
                                                        start=(k == 0), stop=(k == KD - 1))
                            if k1 == KD:
                                last.then_inc(z_in, 1)

                        def sum_decays(f):
                            pe.wait_ge(a_done, after(order(f) + 1))
                            acc = product(f, w_dec(f))
                            for i, m in enumerate((tri16, after16, ones16)):
                                for part in range(2):
                                    last = nc.tensor.matmul(acc[:, i * CH * H:(i + 1) * CH * H], m[:, :],
                                                            al[:, f[1], part, :, :].rearrange("p c h -> p (c h)"),
                                                            start=(part == 0), stop=(part == 1))
                            last.then_inc(dec_in, 1)

                        def chunk_decays(g, c):
                            q, b = CH * order(g) + c, g[1]
                            pe.wait_ge(am_done, after(q + 1))
                            pe.wait_ge(lx_done, after(q))
                            for half in range(2):
                                for part in range(2):
                                    last = nc.tensor.matmul(seg[:, half * 512:(half + 1) * 512], after16[:, :],
                                                            am[:, part, 4 * half:4 * half + 4, :].rearrange("p h i -> p (h i)"),
                                                            start=(part == 0), stop=(part == 1))
                            last.then_inc(seg_done, 1)

                        def chunk_start(g, c):
                            q, b = CH * order(g) + c, g[1]
                            if c == 0:
                                pe.wait_ge(xc_done, after(NCONV * (order(g) + 1)))
                                pe.wait_ge(cc_in, 16 * (order(g) + 1))
                            pe.wait_ge(btok_done, after(q))
                            nc.tensor.matmul(bc[:, 0:P], xc[0:N, b, 4, cols(c)], cc[:, b, cols(c)], start=True, stop=True)
                            nc.tensor.transpose(bc[:, P:P + N], xc[0:N, b, 4, cols(c)], ident[0:N, 0:N]).then_inc(bc_done, 1)
                            pe.wait_ge(ytc_done, after(q))
                            for k in range(KD):
                                last = nc.tensor.transpose(turn[:, cols(k)], xc[:, b, k, cols(c)], ident[:, :])
                            last.then_inc(xt_done, 1)

                        def chunk_y(g, c):
                            q, b = CH * order(g) + c, g[1]
                            pe.wait_ge(s2_done, after(q))
                            nc.tensor.matmul(far[:, :], cc[:, b, cols(c)], state[b], start=True, stop=True)
                            pe.wait_ge(dtx_done, after(q + 1))
                            pe.wait_ge(m_done, after(q + 1))
                            pe.wait_ge(res_done, after(q))
                            for h in range(H):
                                last = nc.tensor.matmul(near[:, h * HD:(h + 1) * HD], lx[:, h, :],
                                                        dtx[:, h * HD:(h + 1) * HD], start=True, stop=True)
                            last.then_inc(y_done, 1)

                        def chunk_state(g, c):
                            q = CH * order(g) + c
                            pe.wait_ge(y1_done, after(q + 1))
                            pe.wait_ge(dtxe_done, after(q + 1))
                            pe.wait_ge(btok_done, after(q + 1))
                            nc.tensor.matmul(far[0:N, :], btok[:, :], xtok[:, :], start=True, stop=True).then_inc(st_done, 1)

                        def turn_y(g, c):
                            q = CH * order(g) + c
                            pe.wait_ge(y4_done, after(q + 1))
                            pe.wait_ge(xtok_done, after(q + 1))
                            for k in range(KD):
                                last = nc.tensor.transpose(turn[:, cols(k)], yv[:, cols(k)], ident[:, :])
                            last.then_inc(yt_done, 1)

                        def project_out(g, c):
                            q = CH * order(g) + c
                            pe.wait_ge(ytc_done, after(q + 1))
                            pe.wait_ge(y2_done, after(q + 1))
                            for k in range(KD):
                                last = nc.tensor.matmul(near[:, :], yt[:, k, :], wout[:, k, :],
                                                        start=(k == 0), stop=(k == KD - 1))
                            last.then_inc(out_done, 1)

                        def group(g, front, ahead):
                            for c in range(CH):
                                if front is not None and c == 0:
                                    transposes(front, 0, 2)
                                    chunk_decays(g, c)
                                    transposes(front, 2, 4)
                                else:
                                    chunk_decays(g, c)
                                chunk_start(g, c)
                                if c:
                                    project_out(g, c - 1)
                                if front is not None:
                                    if c == 0:
                                        project_conv(front, 0, (4, 4, 4, 4))
                                    if c == 3:
                                        sum_decays(front)
                                    if c and front is not LAST:
                                        project_conv(front, c + 1)
                                if g is LAST and c == 0:
                                    project_z(g, 0)
                                chunk_y(g, c)
                                if front is not None and (c == 0 or front is LAST):
                                    project_conv(front, c + 1)
                                if g is not LAST and front is not LAST:
                                    project_z(front, c, 0, KD if c < CH - 1 else KD - 1)
                                if g is LAST and c < CH - 1:
                                    project_z(g, c + 1, 0, KD // 2)
                                elif g is LAST:
                                    transposes(BEHIND, 0, KD // 2)
                                chunk_state(g, c)
                                if g is LAST and c < CH - 1:
                                    project_z(g, c + 1, KD // 2, KD)
                                turn_y(g, c)
                            if g is LAST:
                                transposes(BEHIND, KD // 2, KD)
                            if front is not None and front is not LAST:
                                project_z(front, CH - 1, KD - 1, KD)
                            project_out(g, CH - 1)

                        pe.wait_ge(late_in, 16 * N_LATE)
                        project_conv(FIRST, 0)
                        start_counts(pe, [tr_done, conv_in, dt_in, z_in, dec_in, seg_done, bc_done, xt_done, y_done, st_done,
                                          yt_done, out_done], done_before)
                        project_z(FIRST, 0)
                        project_conv(FIRST, 1, (4, 6, 6, 0))
                        project_z(FIRST, 1)
                        project_conv(FIRST, 2)
                        project_z(FIRST, 2, 0, KD // 2)
                        pe.wait_ge(set_done, N_SET)
                        sum_decays(FIRST)
                        project_z(FIRST, 2, KD // 2, KD)
                        project_conv(FIRST, 3)
                        project_conv(FIRST, 4)
                        project_z(FIRST, 3)
                        all_groups(pe, group)

        ffn_part("f1_", True)
        ssm_part()
        ffn_part("f2_", False)


def kernel(L0_attn_u, L0_attn_W_in, L0_attn_conv_w, L0_attn_conv_b, L0_attn_W_out, L0_attn_A_log, L0_attn_D_param,
           L0_attn_dt_bias, L0_ffn_W_up, L0_ffn_W_gate, L0_ffn_W_down):
    import numpy as np
    import concourse.bacc as bacc
    from concourse.bass_utils import run_bass_kernel_spmd

    def rows(w_t, blocks):
        n = w_t.shape[1]
        return np.ascontiguousarray(w_t.reshape(blocks, P, n).transpose(1, 0, 2).reshape(P, blocks * n))

    def quarters(w):
        v = np.asarray(w).T.reshape(KD, P, 4, E // 4).transpose(1, 2, 0, 3)
        return np.ascontiguousarray(v.reshape(P, KD * E))

    arrays = dict(
        u=np.ascontiguousarray(np.asarray(L0_attn_u).reshape(B * L, D)),
        w_up=quarters(L0_ffn_W_up),
        w_gate=quarters(L0_ffn_W_gate),
        w_down=rows(np.asarray(L0_ffn_W_down).T, KE),
        w_in=rows(np.asarray(L0_attn_W_in).T, KD),
        w_out=rows(np.asarray(L0_attn_W_out).T, KD),
        conv_w=rows(np.asarray(L0_attn_conv_w).reshape(NCONV * P, TAPS), NCONV),
        conv_b=rows(np.asarray(L0_attn_conv_b).reshape(NCONV * P, 1), NCONV),
        head_par=np.ascontiguousarray(np.tile(np.concatenate(
            [np.asarray(L0_attn_A_log), np.asarray(L0_attn_D_param), np.asarray(L0_attn_dt_bias)])[None, :], (P, 1))),
    )
    nc = bacc.Bacc("TRN2", target_bir_lowering=False, num_devices=1)
    args = [nc.dram_tensor("in_" + n, a.shape, mybir.dt.from_np(a.dtype), kind="ExternalInput").ap()
            for n, a in arrays.items()]
    res = nc.dram_tensor("res", (B * L, D), F32, kind="ExternalOutput").ap()
    macaron_kernel(nc, *args, res)
    r = run_bass_kernel_spmd(nc, [{"in_" + n: a for n, a in arrays.items()}], core_ids=[0])
    return r.results[0]["res"].reshape(B, L, D)
```

```python
from contextlib import ExitStack

import concourse.bass as bass
from concourse import mybir

F32 = mybir.dt.float32
F16 = mybir.dt.float16
F8 = mybir.dt.float8e4
ALU = mybir.AluOpType
ACT = mybir.ActivationFunctionType
AX = mybir.AxisListType

P = 128
B, L, D, E = 2, 2048, 512, 2048
H, N, HD = 8, 64, 64
KD, KE = D // P, E // P
TG = 512
CH = TG // P
NG = B * L // TG
GB = NG // B
NCONV = (D + 2 * N) // P
TAPS = 4
ZE = P - H
W_IN = 2 * D + 2 * N + H
LN_EPS, Q_EPS = 1e-5, 1e-8
XS = 2.0 ** 11
HS = 2.0 ** -5
HT, HE, HK = TG // 2, D // 2, KE // 2
AS = 2.0 ** 7
A_MIN = -200.0


def macaron_kernel(nc, u, w_up, w_gate, w_down, w_in, w_out, conv_w, conv_b, head_par, out):
    top = ExitStack()

    def sb(ctx, name, shape, dt=F32):
        return ctx.enter_context(nc.sbuf_tensor(name, shape, dt))

    def ps(ctx, name, shape, dt=F32):
        return ctx.enter_context(nc.psum_tensor(name, shape, dt))

    def sem(ctx, name):
        return ctx.enter_context(nc.semaphore(name))

    def sems(ctx, name, n):
        return [sem(ctx, f"{name}{i}") for i in range(n)]

    with top:
        x = sb(top, "x", [P, NG * CH * D])
        wu = sb(top, "wu", [P, KD, E], F8)
        wg = sb(top, "wg", [P, KD, E], F8)
        wd = sb(top, "wd", [P, 7, HK, HE], F8)
        xn = sb(top, "xn", [P, CH, D])
        xnh, xnl = (xn[:, a:a + CH // 2, :].rearrange("p c d -> p (c d)").bitcast(F16).rearrange("p (c d) -> p c d", c=CH)
                    for a in (0, CH // 2))
        xnt = sb(top, "xnt", [P, KD, TG])
        xtp = [xnt[:, a:a + KD // 2, :].rearrange("p k t -> p (k t)").bitcast(F16) for a in (0, KD // 2)]
        xhi, xlo = (v.rearrange("p (c k t) -> p k c t", c=CH, k=KD) for v in xtp)
        ident = sb(top, "ident", [P, P])
        neg_half = sb(top, "neg_half", [P, CH])
        silu_scale = sb(top, "silu_scale", [P, 1])
        hid_scale = sb(top, "hid_scale", [P, 1])
        tern_done = sem(top, "tern_done")
        out_scale = sb(top, "out_scale", [P, 1])

        late = sb(top, "late", [P, KD * E])
        late_in = sem(top, "late_in")
        bounds = [0]
        for n in (KD * W_IN, KD * D, NCONV * TAPS, NCONV, 3 * H, D, D, N, P, P, P // 2):
            bounds.append(bounds[-1] + n)
        parts = [late[:, a:b] for a, b in zip(bounds, bounds[1:])]
        win = parts[0].rearrange("p (k n) -> p k n", k=KD)
        wout = parts[1].rearrange("p (k n) -> p k n", k=KD)
        cvw = parts[2].rearrange("p (k n) -> p k n", k=NCONV)
        cvb = parts[3]
        head_alog, head_d, head_bias = (parts[4][:, i * H:(i + 1) * H] for i in range(3))
        behind = late[:, KD * E - 4 * HT:]
        state = [parts[5][0:N, :], parts[6][0:N, :]]
        late_loads = [(parts[0], w_in), (parts[1], w_out), (parts[2], conv_w), (parts[3], conv_b), (parts[4], head_par)]
        N_LATE = len(late_loads)

        def after(n):
            return n + 1

        def start_counts(eng, counting, head_start=()):
            ahead = dict(head_start)
            for s in counting:
                eng.sem_inc(s, 1 + ahead.get(s, 0))

        def xt(t):
            return x[:, bass.ds(t * D, D)]

        def by_tile(ap):
            return ap.rearrange("p (c t) -> p c t", c=CH)

        def ffn_part(tag, first):
            ctx = ExitStack()
            with ctx:
                h = sb(ctx, tag + "h", [P, 2, 4, HT])
                sums = behind.rearrange("p (s t) -> p s t", s=4)
                hhi = sb(ctx, tag + "hhi", [P, HK, 7, HT], F16)
                hlo = sb(ctx, tag + "hlo", [P, HK, 7, HT], F16)
                stat = sb(ctx, tag + "stat", [P, CH, 6])
                mv = sb(ctx, tag + "mv", [P, CH, 2])
                var = sb(ctx, tag + "var", [P, CH])
                rstd = sb(ctx, tag + "rstd", [P, CH])
                up_ps = [ps(ctx, f"{tag}up_ps{i}", [P, TG]) for i in range(2)]
                gate_ps = [ps(ctx, f"{tag}gate_ps{i}", [P, TG]) for i in range(2)]
                down_ps = ps(ctx, tag + "down_ps", [P, 4 * HE])
                tr_ps = [ps(ctx, f"{tag}tr_ps{i}", [P, TG]) for i in range(2)]

                stat_done = sem(ctx, tag + "stat_done")
                mv_done = sem(ctx, tag + "mv_done")
                var_done = sem(ctx, tag + "var_done")
                rstd_done = sem(ctx, tag + "rstd_done")
                norm_done = sem(ctx, tag + "norm_done")
                xnh_done = sem(ctx, tag + "xnh_done")
                xnl_done = sem(ctx, tag + "xnl_done")
                turned = sem(ctx, tag + "turned")
                ug_done = sem(ctx, tag + "ug_done")
                sil_done = sem(ctx, tag + "sil_done")
                hid_done = sems(ctx, tag + "hid_done", 2)
                sum_step = sem(ctx, tag + "sum_step")
                hhi_done = sem(ctx, tag + "hhi_done")
                hla_done = sems(ctx, tag + "hla_done", 2)
                hlo_done = sems(ctx, tag + "hlo_done", 2)
                down_done = sem(ctx, tag + "down_done")
                res_done = sem(ctx, tag + "res_done")
                sp_free = sem(ctx, tag + "sp_free")
                pe_free = sem(ctx, tag + "pe_free")
                if first:
                    ones = sb(ctx, "ones", [P, P])
                    raw_u = x[:, 16 * D:32 * D]
                    flat_hi, flat_lo = (v[:, :, :, :].rearrange("p k s t -> p (k s t)") for v in (hhi, hlo))
                    raw_d = [flat_lo[:, 5 * 7 * HT:5 * 7 * HT + 4096].bitcast(F32), xn[:, :, :].rearrange("p c d -> p (c d)"),
                             x[:, 8 * D:12 * D], x[:, 12 * D:16 * D]]
                    masks = [flat_hi[:, 49 * HT:49 * HT + 1024], flat_lo[:, 51 * HT:51 * HT + 1024]]
                    b12 = late[:, 4736:4736 + HK * HE // 4].bitcast(F8).rearrange("p (k d) -> p k d", k=HK)
                    raw_g = late[:, :]
                    wsum = sb(ctx, "wsum", [P, 3, 4])
                    total = sb(ctx, "total", [P, 3])
                    scale = sb(ctx, "scale", [P, 3])
                    half = sb(ctx, "half", [P, 3])
                    nhalf = sb(ctx, "nhalf", [P, 3])
                    rscale = sb(ctx, "rscale", [P, 1])
                    prod = sb(ctx, "prod", [P, 2])
                    const_done = sem(ctx, "const_done")
                    xn_done = sem(ctx, "xn_done")
                    tr_done = sem(ctx, "tr_done")
                    xhi_done = sem(ctx, "xhi_done")
                    xlo_done = sems(ctx, "xlo_done", 2)
                    raw_in = sems(ctx, "raw_in", 12)
                    x_in = sem(ctx, "x_in")
                    abs_done = sem(ctx, "abs_done")
                    up_done = sem(ctx, "up_done")
                    sum_done = sem(ctx, "sum_done")
                    sc_done = sem(ctx, "sc_done")
                    mask_done = sem(ctx, "mask_done")
                    t_done = sem(ctx, "t_done")
                else:
                    x_out = sem(ctx, "x_out")

                done_before = ((norm_done, CH), (xnh_done, CH), (xnl_done, CH), (turned, 32))
                if not first:
                    done_before += ((stat_done, CH), (mv_done, 1), (var_done, 1), (rstd_done, 1))

                u_v = u.rearrange("(t p) d -> p t d", p=P)
                out_v = out.rearrange("(t p) d -> p t d", p=P)
                x_v = x[:, :].rearrange("p (t d) -> p t d", d=D)
                raws = [(w_up, 0), (w_gate, 1), (w_down, 2)]

                def raw_q(w, q):
                    if w == 2:
                        return raw_d[q]
                    at = q if w == 0 else 3 - q
                    return (raw_u, raw_g)[w][:, at * 2048:(at + 1) * 2048]

                TERNARY = ([(0, q, n, n + 256) for q in (0, 2) for n in (0, 256)]
                           + [(1, q, 0, P) for q in (0, 2)]
                           + [(1, 0, P, 256), (1, 2, P, 256), (1, 0, 256, 512), (1, 2, 256, 512)]
                           + [(w, q, n, n + 256) for n in (0, 256) for q in (1, 3) for w in (0, 1)]
                           + [(2, q, n, n + HE) for q in range(4) for n in (0, HE)])
                N_TERN, T_EARLY, T_AFTER = len(TERNARY), 8, (1, 1, 1, 1, 1, 1, 1, 1, 2, 1, 2, 1, 2, 1, 1, 0)
                AT_DOWN = [n for n, piece in enumerate(TERNARY) if piece[0] == 2]

                def block_of(i):
                    return i // 2 + HK * (i % 2)

                def halves(i, buf):
                    return h[:, buf, 0:4:3, :] if i % 2 == 0 else h[:, buf, 1:3, :]

                def two(ap):
                    return ap.rearrange("p (a t) -> p a t", a=2)

                PRODUCT = dict(P1=(0, 0, ((0, 0), (0, 1), (1, 0), (1, 1))), P2=(1, 1, ((0, 0),)), P3=(2, 6, ((0, 1),)),
                               P4=(3, 2, ((1, 0),)), P5=(4, 3, ((0, 1), (1, 1))), P6=(5, 4, ((0, 1), (1, 0), (1, 1))),
                               P7=(6, 5, ((1, 0), (1, 1))))
                ORDER = ("P2", "P1", "P3", "P5", "P7", "P6", "P4")
                T_ORDER = ("P5", "P7", "P6", "P4")
                STEPS = [sum(len(PRODUCT[name][2]) for name in ORDER[:j + 1]) for j in range(7)]

                def down_at(g, name):
                    return after(7 * g + 1 + ORDER.index(name))

                def res_at(g, k):
                    return after(STEPS[-1] * g + k)

                BANK = (0, 1, 2, 0, 1, 0, 1)

                def bank(name):
                    n = BANK[ORDER.index(name)]
                    return up_ps[0][:, :] if n == 2 else down_ps[:, D * n:D * (n + 1)]

                def bank_sum(w):
                    return down_ps[:, D * (w % 2):D * (w % 2) + 4]

                def at_first(p):
                    return 3 if p < HK - 1 else 2

                def pair_sums(eng, ops, g, p):
                    n = 4 * (HK * g + p)
                    A11, A12, A22, A21 = (h[:, p % 2, k, :] for k in range(4))
                    S1, S2, S3, S4 = (sums[:, k, :] for k in range(4))
                    for half in range(2):
                        eng.wait_ge(hid_done[half], after(HK * g + p + 1))
                    if p:
                        eng.wait_ge(hlo_done[(p - 1) % 2], after(HK // 2 * g + (p - 1) // 2 + 1))
                    else:
                        eng.wait_ge(hlo_done[1], after(HK // 2 * g))
                        if first:
                            eng.wait_ge(tern_done, 1 + max(n for n, v in enumerate(TERNARY) if v[:2] == (1, 0)))
                    ops.tensor_tensor(S1, A21, A22, ALU.add).then_inc(sum_step, 1)
                    ops.tensor_tensor(S3, A11, A21, ALU.subtract).then_inc(sum_step, 1)
                    eng.wait_ge(sum_step, after(n + 1))
                    ops.tensor_tensor(S2, S1, A11, ALU.subtract).then_inc(sum_step, 1)
                    eng.wait_ge(sum_step, after(n + 3))
                    ops.tensor_tensor(S4, A12, S2, ALU.subtract).then_inc(sum_step, 1)

                with nc.Block() as block:

                    @block.sync
                    def _(sp):
                        start_counts(sp, [turned], done_before)

                        def turn(g):
                            sp.wait_ge(xnh_done, after(CH * g + CH))
                            sp.wait_ge(xnl_done, after(CH * g + CH))
                            sp.wait_ge(ug_done, after(KE * g))
                            sp.sem_inc(sp_free, 1)
                            for dst, src in zip(xtp, (xnh, xnl)):
                                sp.dma_start_transpose(dst.rearrange("p (n t) -> p n t", t=P),
                                                       src.rearrange("p c d -> p (c d)")).then_inc(turned, 16)

                        if first:
                            def load_x(g):
                                sp.dma_start(x_v[:, CH * g:CH * g + CH, :],
                                             u_v[:, CH * g:CH * g + CH, :]).then_inc(x_in, 16)

                            load_x(0)
                            for w in (0, 1, 2):
                                for q in range(4):
                                    if (w, q) == (2, 1):
                                        sp.wait_ge(tr_done, after(KD))
                                    sp.dma_start(raw_q(w, q), raws[w][0][:, q * 2048:(q + 1) * 2048])\
                                      .then_inc(raw_in[4 * w + q], 16)
                            for g in range(1, NG):
                                sp.wait_ge(x_in, 16 * g)
                                if g == 2:
                                    turn(1)
                                    sp.wait_ge(tern_done, N_TERN)
                                    sp.wait_ge(t_done, 4)
                                    for dst, src in late_loads:
                                        sp.dma_start(dst, src[:, :]).then_inc(late_in, 16)
                                load_x(g)
                            sp.wait_ge(x_in, 16 * NG)
                            with sp.Fori(2, NG) as g:
                                turn(g)
                        else:
                            def store(g):
                                sp.wait_ge(res_done, res_at(g, STEPS[-1]))
                                sp.dma_start(out_v[:, bass.ds(CH * g, CH), :],
                                             x_v[:, bass.ds(CH * g, CH), :]).then_inc(x_out, 16)

                            with sp.Fori(0, NG - 1) as g:
                                turn(g + 1)
                                store(g)
                            store(NG - 1)
                            sp.wait_ge(x_out, 16 * NG)

                    @block.gpsimd
                    def _(pool):
                        start_counts(pool, [rstd_done, *hla_done, *hlo_done] + [sum_step] * first, done_before)
                        if first:
                            nc.gpsimd.memset(ones[:, :], 1.0).then_inc(const_done, 1)
                            nc.gpsimd.memset(neg_half[:, :], -0.5).then_inc(const_done, 1)
                            pool.wait_ge(const_done, 1)
                            nc.gpsimd.affine_select(out=ident[:, :], in_=ones[:, :], compare_op=ALU.is_equal, fill=0.0,
                                                    base=0, pattern=[[-1, P]], channel_multiplier=1)\
                              .then_inc(const_done, 1)
                            pool.wait_ge(const_done, 3)

                        def inv_std(g):
                            pool.wait_ge(var_done, after(g + 1))
                            nc.gpsimd.tensor_tensor(rstd[:, :], var[:, :], neg_half[:, :], ALU.pow)\
                              .then_inc(rstd_done, 1)

                        def low_parts(g, p, part):
                            pool.wait_ge(hhi_done, after(2 * (HK * g + p) + part + 1))
                            n = at_first(p)
                            mine, rest = h[:, p % 2, 0:n, :], h[:, p % 2, n:3, :]
                            for a, b, src in (((0, n, mine),), ((n, 3, rest), (3, 7, sums)))[part]:
                                if a < b:
                                    last = nc.gpsimd.tensor_tensor(hlo[:, p, a:b, :], src, hhi[:, p, a:b, :], ALU.subtract)
                            last.then_inc((hla_done, hlo_done)[part][p % 2], 1)

                        def t_sums():
                            B11, B21, B22, T4, T1, T2, T3 = (wd[:, i, :, :] for i in range(7))
                            pool.wait_ge(tern_done, N_TERN)
                            for dst, a, b in ((T1, b12, B11), (T3, B22, b12), (T2, B22, T1), (T4, B21, T2)):
                                if dst is T4 or dst is T2:
                                    pool.wait_ge(t_done, 3 if dst is T4 else 1)
                                nc.gpsimd.tensor_tensor(dst, a, b, ALU.subtract, saturate=False).then_inc(t_done, 1)

                        def group(g, more_ln, between=None):
                            for p in range(HK):
                                if first and p == 5:
                                    pool.wait_ge(tern_done, 2 + AT_DOWN[0])
                                if first and p == HK - 1:
                                    pool.wait_ge(tern_done, N_TERN)
                                if between is not None and p < HK - 1:
                                    pair_sums(pool, nc.gpsimd, g, p)
                                low_parts(g, p, 0)
                                low_parts(g, p, 1)
                                if between is not None:
                                    between(p)
                                if p == 3 and more_ln:
                                    inv_std(g + 1)

                        if first:
                            inv_std(0)
                            group(0, True, lambda p: t_sums() if p == HK - 1 else None)
                        with pool.Fori(1 if first else 0, NG - 1) as g:
                            group(g, True)
                        group(NG - 1, first)

                    @block.scalar
                    def _(act):
                        start_counts(act, [xnh_done, sil_done, hhi_done] + ([xhi_done] if first else []), done_before)

                        def abs_sum(w, q):
                            at = (q if w < 2 else 3) * 2048
                            act.wait_ge(raw_in[4 * w + q], 16)
                            if w:
                                act.wait_ge(abs_done, 4 * (w - 1) + q + 1 if w < 2 else 4 * w + q)
                            nc.scalar.activation(flat_hi[:, at:at + 2048], raw_q(w, q), ACT.Abs,
                                                 accum_out=wsum[:, w, q:q + 1]).then_inc(abs_done, 1)

                        def high_part(k):
                            act.wait_ge(tr_done, after(k + 1))
                            nc.scalar.activation(xhi[:, k], by_tile(tr_ps[k % 2][:, :]), ACT.Copy, scale=XS)\
                              .then_inc(xhi_done, 1)

                        def copy_transposed(k):
                            act.wait_ge(tr_done, after(KD + k + 1))
                            nc.scalar.activation(xnt[:, k, :], tr_ps[k % 2][:, :], ACT.Copy).then_inc(xlo_done[k % 2], 1)

                        def high_rows(g, c0, c1):
                            for c in range(c0, c1):
                                if c == 0:
                                    act.wait_ge(turned, after(32 * g))
                                    if first and isinstance(g, int):
                                        act.wait_ge(tern_done, 1 + AT_DOWN[3])
                                act.wait_ge(norm_done, after(CH * g + c + 1))
                                nc.scalar.activation(xnh[:, c, :], tr_ps[c % 2][:, :], ACT.Copy, scale=XS).then_inc(xnh_done, 1)

                        def silu(g, i):
                            if first and i < 2 and isinstance(g, int) and g == 0:
                                act.wait_ge(up_done, i + 1)
                            else:
                                act.wait_ge(ug_done, after(KE * g + i + 1))
                            act.wait_ge(hlo_done[i // 2 % 2], after(HK // 2 * g + i // 4))
                            nc.scalar.activation(halves(i, i // 2 % 2), two(up_ps[i % 2][:, :]), ACT.Silu,
                                                 scale=silu_scale[:, 0:1]).then_inc(sil_done, 1)

                        if first:
                            for w in range(2):
                                for q in range(4):
                                    if w == 0 and q >= 2:
                                        for k in range(2 * q - 4, 2 * q - 2):
                                            high_part(k)
                                    if (w, q) == (1, 3):
                                        silu(0, 0)
                                    abs_sum(w, q)

                        def hid_high(g, p):
                            if first and p == 3:
                                act.wait_ge(abs_done, 12)
                            if first and p == HK - 1:
                                act.wait_ge(tern_done, N_TERN)
                            for half in range(2):
                                act.wait_ge(hid_done[half], after(HK * g + p + 1))
                            n = at_first(p)
                            nc.scalar.activation(hhi[:, p, 0:n, :], h[:, p % 2, 0:n, :], ACT.Copy).then_inc(hhi_done, 1)
                            if n < 3:
                                nc.scalar.activation(hhi[:, p, n:3, :], h[:, p % 2, n:3, :], ACT.Copy)

                        def sums_high(g, p):
                            act.wait_ge(sum_step, after(4 * (HK * g + p) + 4))
                            nc.scalar.activation(hhi[:, p, 3:7, :], sums, ACT.Copy).then_inc(hhi_done, 1)

                        def group(g, more, between=None):
                            for i in range(KE):
                                if between is None or i:
                                    silu(g, i)
                                if between is not None:
                                    between(i)
                                if i and i % 2 == 0:
                                    hid_high(g, i // 2 - 1)
                                    sums_high(g, i // 2 - 1)
                                if more and between is None and i in (11, 13):
                                    high_rows(g + 1, i - 11, i - 9)
                            hid_high(g, HK - 1)
                            sums_high(g, HK - 1)
                            if between is not None:
                                high_rows(g + 1, 0, CH)
                            if first and not more:
                                for k in range(KD):
                                    copy_transposed(k)

                        if first:
                            def w_down_sums(e):
                                if 1 <= e <= 4:
                                    abs_sum(2, e - 1)

                            group(0, True, w_down_sums)
                        with act.Fori(1 if first else 0, NG - 1) as g:
                            group(g, True)
                        group(NG - 1, False)

                    @block.vector
                    def _(dve):
                        start_counts(dve, [*hid_done, stat_done, mv_done, var_done, norm_done, xnl_done, res_done]
                                     + ([*xlo_done, xn_done] if first else [])
                                     + [sum_step] * (not first), done_before)

                        def tile(g, c):
                            return CH * (0 if isinstance(g, int) and g == NG else g) + c

                        def stats(g, c):
                            nc.vector.bn_stats(stat[:, c, :], xt(tile(g, c))).then_inc(stat_done, 1)

                        def variance(g):
                            for c in range(CH):
                                last = nc.vector.bn_aggr(mv[:, c, :], stat[:, c, :])
                            last.then_inc(mv_done, 1)
                            dve.wait_ge(mv_done, after(g + 1))
                            nc.vector.tensor_scalar(var[:, :], mv[:, :, 1], LN_EPS, None, ALU.add)\
                              .then_inc(var_done, 1)

                        def normalize(g, c0, c1, dst, signal):
                            dve.wait_ge(rstd_done, after(g + 1))
                            for c in range(c0, c1):
                                if signal is norm_done:
                                    dve.wait_ge(xnl_done, after(CH * g - 1 + c))
                                last = nc.vector.tensor_scalar(dst(c), xt(tile(g, c)), mv[:, c, 0:1],
                                                               rstd[:, c:c + 1], ALU.subtract, ALU.mult)
                                if signal is norm_done:
                                    last.then_inc(norm_done, 1)
                            if signal is not norm_done and c1 == CH:
                                last.then_inc(signal, 1)

                        def normalize_rows(g, c0, c1):
                            if c0 == 0 and first:
                                dve.wait_ge(xlo_done[0], after(KD // 2))
                                dve.wait_ge(xlo_done[1], after(KD // 2))
                            normalize(g, c0, c1, lambda c: tr_ps[c % 2][:, :], norm_done)

                        def low_rows(g, c0, c1):
                            for c in range(c0, c1):
                                dve.wait_ge(xnh_done, after(CH * g + c + 1))
                                nc.vector.scalar_tensor_tensor(xnl[:, c, :], tr_ps[c % 2][:, :], XS, xnh[:, c, :],
                                                               ALU.mult, ALU.subtract).then_inc(xnl_done, 1)

                        def low_part(k):
                            dve.wait_ge(xhi_done, after(k + 1))
                            nc.vector.scalar_tensor_tensor(xlo[:, k], by_tile(tr_ps[k % 2][:, :]), XS, xhi[:, k],
                                                           ALU.mult, ALU.subtract).then_inc(xlo_done[k % 2], 1)

                        def hidden(g, i, stats_of=None):
                            if stats_of is not None:
                                dve.wait_ge(stat_done, after(CH * stats_of + CH))
                            dve.wait_ge(sil_done, after(KE * g + i + 1))
                            if first and i < 2 and isinstance(g, int) and g == 0:
                                dve.wait_ge(ug_done, after(i + 1))
                            at = halves(i, i // 2 % 2)
                            nc.vector.scalar_tensor_tensor(at, at, hid_scale[:, 0:1], two(gate_ps[i % 2][:, :]),
                                                           ALU.mult, ALU.mult).then_inc(hid_done[i % 2], 1)

                        def add_product(g, name):
                            j = ORDER.index(name)
                            dve.wait_ge(down_done, down_at(g, name))
                            for n, (row, column) in enumerate(PRODUCT[name][2]):
                                if n == 0 and j:
                                    dve.wait_ge(res_done, res_at(g, STEPS[j - 1]))
                                dst = x_v[:, bass.ds(CH * g + 2 * row, 2), HE * column:HE * (column + 1)]
                                src = bank(name).rearrange("p (m d) -> p m d", m=2)
                                nc.vector.scalar_tensor_tensor(dst, src, out_scale[:, 0:1], dst, ALU.mult, ALU.add)\
                                  .then_inc(res_done, 1)

                        def group(g, more, between=None):
                            more_ln = more or first
                            for i in range(KE):
                                hidden(g, i, g + 1 if more_ln and i == 8 else None)
                                if i % 2 and (between is None or i == KE - 1):
                                    pair_sums(dve, nc.vector, g, i // 2)
                                if between is not None:
                                    between(i)
                                if more_ln:
                                    if i == 4 and first and more:
                                        dve.wait_ge(x_in, 16 * g + 32)
                                    if i in (4, 6):
                                        stats(g + 1, i - 4)
                                        stats(g + 1, i - 3)
                                    if i == 8:
                                        variance(g + 1)
                                    if more and between is None:
                                        if i in (10, 12):
                                            if i == 12:
                                                low_rows(g + 1, 0, 2)
                                            normalize_rows(g + 1, i - 10, i - 8)
                                        if i == 14:
                                            low_rows(g + 1, 2, 4)
                                    if not more and i in (12, 14):
                                        if i == 12:
                                            dve.wait_ge(turned, after(32 * NG))
                                        normalize(g + 1, i - 12, i - 10, lambda c: xn[:, c, :], xn_done)
                            for name in ORDER:
                                add_product(g, name)
                                if between is not None and name in ("P1", "P3"):
                                    c = 0 if name == "P1" else 2
                                    normalize_rows(g + 1, c, c + 2)
                                    low_rows(g + 1, c, c + 2)

                        if first:
                            dve.wait_ge(x_in, 16)
                            for c in range(CH):
                                stats(0, c)
                            dve.wait_ge(stat_done, after(CH))
                            variance(0)
                            normalize(0, 0, CH, lambda c: xn[:, c, :], xn_done)

                        steps = [0]

                        def step(ins):
                            steps[0] += 1
                            ins.then_inc(sc_done, 1)
                            dve.wait_ge(sc_done, steps[0])

                        def weight_scale(w):
                            dve.wait_ge(sum_done, w + 1)
                            step(nc.vector.tensor_reduce(total[:, w:w + 1], bank_sum(w), AX.X, ALU.add))
                            step(nc.vector.tensor_scalar(scale[:, w:w + 1], total[:, w:w + 1], 1.0 / (D * E), Q_EPS,
                                                         ALU.mult, ALU.add))
                            step(nc.vector.tensor_scalar(half[:, w:w + 1], scale[:, w:w + 1], 0.5, None, ALU.mult))
                            step(nc.vector.tensor_scalar(nhalf[:, w:w + 1], scale[:, w:w + 1], -0.5, None, ALU.mult))

                        def ternary(n):
                            w, q, e0, e1 = TERNARY[n]
                            src = raw_q(w, q).rearrange("p (k e) -> p k e", k=4)[:, :, e0:e1]
                            if w < 2:
                                dst = (wu, wg)[w][:, :, q * 512 + e0:q * 512 + e1]
                            elif (q // 2, e0) == (0, HE):
                                dst = b12[:, 4 * q:4 * q + 4, :]
                            else:
                                dst = wd[:, {(0, 0): 0, (1, 0): 1, (1, HE): 2}[q // 2, e0], 4 * (q % 2):4 * (q % 2) + 4, :]
                            m = masks[n % 2][:, 0:4 * (e1 - e0)].rearrange("p (k e) -> p k e", k=4)
                            if w == 2 and (q, e0) == (0, HE):
                                dve.wait_ge(tern_done, n)
                            nc.vector.tensor_scalar(m, src, nhalf[:, w:w + 1], None, ALU.is_lt).then_inc(mask_done, 1)
                            dve.wait_ge(mask_done, n + 1)
                            nc.vector.scalar_tensor_tensor(dst, src, half[:, w:w + 1], m, ALU.is_gt, ALU.subtract,
                                                           saturate=False)\
                              .then_inc(tern_done, 1)

                        def last_weights(e):
                            if e == 6:
                                weight_scale(2)
                                step(nc.vector.tensor_tensor(prod[:, 0:1], scale[:, 0:1], scale[:, 1:2], ALU.mult))
                                step(nc.vector.tensor_tensor(prod[:, 1:2], prod[:, 0:1], scale[:, 2:3], ALU.mult))
                                step(nc.vector.tensor_scalar(out_scale[:, :], prod[:, 1:2], 0.5 / HS, None, ALU.mult))
                            done = T_EARLY + sum(T_AFTER[:e])
                            for n in range(done, done + T_AFTER[e]):
                                ternary(n)

                        if first:
                            for k in range(KD):
                                low_part(k)
                            weight_scale(0)
                            step(nc.vector.tensor_scalar(silu_scale[:, :], scale[:, 0:1], 1.0 / XS, None, ALU.mult))
                            step(nc.vector.reciprocal(rscale[:, :], scale[:, 0:1]))
                            step(nc.vector.tensor_scalar(hid_scale[:, :], rscale[:, :], HS / XS, None, ALU.mult))
                            for n in range(T_EARLY):
                                if n == 4:
                                    weight_scale(1)
                                ternary(n)
                            group(0, True, last_weights)
                        with dve.Fori(1 if first else 0, NG - 1) as g:
                            group(g, True)
                        group(NG - 1, False)

                    @block.tensor
                    def _(pe):
                        start_counts(pe, [ug_done, down_done] + ([tr_done] if first else []), done_before)

                        def transposes(n, k):
                            if k == 0:
                                pe.wait_ge(xn_done, after(n + 1))
                                if n:
                                    pe.wait_ge(xnl_done, after(CH * NG))
                            pe.wait_ge(xlo_done[k % 2], after(2 * n + k // 2))
                            for c in range(CH):
                                last = nc.tensor.transpose(tr_ps[k % 2][:, c * P:(c + 1) * P],
                                                           xn[:, c, k * P:(k + 1) * P], ident[:, :])
                            last.then_inc(tr_done, 1)

                        def up_gate(g, i):
                            if i == 0:
                                pe.wait_ge(turned, after(32 * (g + 1)))
                            pe.wait_ge(hid_done[i % 2], after(HK * g + i // 2))
                            pe.sem_inc(pe_free, 1)
                            up_or_gate(i, 0)
                            up_or_gate(i, 1).then_inc(ug_done, 1)

                        def up_or_gate(i, which):
                            e, w, acc = block_of(i), (wu, wg)[which], (up_ps, gate_ps)[which][i % 2]
                            if first:
                                pe.wait_ge(tern_done, 1 + max(n for n, (v, q, e0, e1) in enumerate(TERNARY)
                                                              if v == which and q == e // 4 and e0 <= e % 4 * P < e1))
                            for k in range(KD):
                                for part in (xhi, xlo):
                                    last = nc.tensor.matmul(acc[:, :], w[:, k, e * P:(e + 1) * P], part[:, k],
                                                            start=(k == 0 and part is xhi),
                                                            stop=(k == KD - 1 and part is xlo))
                            return last

                        def product(g, name, m, p0=0, p1=HK):
                            weight, kind, _ = PRODUCT[name]
                            j = ORDER.index(name)
                            if m == 0 and p0 == 0:
                                if BANK[j] == 2:
                                    pe.wait_ge(hid_done[0], after(HK * (g + 1)))
                                else:
                                    before = [k for k in range(j) if BANK[k] == BANK[j]]
                                    pe.wait_ge(res_done, res_at(g, STEPS[before[-1]] if before else 0))
                            if m == 0 and name == "P2":
                                for p in range(p0, p1):
                                    pe.wait_ge(hla_done[p % 2], after(HK // 2 * g + p // 2 + 1))
                            if m == 0 and name == "P3":
                                for p in range(max(p0, p1 - 2), p1):
                                    pe.wait_ge(hlo_done[p % 2], after(HK // 2 * g + p // 2 + 1))
                            pe.sem_inc(pe_free, 1)
                            if first and m == 0 and p0 == 0:
                                pe.wait_ge(tern_done, N_TERN)
                                if name in T_ORDER:
                                    pe.wait_ge(t_done, 1 + T_ORDER.index(name))
                            at = bank(name)[:, m * HE:(m + 1) * HE]
                            for p in range(p0, p1):
                                for part in (hhi, hlo):
                                    last = nc.tensor.matmul(at, part[:, p, kind, m * P:(m + 1) * P], wd[:, weight, p, :],
                                                            start=(p == 0 and part is hhi),
                                                            stop=(p == HK - 1 and part is hlo))
                            if m == 1:
                                last.then_inc(down_done, 1)

                        def group(g, more, between=None):
                            leave = first and not more
                            for i in range(KE):
                                if between is None or i > 3:
                                    up_gate(g, i)
                                if between is not None:
                                    between(i)
                            product(g, "P2", 0, 0, HK - 1)
                            product(g, "P1", 0, 0, HK - 1)
                            product(g, "P3", 0, 0, HK - 1)
                            if leave:
                                transposes(1, 0)
                                transposes(1, 1)
                            for name in ORDER[0:3]:
                                product(g, name, 0, HK - 1, HK)
                                product(g, name, 1)
                            if leave:
                                transposes(1, 2)
                                transposes(1, 3)
                            for name in ORDER[3:]:
                                product(g, name, 0)
                                product(g, name, 1)

                        if first:
                            pe.wait_ge(const_done, 3)

                            def weight_sum(w):
                                pe.wait_ge(abs_done, 4 * w + 4)
                                if w == 2:
                                    pe.wait_ge(sc_done, 1)
                                nc.tensor.matmul(bank_sum(w), ones[:, :], wsum[:, w, :], start=True, stop=True)\
                                  .then_inc(sum_done, 1)

                            def last_sum(i):
                                if i == 1:
                                    for half in range(2):
                                        pe.wait_ge(xlo_done[half], after(KD // 2))
                                    for k in range(2):
                                        up_or_gate(k, 0).then_inc(up_done, 1)
                                    for k in range(2):
                                        pe.wait_ge(sil_done, after(k + 1))
                                        up_or_gate(k + 2, 0)
                                        if k == 0:
                                            weight_sum(1)
                                    for k in range(2):
                                        up_or_gate(k, 1).then_inc(ug_done, 1)
                                if i in (2, 3):
                                    pe.wait_ge(hid_done[i % 2], after(1))
                                    up_or_gate(i, 1).then_inc(ug_done, 1)
                                if i == 5:
                                    weight_sum(2)

                            for k in range(KD):
                                transposes(0, k)
                            weight_sum(0)
                            group(0, True, last_sum)
                        with pe.Fori(1 if first else 0, NG - 1) as g:
                            group(g, True)
                        group(NG - 1, False)

        def ssm_part():
            ctx = ExitStack()
            with ctx:
                xpad = sb(ctx, "s_xpad", [P, TAPS - 1 + TG])
                hist = sb(ctx, "s_hist", [P, B, NCONV, TAPS - 1])
                xc = sb(ctx, "s_xc", [P, B, NCONV, TG])
                cc = sb(ctx, "s_cc", [N, B, TG])
                ze = sb(ctx, "s_ze", [P, B, CH, ZE])
                zs = sb(ctx, "s_zs", [P, CH, D - ZE])
                dtv = sb(ctx, "s_dtv", [P, CH * H])
                sp_t = sb(ctx, "s_sp", [P, 7, CH * H])
                dt = sb(ctx, "s_dt", [P, B, CH, H])
                a32 = sp_t[:, 6, :]
                al = sb(ctx, "s_al", [P, B, 2, CH, H], F16)
                dec = sb(ctx, "s_dec", [P, B, 3, CH, H])
                am = sb(ctx, "s_am", [P, 2, H, P], F16)
                lx = sb(ctx, "s_lx", [P, H, P])
                btok = parts[7]
                gm = parts[8]
                xtok = sb(ctx, "s_xtok", [P, D])
                dtx = sb(ctx, "s_dtx", [P, D])
                dx = sb(ctx, "s_dx", [P, D])
                yv = sb(ctx, "s_yv", [P, D])
                yt = sb(ctx, "s_yt", [P, KD, P])
                stat = sb(ctx, "s_stat", [P, CH, 6])
                mv = sb(ctx, "s_mv", [P, CH, 2])
                var = sb(ctx, "s_var", [P, CH])
                rstd = sb(ctx, "s_rstd", [P, CH])
                a_neg = sb(ctx, "s_a_neg", [P, H])
                a_exp = sb(ctx, "s_a_exp", [P, H])
                tri = parts[9]
                tri16 = sb(ctx, "s_tri16", [P, P], F16)
                after16 = sb(ctx, "s_after16", [P, P], F16)
                ones16 = parts[10].bitcast(F16)

                wide = [ps(ctx, f"s_wide{i}", [P, 512]) for i in range(2)]
                seg = ps(ctx, "s_seg", [P, H * P])
                turn = ps(ctx, "s_turn", [P, D])
                bc = ps(ctx, "s_bc", [P, P + N])
                near = ps(ctx, "s_near", [P, D])
                far = ps(ctx, "s_far", [P, D])

                stat_done = sem(ctx, "s_stat_done")
                mv_done = sem(ctx, "s_mv_done")
                var_done = sem(ctx, "s_var_done")
                rstd_done = sem(ctx, "s_rstd_done")
                xn_done = sem(ctx, "s_xn_done")
                wide_free = sems(ctx, "s_wide_free", 2)
                tr_done = sem(ctx, "s_tr_done")
                conv_in = sem(ctx, "s_conv_in")
                dt_in = sem(ctx, "s_dt_in")
                dtv_done = sem(ctx, "s_dtv_done")
                z_in = sem(ctx, "s_z_in")
                dec_in = sem(ctx, "s_dec_in")
                pad_done = sem(ctx, "s_pad_done")
                tap_done = sem(ctx, "s_tap_done")
                xhi_done = sem(ctx, "s_xhi_done")
                xc_done = sem(ctx, "s_xc_done")
                cc_in = sem(ctx, "s_cc_in")
                bias_done = sem(ctx, "s_bias_done")
                abs_done = sem(ctx, "s_abs_done")
                exp_done = sem(ctx, "s_exp_done")
                sp_step = sem(ctx, "s_sp_step")
                a_done = sem(ctx, "s_a_done")
                am_done = sem(ctx, "s_am_done")
                seg_done = sem(ctx, "s_seg_done")
                bc_done = sem(ctx, "s_bc_done")
                xt_done = sem(ctx, "s_xt_done")
                y_done = sem(ctx, "s_y_done")
                st_done = sem(ctx, "s_st_done")
                yt_done = sem(ctx, "s_yt_done")
                out_done = sem(ctx, "s_out_done")
                lx_done = sem(ctx, "s_lx_done")
                xtok_done = sem(ctx, "s_xtok_done")
                ytc_done = sem(ctx, "s_ytc_done")
                gm_done = sem(ctx, "s_gm_done")
                btok_done = sem(ctx, "s_btok_done")
                dtx_done = sem(ctx, "s_dtx_done")
                m_done = sem(ctx, "s_m_done")
                y1_done = sem(ctx, "s_y1_done")
                y2_done = sem(ctx, "s_y2_done")
                y3_done = sem(ctx, "s_y3_done")
                y4_done = sem(ctx, "s_y4_done")
                s1_done = sem(ctx, "s_s1_done")
                s2_done = sem(ctx, "s_s2_done")
                res_done = sem(ctx, "s_res_done")
                dx_done = sem(ctx, "s_dx_done")
                dtxe_done = sem(ctx, "s_dtxe_done")
                set_done = sem(ctx, "s_set_done")
                a_exp_done = sem(ctx, "s_a_exp_done")
                a_neg_done = sem(ctx, "s_a_neg_done")

                done_before = ((stat_done, CH), (mv_done, 1), (var_done, 1), (rstd_done, 1), (xn_done, 1), (tr_done, KD),
                               *((s, KD // 2) for s in wide_free))

                N_SET = 8
                W_TR, W_CONV0, W_DT, W_ALL = (0, 1, 2, 3), 4, 5, 15
                CONV = (4, 0, 1, 2, 3)
                FIRST, LAST, BEHIND = (0, 0), (GB - 1, 1), (GB, 0)

                def w_conv(f, i):
                    others = (6, 7, 8, 10) if f is LAST else (6, 8, 12, 13) if f is FIRST else (6, 8, 10, 13)
                    return (W_CONV0, *others)[i]

                def w_z(f, c):
                    return ((11, 12, 13, 14) if f is LAST else (7, 9, 11, 14))[c]

                def w_dec(f):
                    return 9 if f is LAST else 10 if f is FIRST else 12

                SP_STEPS = 17

                def order(g):
                    return 2 * g[0] + g[1]

                def follower(g):
                    return (g[0], 1) if g[1] == 0 else (g[0] + 1, 0)

                def tile(g, c):
                    return c if g is BEHIND else GB * CH * g[1] + CH * g[0] + c

                def wide_use(g, k):
                    j, b = g
                    return (W_ALL * b + k) % 2, W_ALL * j + (W_ALL * b + k) // 2

                def taken(eng, g, k):
                    bank, before = wide_use(g, k)
                    eng.wait_ge(wide_free[bank], after(before + 1))

                def cols(c):
                    return slice(c * P, (c + 1) * P)

                def heads(ap):
                    return ap.rearrange("p (h n) -> p h n", h=H)

                def over(ap, n):
                    return ap.unsqueeze(2).to_broadcast([ap.shape[0], H, n])

                def all_groups(eng, group):
                    with eng.Fori(0, GB - 1) as j:
                        for b in range(B):
                            group((j, b), follower((j, b)), (j + 1, b))
                    group((GB - 1, 0), LAST, None)
                    group(LAST, None, BEHIND)

                with nc.Block() as block:

                    @block.sync
                    def _(sp):
                        def move_c(f):
                            n = order(f)
                            sp.wait_ge(xc_done, after(NCONV * n + 1))
                            sp.dma_start(cc[:, f[1], :], xc[N:2 * N, f[1], 4, :]).then_inc(cc_in, 16)

                        move_c((0, 0))

                        def group(g, front, ahead):
                            if front is not None:
                                move_c(front)

                        all_groups(sp, group)
                        sp.wait_ge(cc_in, 16 * NG)

                    @block.gpsimd
                    def _(pool):
                        start_counts(pool, [rstd_done, am_done, dx_done, dtxe_done], done_before)

                        def mask(out, src, base, step, mult):
                            return nc.gpsimd.affine_select(out=out, in_=src, compare_op=ALU.is_ge, fill=0.0, base=base,
                                                           pattern=[[step, P]], channel_multiplier=mult)

                        nc.gpsimd.memset(hist[:, :, :, :], 0.0).then_inc(set_done, 1)
                        nc.gpsimd.memset(ones16[:, :], 1.0).then_inc(set_done, 1)
                        nc.gpsimd.memset(state[0], 0.0).then_inc(set_done, 1)
                        nc.gpsimd.memset(state[1], 0.0).then_inc(set_done, 1)
                        nc.gpsimd.memset(tri[:, :], 1.0).then_inc(set_done, 1)
                        pool.wait_ge(set_done, 5)
                        mask(tri[:, :], tri[:, :], 0, 1, -1).then_inc(set_done, 1)
                        mask(tri16[:, :], ones16[:, :], 0, 1, -1).then_inc(set_done, 1)
                        mask(after16[:, :], ones16[:, :], -1, -1, 1).then_inc(set_done, 1)
                        pool.wait_ge(set_done, N_SET)

                        def inv_std(f):
                            pool.wait_ge(var_done, after(order(f) + 1))
                            nc.gpsimd.tensor_tensor(rstd[:, :], var[:, :], neg_half[:, :], ALU.pow).then_inc(rstd_done, 1)

                        def masked(g, c):
                            q = CH * order(g) + c
                            if c == 0:
                                pool.wait_ge(a_done, after(order(g) + 1))
                            pool.wait_ge(seg_done, after(q))
                            nc.gpsimd.tensor_tensor(
                                am[:, :, :, :],
                                tri16[:, :].unsqueeze(1).unsqueeze(1).to_broadcast([P, 2, H, P]),
                                al[:, g[1], :, c, :].unsqueeze(3).to_broadcast([P, 2, H, P]),
                                ALU.mult).then_inc(am_done, 1)

                        def group(g, front, ahead):
                            for c in range(CH):
                                q = CH * order(g) + c
                                if c == 0:
                                    taken(pool, g, w_dec(g))
                                pool.wait_ge(xtok_done, after(q + 1))
                                pool.wait_ge(y3_done, after(q))
                                nc.gpsimd.tensor_tensor(heads(dx[:, :]), heads(xtok[:, :]), over(head_d, HD), ALU.mult)\
                                  .then_inc(dx_done, 1)
                                pool.wait_ge(dtx_done, after(q + 1))
                                pool.wait_ge(dx_done, after(q + 1))
                                nc.gpsimd.tensor_tensor(heads(xtok[:, :]), heads(dtx[:, :]),
                                                        over(dec[:, g[1], 1, c, :], HD), ALU.mult).then_inc(dtxe_done, 1)
                                if c < CH - 1:
                                    masked(g, c + 1)
                                elif front is not None:
                                    masked(front, 0)
                                if c == 1 and ahead is not None:
                                    inv_std(ahead)

                        inv_std((0, 1))
                        masked((0, 0), 0)
                        all_groups(pool, group)

                    @block.scalar
                    def _(act):
                        start_counts(act, [*wide_free, pad_done, xc_done, exp_done, lx_done, xtok_done, ytc_done, dtv_done],
                                     done_before)

                        def copy_transposed(f, k):
                            bank, _ = wide_use(f, W_TR[k])
                            act.wait_ge(tr_done, after(KD * order(f) + k + 1))
                            nc.scalar.activation(xnt[:, k, :], wide[bank][:, :], ACT.Copy).then_inc(wide_free[bank], 1)

                        def high_parts(k0, k1):
                            act.wait_ge(z_in, after(CH * order(LAST) + CH))
                            for k in range(k0, k1):
                                act.wait_ge(tr_done, after(KD * order(BEHIND) + k + 1))
                                bank, _ = wide_use(BEHIND, W_TR[k])
                                nc.scalar.activation(xhi[:, k], by_tile(wide[bank][:, :]), ACT.Copy, scale=XS)\
                                  .then_inc(xhi_done, 1)

                        def conv_start(f, i):
                            b, blk, n = f[1], CONV[i], NCONV * order(f) + i
                            bank, _ = wide_use(f, w_conv(f, i))
                            act.wait_ge(conv_in, after(n + 1))
                            act.wait_ge(tap_done, after((TAPS - 1) * n))
                            nc.scalar.activation(xpad[:, 0:TAPS - 1], hist[:, b, blk, :], ACT.Copy)
                            nc.scalar.activation(xpad[:, TAPS - 1:], wide[bank][:, :], ACT.Copy).then_inc(pad_done, 1)
                            act.wait_ge(pad_done, after(n + 1))
                            nc.scalar.activation(hist[:, b, blk, :], wide[bank][:, TG - TAPS + 1:], ACT.Copy)
                            nc.scalar.activation(xc[:, b, blk, :], wide[bank][:, :], ACT.Identity,
                                                 bias=cvb[:, blk:blk + 1], scale=cvw[:, blk, TAPS - 1:TAPS])\
                              .then_inc(wide_free[bank], 1)

                        def conv_end(f, i):
                            b, blk, n = f[1], CONV[i], NCONV * order(f) + i
                            act.wait_ge(tap_done, after((TAPS - 1) * (n + 1)))
                            nc.scalar.activation(xc[:, b, blk, :], xc[:, b, blk, :], ACT.Silu).then_inc(xc_done, 1)

                        def gate(f, c, g):
                            bank, _ = wide_use(f, w_z(f, c))
                            act.wait_ge(z_in, after(CH * order(f) + c + 1))
                            if g is not None:
                                act.wait_ge(y4_done, after(CH * order(g) + c + 1))
                            nc.scalar.activation(zs[:, c, :], wide[bank][:, 0:D - ZE], ACT.Silu).then_inc(wide_free[bank], 1)

                        def dt_and_z(f):
                            return wide[wide_use(f, W_DT)[0]][:, :].rearrange("p (c n) -> p c n", c=CH)

                        def copy_dt(f):
                            act.wait_ge(dt_in, after(order(f) + 1))
                            act.wait_ge(a_done, after(order(f)))
                            nc.scalar.activation(dtv[:, :].rearrange("p (c h) -> p c h", h=H), dt_and_z(f)[:, :, 0:H],
                                                 ACT.Copy).then_inc(dtv_done, 1)

                        def gate_early(f, g):
                            if g is not None:
                                act.wait_ge(y4_done, after(CH * order(g)))
                            nc.scalar.activation(ze[:, f[1], :, :], dt_and_z(f)[:, :, H:], ACT.Silu)\
                              .then_inc(wide_free[wide_use(f, W_DT)[0]], 1)

                        def softplus_exp(f):
                            act.wait_ge(abs_done, after(order(f) + 1))
                            nc.scalar.activation(sp_t[:, 1, :], sp_t[:, 0, :], ACT.Exp).then_inc(exp_done, 1)

                        def decays(f):
                            bank, _ = wide_use(f, w_dec(f))
                            act.wait_ge(dec_in, after(order(f) + 1))
                            nc.scalar.activation(dec[:, f[1], :, :, :].rearrange("p a c h -> p (a c h)"),
                                                 wide[bank][:, 0:3 * CH * H], ACT.Exp, scale=1.0 / AS)\
                              .then_inc(wide_free[bank], 1)

                        def group(g, front, ahead):
                            for c in range(CH):
                                q = CH * order(g) + c
                                if front is not None and c == 0:
                                    for k in range(KD):
                                        copy_transposed(front, k)
                                act.wait_ge(seg_done, after(q + 1))
                                act.wait_ge(y_done, after(q))
                                nc.scalar.activation(lx[:, :, :].rearrange("p h i -> p (h i)"), seg[:, :], ACT.Exp,
                                                     scale=1.0 / AS).then_inc(lx_done, 1)
                                if front is not None and c == 1:
                                    softplus_exp(front)
                                act.wait_ge(xt_done, after(q + 1))
                                act.wait_ge(st_done, after(q))
                                nc.scalar.activation(xtok[:, :], turn[:, :], ACT.Copy).then_inc(xtok_done, 1)
                                if front is not None:
                                    if c == 0:
                                        conv_start(front, 0)
                                    if c == 3:
                                        decays(front)
                                    conv_end(front, c)
                                    if c == 0:
                                        copy_dt(front)
                                        gate_early(front, g)
                                    conv_start(front, c + 1)
                                    if c < CH - 1 and front is not LAST:
                                        gate(front, c, g)
                                if g is LAST:
                                    gate(g, c, (GB - 1, 0))
                                    if c == CH - 1:
                                        high_parts(0, KD // 2)
                                act.wait_ge(yt_done, after(q + 1))
                                act.wait_ge(out_done, after(q))
                                nc.scalar.activation(yt[:, :, :].rearrange("p k i -> p (k i)"), turn[:, :], ACT.Copy)\
                                  .then_inc(ytc_done, 1)
                                if g is LAST and c == CH - 1:
                                    high_parts(KD // 2, KD)
                                if front is not None and c == CH - 1:
                                    if front is not LAST:
                                        gate(front, c, g)
                                    conv_end(front, CH)

                        act.wait_ge(late_in, 16 * N_LATE)
                        nc.scalar.activation(a_exp[:, :], head_alog, ACT.Exp).then_inc(a_exp_done, 1)
                        act.wait_ge(set_done, 1)
                        conv_start(FIRST, 0)
                        copy_dt(FIRST)
                        softplus_exp(FIRST)
                        gate_early(FIRST, None)
                        conv_end(FIRST, 0)
                        conv_start(FIRST, 1)
                        gate(FIRST, 0, None)
                        conv_end(FIRST, 1)
                        conv_start(FIRST, 2)
                        gate(FIRST, 1, None)
                        decays(FIRST)
                        conv_end(FIRST, 2)
                        gate(FIRST, 2, None)
                        conv_start(FIRST, 3)
                        conv_end(FIRST, 3)
                        conv_start(FIRST, 4)
                        gate(FIRST, 3, None)
                        conv_end(FIRST, 4)
                        all_groups(act, group)

                    @block.vector
                    def _(dve):
                        start_counts(dve, [stat_done, mv_done, var_done, xn_done, tap_done, bias_done, abs_done, sp_step,
                                           a_done, gm_done, btok_done, dtx_done, m_done, y1_done, y2_done, y3_done, y4_done,
                                           s1_done, s2_done, res_done], done_before)

                        def stats(f):
                            for c in range(CH):
                                nc.vector.bn_stats(stat[:, c, :], xt(tile(f, c))).then_inc(stat_done, 1)

                        def variance(f):
                            for c in range(CH):
                                last = nc.vector.bn_aggr(mv[:, c, :], stat[:, c, :])
                            last.then_inc(mv_done, 1)
                            dve.wait_ge(mv_done, after(order(f) + 1))
                            nc.vector.tensor_scalar(var[:, :], mv[:, :, 1], LN_EPS, None, ALU.add).then_inc(var_done, 1)

                        def normalize(f):
                            dve.wait_ge(rstd_done, after(order(f) + 1))
                            dve.wait_ge(tr_done, after(KD * order(f)))
                            for c in range(CH):
                                last = nc.vector.tensor_scalar(xn[:, c, :], xt(tile(f, c)), mv[:, c, 0:1],
                                                               rstd[:, c:c + 1], ALU.subtract, ALU.mult)
                            last.then_inc(xn_done, 1)

                        def low_parts(k0, k1):
                            for k in range(k0, k1):
                                bank, _ = wide_use(BEHIND, W_TR[k])
                                dve.wait_ge(xhi_done, k + 1)
                                nc.vector.scalar_tensor_tensor(xlo[:, k], by_tile(wide[bank][:, :]), XS, xhi[:, k],
                                                               ALU.mult, ALU.subtract).then_inc(wide_free[bank], 1)

                        def taps(f, i):
                            b, blk, n = f[1], CONV[i], NCONV * order(f) + i
                            dve.wait_ge(pad_done, after(n + 1))
                            taken(dve, f, w_conv(f, i))
                            for t in range(TAPS - 1):
                                if t:
                                    dve.wait_ge(tap_done, after((TAPS - 1) * n + t))
                                nc.vector.scalar_tensor_tensor(xc[:, b, blk, :], xpad[:, t:t + TG], cvw[:, blk, t:t + 1],
                                                               xc[:, b, blk, :], ALU.mult, ALU.add).then_inc(tap_done, 1)

                        def softplus_start(f):
                            dve.wait_ge(dtv_done, after(order(f) + 1))
                            at = dtv[:, :].rearrange("p (c h) -> p c h", h=H)
                            nc.vector.tensor_tensor(at, at, head_bias.unsqueeze(1).to_broadcast([P, CH, H]), ALU.add)\
                              .then_inc(bias_done, 1)
                            dve.wait_ge(bias_done, after(order(f) + 1))
                            nc.vector.scalar_tensor_tensor(sp_t[:, 0, :], dtv[:, :], -1.0, dtv[:, :], ALU.mult, ALU.min)\
                              .then_inc(abs_done, 1)

                        def softplus_end(f):
                            n = order(f)
                            count = [0]

                            def step(ins):
                                count[0] += 1
                                ins.then_inc(sp_step, 1)
                                dve.wait_ge(sp_step, after(SP_STEPS * n + count[0]))

                            v, u, r, s, s2, p = (sp_t[:, i, :] for i in (0, 1, 2, 3, 4, 5))
                            dve.wait_ge(exp_done, after(n + 1))
                            step(nc.vector.tensor_scalar(r, dtv[:, :], 0.0, None, ALU.max))
                            step(nc.vector.tensor_scalar(v, u, 2.0, None, ALU.add))
                            step(nc.vector.reciprocal(s2, v))
                            step(nc.vector.tensor_tensor(s, u, s2, ALU.mult))
                            step(nc.vector.tensor_tensor(s2, s, s, ALU.mult))
                            step(nc.vector.tensor_scalar(p, s2, 1.0 / 15, None, ALU.mult))
                            for odd in (13, 11, 9, 7, 5, 3):
                                step(nc.vector.scalar_tensor_tensor(p, p, 1.0 / odd, s2, ALU.add, ALU.mult))
                            step(nc.vector.scalar_tensor_tensor(p, p, 1.0, s, ALU.add, ALU.mult))
                            d = dt[:, f[1], :, :].rearrange("p c h -> p (c h)")
                            step(nc.vector.scalar_tensor_tensor(d, p, 2.0, r, ALU.mult, ALU.add))
                            step(nc.vector.tensor_tensor(a32.rearrange("p (c h) -> p c h", h=H), dt[:, f[1], :, :],
                                                         a_neg[:, :].unsqueeze(1).to_broadcast([P, CH, H]), ALU.mult))
                            step(nc.vector.tensor_scalar(a32, a32, A_MIN, AS, ALU.max, ALU.mult))
                            hi, lo = (al[:, f[1], i, :, :].rearrange("p c h -> p (c h)") for i in (0, 1))
                            step(nc.vector.tensor_copy(hi, a32))
                            assert count[0] == SP_STEPS
                            nc.vector.tensor_tensor(lo, a32, hi, ALU.subtract).then_inc(a_done, 1)

                        def residual(g, c):
                            q = CH * order(g) + c
                            dve.wait_ge(out_done, after(q + 1))
                            nc.vector.tensor_tensor(xt(tile(g, c)), xt(tile(g, c)), near[:, :], ALU.add)\
                              .then_inc(res_done, 1)

                        def group(g, front, ahead):
                            b = g[1]
                            for c in range(CH):
                                q = CH * order(g) + c
                                dve.wait_ge(bc_done, after(q + 1))
                                dve.wait_ge(m_done, after(q))
                                nc.vector.tensor_tensor(gm[:, :], bc[:, 0:P], tri[:, :], ALU.mult).then_inc(gm_done, 1)
                                dve.wait_ge(st_done, after(q))
                                nc.vector.tensor_copy(btok[:, :], bc[:, P:P + N]).then_inc(btok_done, 1)
                                dve.wait_ge(xtok_done, after(q + 1))
                                dve.wait_ge(dtxe_done, after(q))
                                if c == 0:
                                    dve.wait_ge(a_done, after(order(g) + 1))
                                nc.vector.tensor_tensor(heads(dtx[:, :]), heads(xtok[:, :]), over(dt[:, b, c, :], HD),
                                                        ALU.mult).then_inc(dtx_done, 1)
                                dve.wait_ge(lx_done, after(q + 1))
                                dve.wait_ge(gm_done, after(q + 1))
                                nc.vector.tensor_tensor(lx[:, :, :], lx[:, :, :],
                                                        gm[:, :].unsqueeze(1).to_broadcast([P, H, P]), ALU.mult)\
                                  .then_inc(m_done, 1)
                                if c:
                                    residual(g, c - 1)
                                if c == 0 and ahead is not None:
                                    stats(ahead)
                                if c == 0 and front is not None:
                                    taps(front, 0)
                                    softplus_start(front)
                                if c == 2 and front is not None:
                                    softplus_end(front)
                                if c == (2 if ahead is BEHIND else 3) and ahead is not None:
                                    normalize(ahead)
                                dve.wait_ge(y_done, after(q + 1))
                                dve.wait_ge(yt_done, after(q))
                                if c == 0:
                                    taken(dve, g, w_dec(g))
                                nc.vector.tensor_tensor(heads(yv[:, :]), heads(far[:, :]), over(dec[:, b, 0, c, :], HD),
                                                        ALU.mult).then_inc(y1_done, 1)
                                dve.wait_ge(y1_done, after(q + 1))
                                nc.vector.tensor_tensor(yv[:, :], yv[:, :], near[:, :], ALU.add).then_inc(y2_done, 1)
                                dve.wait_ge(y2_done, after(q + 1))
                                dve.wait_ge(dx_done, after(q + 1))
                                nc.vector.tensor_tensor(yv[:, :], yv[:, :], dx[:, :], ALU.add).then_inc(y3_done, 1)
                                dve.wait_ge(y3_done, after(q + 1))
                                taken(dve, g, w_z(g, c))
                                nc.vector.tensor_tensor(yv[:, 0:ZE], yv[:, 0:ZE], ze[:, b, c, :], ALU.mult)
                                nc.vector.tensor_tensor(yv[:, ZE:], yv[:, ZE:], zs[:, c, :], ALU.mult).then_inc(y4_done, 1)
                                if g is LAST and c == CH - 1:
                                    low_parts(0, KD // 2)
                                if c == 1 and ahead is not None:
                                    dve.wait_ge(stat_done, after(CH * order(ahead) + CH))
                                dve.wait_ge(s2_done, after(q))
                                nc.vector.tensor_tensor(heads(state[b]), heads(state[b]), over(dec[0:N, b, 2, c, :], HD),
                                                        ALU.mult).then_inc(s1_done, 1)
                                if c == 1 and ahead is not None:
                                    variance(ahead)
                                dve.wait_ge(st_done, after(q + 1))
                                dve.wait_ge(s1_done, after(q + 1))
                                nc.vector.tensor_tensor(state[b], state[b], far[0:N, :], ALU.add).then_inc(s2_done, 1)
                                if front is not None:
                                    taps(front, c + 1)
                            if g is LAST:
                                low_parts(KD // 2, KD)
                            residual(g, CH - 1)

                        f1 = (0, 1)
                        stats(f1)
                        dve.wait_ge(late_in, 16 * N_LATE)
                        dve.wait_ge(a_exp_done, 1)
                        nc.vector.tensor_scalar(a_neg[:, :], a_exp[:, :], -1.0, None, ALU.mult).then_inc(a_neg_done, 1)
                        dve.wait_ge(stat_done, after(CH * order(f1) + CH))
                        variance(f1)
                        dve.wait_ge(a_neg_done, 1)
                        taps(FIRST, 0)
                        softplus_start(FIRST)
                        taps(FIRST, 1)
                        softplus_end(FIRST)
                        taps(FIRST, 2)
                        normalize(f1)
                        taps(FIRST, 3)
                        taps(FIRST, 4)
                        dve.wait_ge(set_done, N_SET)
                        all_groups(dve, group)

                    @block.tensor
                    def _(pe):
                        def product(f, k):
                            bank, before = wide_use(f, k)
                            pe.wait_ge(wide_free[bank], after(before))
                            return wide[bank]

                        def transposes(f, k0, k1):
                            if k0 == 0:
                                pe.wait_ge(xn_done, after(order(f) + 1))
                            for k in range(k0, k1):
                                acc = product(f, W_TR[k])
                                for c in range(CH):
                                    last = nc.tensor.transpose(acc[:, cols(c)], xn[:, c, cols(k)], ident[:, :])
                                last.then_inc(tr_done, 1)

                        def project_conv(f, i):
                            if i == 0:
                                taken(pe, f, W_TR[2])
                                taken(pe, f, W_TR[3])
                            acc = product(f, w_conv(f, i))
                            row = H + D + CONV[i] * P
                            for k in range(KD):
                                last = nc.tensor.matmul(acc[:, :], win[:, k, row:row + P], xnt[:, k, :],
                                                        start=(k == 0), stop=(k == KD - 1))
                            last.then_inc(conv_in, 1)

                        def project_dt(f):
                            acc = product(f, W_DT)
                            for c in range(CH):
                                for k in range(KD):
                                    last = nc.tensor.matmul(acc[:, cols(c)], xnt[:, k, cols(c)], win[:, k, 0:P],
                                                            start=(k == 0), stop=(k == KD - 1))
                            last.then_inc(dt_in, 1)

                        def project_z(f, c, k0=0, k1=KD):
                            acc = product(f, w_z(f, c)) if k0 == 0 else wide[wide_use(f, w_z(f, c))[0]]
                            for k in range(k0, k1):
                                last = nc.tensor.matmul(acc[:, 0:D - ZE], xnt[:, k, cols(c)], win[:, k, P:H + D],
                                                        start=(k == 0), stop=(k == KD - 1))
                            if k1 == KD:
                                last.then_inc(z_in, 1)

                        def sum_decays(f):
                            pe.wait_ge(a_done, after(order(f) + 1))
                            acc = product(f, w_dec(f))
                            for i, m in enumerate((tri16, after16, ones16)):
                                for part in range(2):
                                    last = nc.tensor.matmul(acc[:, i * CH * H:(i + 1) * CH * H], m[:, :],
                                                            al[:, f[1], part, :, :].rearrange("p c h -> p (c h)"),
                                                            start=(part == 0), stop=(part == 1))
                            last.then_inc(dec_in, 1)

                        def chunk_decays(g, c):
                            q, b = CH * order(g) + c, g[1]
                            pe.wait_ge(am_done, after(q + 1))
                            pe.wait_ge(lx_done, after(q))
                            for half in range(2):
                                for part in range(2):
                                    last = nc.tensor.matmul(seg[:, half * 512:(half + 1) * 512], after16[:, :],
                                                            am[:, part, 4 * half:4 * half + 4, :].rearrange("p h i -> p (h i)"),
                                                            start=(part == 0), stop=(part == 1))
                            last.then_inc(seg_done, 1)

                        def chunk_start(g, c):
                            q, b = CH * order(g) + c, g[1]
                            if c == 0:
                                pe.wait_ge(xc_done, after(NCONV * (order(g) + 1)))
                                pe.wait_ge(cc_in, 16 * (order(g) + 1))
                            pe.wait_ge(btok_done, after(q))
                            nc.tensor.matmul(bc[:, 0:P], xc[0:N, b, 4, cols(c)], cc[:, b, cols(c)], start=True, stop=True)
                            nc.tensor.transpose(bc[:, P:P + N], xc[0:N, b, 4, cols(c)], ident[0:N, 0:N]).then_inc(bc_done, 1)
                            pe.wait_ge(ytc_done, after(q))
                            for k in range(KD):
                                last = nc.tensor.transpose(turn[:, cols(k)], xc[:, b, k, cols(c)], ident[:, :])
                            last.then_inc(xt_done, 1)

                        def chunk_y(g, c):
                            q, b = CH * order(g) + c, g[1]
                            pe.wait_ge(s2_done, after(q))
                            nc.tensor.matmul(far[:, :], cc[:, b, cols(c)], state[b], start=True, stop=True)
                            pe.wait_ge(dtx_done, after(q + 1))
                            pe.wait_ge(m_done, after(q + 1))
                            pe.wait_ge(res_done, after(q))
                            for h in range(H):
                                last = nc.tensor.matmul(near[:, h * HD:(h + 1) * HD], lx[:, h, :],
                                                        dtx[:, h * HD:(h + 1) * HD], start=True, stop=True)
                            last.then_inc(y_done, 1)

                        def chunk_state(g, c):
                            q = CH * order(g) + c
                            pe.wait_ge(y1_done, after(q + 1))
                            pe.wait_ge(dtxe_done, after(q + 1))
                            pe.wait_ge(btok_done, after(q + 1))
                            nc.tensor.matmul(far[0:N, :], btok[:, :], xtok[:, :], start=True, stop=True).then_inc(st_done, 1)

                        def turn_y(g, c):
                            q = CH * order(g) + c
                            pe.wait_ge(y4_done, after(q + 1))
                            pe.wait_ge(xtok_done, after(q + 1))
                            for k in range(KD):
                                last = nc.tensor.transpose(turn[:, cols(k)], yv[:, cols(k)], ident[:, :])
                            last.then_inc(yt_done, 1)

                        def project_out(g, c):
                            q = CH * order(g) + c
                            pe.wait_ge(ytc_done, after(q + 1))
                            pe.wait_ge(y2_done, after(q + 1))
                            for k in range(KD):
                                last = nc.tensor.matmul(near[:, :], yt[:, k, :], wout[:, k, :],
                                                        start=(k == 0), stop=(k == KD - 1))
                            last.then_inc(out_done, 1)

                        def group(g, front, ahead):
                            for c in range(CH):
                                if front is not None and c == 0:
                                    transposes(front, 0, 2)
                                    chunk_decays(g, c)
                                    transposes(front, 2, 4)
                                else:
                                    chunk_decays(g, c)
                                chunk_start(g, c)
                                if c:
                                    project_out(g, c - 1)
                                if front is not None:
                                    if c == 0:
                                        project_conv(front, 0)
                                        project_dt(front)
                                    if c == 3:
                                        sum_decays(front)
                                    if c and front is not LAST:
                                        project_conv(front, c + 1)
                                if g is LAST and c == 0:
                                    project_z(g, 0)
                                chunk_y(g, c)
                                if front is not None and (c == 0 or front is LAST):
                                    project_conv(front, c + 1)
                                if g is not LAST and front is not LAST:
                                    project_z(front, c, 0, KD if c < CH - 1 else KD - 1)
                                if g is LAST and c < CH - 1:
                                    project_z(g, c + 1, 0, KD // 2)
                                elif g is LAST:
                                    transposes(BEHIND, 0, KD // 2)
                                chunk_state(g, c)
                                if g is LAST and c < CH - 1:
                                    project_z(g, c + 1, KD // 2, KD)
                                turn_y(g, c)
                            if g is LAST:
                                transposes(BEHIND, KD // 2, KD)
                            if front is not None and front is not LAST:
                                project_z(front, CH - 1, KD - 1, KD)
                            project_out(g, CH - 1)

                        pe.wait_ge(late_in, 16 * N_LATE)
                        project_conv(FIRST, 0)
                        start_counts(pe, [tr_done, conv_in, dt_in, z_in, dec_in, seg_done, bc_done, xt_done, y_done, st_done,
                                          yt_done, out_done], done_before)
                        project_dt(FIRST)
                        project_conv(FIRST, 1)
                        project_z(FIRST, 0)
                        project_conv(FIRST, 2)
                        project_z(FIRST, 1)
                        pe.wait_ge(set_done, N_SET)
                        sum_decays(FIRST)
                        project_z(FIRST, 2)
                        project_conv(FIRST, 3)
                        project_conv(FIRST, 4)
                        project_z(FIRST, 3)
                        all_groups(pe, group)

        ffn_part("f1_", True)
        ssm_part()
        ffn_part("f2_", False)


def kernel(L0_attn_u, L0_attn_W_in, L0_attn_conv_w, L0_attn_conv_b, L0_attn_W_out, L0_attn_A_log, L0_attn_D_param,
           L0_attn_dt_bias, L0_ffn_W_up, L0_ffn_W_gate, L0_ffn_W_down):
    import numpy as np
    import concourse.bacc as bacc
    from concourse.bass_utils import run_bass_kernel_spmd

    def rows(w_t, blocks):
        n = w_t.shape[1]
        return np.ascontiguousarray(w_t.reshape(blocks, P, n).transpose(1, 0, 2).reshape(P, blocks * n))

    def quarters(w):
        v = np.asarray(w).T.reshape(KD, P, 4, E // 4).transpose(1, 2, 0, 3)
        return np.ascontiguousarray(v.reshape(P, KD * E))

    arrays = dict(
        u=np.ascontiguousarray(np.asarray(L0_attn_u).reshape(B * L, D)),
        w_up=quarters(L0_ffn_W_up),
        w_gate=quarters(L0_ffn_W_gate),
        w_down=rows(np.asarray(L0_ffn_W_down).T, KE),
        w_in=rows(np.roll(np.asarray(L0_attn_W_in), H, axis=0).T, KD),
        w_out=rows(np.asarray(L0_attn_W_out).T, KD),
        conv_w=rows(np.asarray(L0_attn_conv_w).reshape(NCONV * P, TAPS), NCONV),
        conv_b=rows(np.asarray(L0_attn_conv_b).reshape(NCONV * P, 1), NCONV),
        head_par=np.ascontiguousarray(np.tile(np.concatenate(
            [np.asarray(L0_attn_A_log), np.asarray(L0_attn_D_param), np.asarray(L0_attn_dt_bias)])[None, :], (P, 1))),
    )
    nc = bacc.Bacc("TRN2", target_bir_lowering=False, num_devices=1)
    args = [nc.dram_tensor("in_" + n, a.shape, mybir.dt.from_np(a.dtype), kind="ExternalInput").ap()
            for n, a in arrays.items()]
    res = nc.dram_tensor("res", (B * L, D), F32, kind="ExternalOutput").ap()
    macaron_kernel(nc, *args, res)
    r = run_bass_kernel_spmd(nc, [{"in_" + n: a for n, a in arrays.items()}], core_ids=[0])
    return r.results[0]["res"].reshape(B, L, D)
```
